# Optimizing a Trainium2 kernel written in Bass

```python
import numpy as np
import jax
import jax.numpy as jnp

def _softmax(x, axis=-1):
    return jax.nn.softmax(x, axis=axis)

def _gelu(x):
    return jax.nn.gelu(x, approximate=True)

def _silu(x):
    return jax.nn.silu(x)

def _sigmoid(x):
    return jax.nn.sigmoid(x)

def _layernorm(x, axis=-1, eps=1e-05):
    m = jnp.mean(x, axis=axis, keepdims=True)
    v = jnp.var(x, axis=axis, keepdims=True)
    return (x - m) / jnp.sqrt(v + eps)

def _scatter_add(tgt, idx, src, axis=0):
    return tgt.at[idx].add(src)

def _segment_sum(src, seg, n):
    return jax.ops.segment_sum(src, seg, n)
kernel_name = 'mk_vit_tower_d2_tok_img1024_r4_e839d7'

def setup_inputs(seed: int=0):
    np.random.seed(seed)
    _w = jnp.asarray

    def _rec_inputs():
        import jax
        import jax.numpy as jnp
        _rk = jax.random.key(seed)
        x = -0.00016672 + 0.999947 * jax.random.normal(jax.random.fold_in(_rk, 1), (16, 3, 96, 96), jnp.float32)
        return x
    x = _rec_inputs()

    def _L0_tok_setup():
        import jax, jax.numpy as jnp
        import numpy as np
        EPS = 1e-05

        def _layernorm(x, w, b):
            mu = jnp.mean(x, axis=-1, keepdims=True)
            var = jnp.mean(jnp.square(x - mu), axis=-1, keepdims=True)
            return (x - mu) * jax.lax.rsqrt(var + EPS) * w + b
        key = jax.random.key(seed)
        ks = jax.random.split(key, 8)
        B, C, H, W = (64, 3, 96, 96)
        P, D = (16, 256)
        patch_dim = C * P * P
        num_patches = H // P * (W // P)
        x = jax.random.normal(ks[0], (B, C, H, W), dtype=jnp.float32)
        ln1_w = jnp.ones((patch_dim,), jnp.float32)
        ln1_b = jnp.zeros((patch_dim,), jnp.float32)
        lin_w = jax.random.normal(ks[1], (patch_dim, D), jnp.float32) / np.sqrt(patch_dim)
        lin_b = jnp.zeros((D,), jnp.float32)
        ln2_w = jnp.ones((D,), jnp.float32)
        ln2_b = jnp.zeros((D,), jnp.float32)
        pos_embedding = jax.random.normal(ks[2], (1, num_patches + 1, D), jnp.float32)
        cls_token = jax.random.normal(ks[3], (1, 1, D), jnp.float32)
        return dict(x=x, ln1_w=ln1_w, ln1_b=ln1_b, lin_w=lin_w, lin_b=lin_b, ln2_w=ln2_w, ln2_b=ln2_b, pos_embedding=pos_embedding, cls_token=cls_token)
    _L0_tok_all = _L0_tok_setup()
    _L0_tok_in = {k: v for k, v in _L0_tok_all.items() if k in ('ln1_w', 'ln1_b', 'lin_w', 'lin_b', 'ln2_w', 'ln2_b', 'pos_embedding', 'cls_token')}
    del _L0_tok_all

    def _L0_attn_setup():
        import jax, jax.numpy as jnp
        import numpy as np
        EMBED_DIM = 256
        NUM_HEADS = 16
        HEAD_DIM = EMBED_DIM // NUM_HEADS
        B, T = (2, 512)
        key = jax.random.key(seed)
        ks = jax.random.split(key, 7)
        s = 0.02
        return {'x': jax.random.normal(ks[0], (B, T, EMBED_DIM), dtype=jnp.float32), 'Wq': jax.random.normal(ks[1], (EMBED_DIM, EMBED_DIM), dtype=jnp.float32) * s, 'bq': jax.random.normal(ks[2], (EMBED_DIM,), dtype=jnp.float32) * s, 'Wkv': jax.random.normal(ks[3], (2 * HEAD_DIM, EMBED_DIM), dtype=jnp.float32) * s, 'bkv': jax.random.normal(ks[4], (2 * HEAD_DIM,), dtype=jnp.float32) * s, 'Wo': jax.random.normal(ks[5], (EMBED_DIM, EMBED_DIM), dtype=jnp.float32) * s, 'bo': jax.random.normal(ks[6], (EMBED_DIM,), dtype=jnp.float32) * s}
    _L0_attn_all = _L0_attn_setup()
    _L0_attn_in = {k: v for k, v in _L0_attn_all.items() if k in ('Wq', 'bq', 'Wkv', 'bkv', 'Wo', 'bo')}
    del _L0_attn_all

    def _L0_ffn_setup():
        import jax, jax.numpy as jnp
        import numpy as np
        TOP_K = 2
        N_GROUP = 4
        TOPK_GROUP = 2
        ROUTED_SCALE = 2.5

        def _gate(xf, gate_w, gate_bias):
            logits = xf.astype(jnp.float32) @ gate_w.astype(jnp.float32)
            scores = jax.nn.sigmoid(logits)
            sfc = scores + gate_bias.astype(jnp.float32)[None]
            T, E = sfc.shape
            e_g = E // N_GROUP
            group_feat = sfc.reshape(T, N_GROUP, e_g)
            group_scores = jax.lax.top_k(group_feat, 2)[0].sum(axis=-1)
            _, group_idx = jax.lax.top_k(group_scores, TOPK_GROUP)
            group_mask = jax.nn.one_hot(group_idx, N_GROUP, dtype=sfc.dtype).sum(axis=1)
            score_mask = jnp.broadcast_to(group_mask[..., None], (T, N_GROUP, e_g)).reshape(T, E)
            tmp_scores = jnp.where(score_mask > 0, sfc, 0.0)
            _, topk_idx = jax.lax.top_k(tmp_scores, TOP_K)
            topk_w = jnp.take_along_axis(sfc, topk_idx, axis=-1)
            topk_w = topk_w / (topk_w.sum(axis=-1, keepdims=True) + 1e-20)
            return (topk_idx, topk_w * ROUTED_SCALE)
        key = jax.random.key(seed)
        ks = jax.random.split(key, 9)
        B, N, H, I, E, SH_I = (2, 256, 256, 128, 8, 256)
        s = lambda k, shape, scale: jax.random.normal(k, shape, jnp.float32) * scale
        return {'x': s(ks[0], (B, N, H), 1.0), 'gate_w': s(ks[1], (H, E), 0.02), 'gate_bias': s(ks[2], (E,), 0.02), 'w_gate': s(ks[3], (E, H, I), 0.02), 'w_up': s(ks[4], (E, H, I), 0.02), 'w_down': s(ks[5], (E, I, H), 0.02), 'sw_gate': s(ks[6], (H, SH_I), 0.02), 'sw_up': s(ks[7], (H, SH_I), 0.02), 'sw_down': s(ks[8], (SH_I, H), 0.02)}
    _L0_ffn_all = _L0_ffn_setup()
    _L0_ffn_in = {k: v for k, v in _L0_ffn_all.items() if k in ('gate_w', 'gate_bias', 'w_gate', 'w_up', 'w_down', 'sw_gate', 'sw_up', 'sw_down')}
    del _L0_ffn_all

    def _L1_attn_setup():
        import jax, jax.numpy as jnp
        import numpy as np
        DIMS, HEAD = (256, 16)
        HD = DIMS // HEAD
        MAX_ITER = 3
        B, T = (4, 512)

        def _ln(x, w, eps=1e-05):
            m = jnp.mean(x, axis=-1, keepdims=True)
            v = jnp.var(x, axis=-1, keepdims=True)
            return (x - m) * jax.lax.rsqrt(v + eps) * w
        key = jax.random.key(seed)
        ks = jax.random.split(key, 10)
        n = lambda k, s: jax.random.normal(k, s, jnp.float32) * 0.02
        z = lambda s: jnp.zeros(s, jnp.float32)
        o = lambda s: jnp.ones(s, jnp.float32)
        return {'x': jax.random.normal(ks[0], (B, T, DIMS), jnp.float32), 'Wq': n(ks[1], (DIMS, DIMS)), 'bq': z((DIMS,)), 'Wk': n(ks[2], (DIMS, DIMS)), 'Wv': n(ks[3], (DIMS, DIMS)), 'bv': z((DIMS,)), 'Wo': n(ks[4], (DIMS, DIMS)), 'bo': z((DIMS,)), 'lna_w': o((DIMS,)), 'lnc_w': o((HD,)), 'lnd_w': o((HD,)), 'Wlq': n(ks[5], (HD, HD)), 'blq': z((HD,)), 'Wlk': n(ks[6], (HD, HD)), 'blk': z((HD,)), 'Wlv': n(ks[7], (HD, HD)), 'blv': z((HD,)), 'temp': jnp.float32(1.0), 'threshold': jnp.float32(0.01), 'factor': jnp.float32(0.1)}
    _L1_attn_all = _L1_attn_setup()
    _L1_attn_in = {k: v for k, v in _L1_attn_all.items() if k in ('Wq', 'bq', 'Wk', 'Wv', 'bv', 'Wo', 'bo', 'lna_w', 'lnc_w', 'lnd_w', 'Wlq', 'blq', 'Wlk', 'blk', 'Wlv', 'blv', 'temp', 'threshold', 'factor')}
    del _L1_attn_all

    def _L1_ffn_setup():
        import jax, jax.numpy as jnp
        import numpy as np
        BLOCK = 32
        W_BITS = 4
        ACT_BITS = 16

        def act_qdq(x):
            qmax = 2.0 ** (ACT_BITS - 1) - 1.0
            scale = jnp.maximum(jnp.max(jnp.abs(x)) / qmax, 1e-12)
            return jnp.clip(jnp.round(x / scale), -qmax - 1.0, qmax) * scale

        def fixed_qdq_u16(x):
            scale = 1.0 / 65536.0
            return jnp.clip(jnp.round(x / scale), 0.0, 65535.0) * scale

        def lpbq_dequant(w):
            O, I = w.shape
            qmax = 2.0 ** (W_BITS - 1) - 1.0
            wb = w.reshape(O, I // BLOCK, BLOCK)
            s = jnp.maximum(jnp.max(jnp.abs(wb), axis=-1, keepdims=True) / qmax, 1e-12)
            wq = jnp.clip(jnp.round(wb / s), -qmax - 1.0, qmax) * s
            return wq.reshape(O, I)
        key = jax.random.key(seed)
        k1, k2, k3, k4 = jax.random.split(key, 4)
        B, S, H, I = (2, 1024, 256, 768)
        x = jax.random.normal(k1, (B, S, H), jnp.float32)
        w_gate = jax.random.normal(k2, (I, H), jnp.float32) * 0.02
        w_up = jax.random.normal(k3, (I, H), jnp.float32) * 0.02
        w_down = jax.random.normal(k4, (H, I), jnp.float32) * 0.02
        return {'x': x, 'w_gate': w_gate, 'w_up': w_up, 'w_down': w_down}
    _L1_ffn_all = _L1_ffn_setup()
    _L1_ffn_in = {k: v for k, v in _L1_ffn_all.items() if k in ('w_gate', 'w_up', 'w_down')}
    del _L1_ffn_all
    return {'x': x, 'L0_tok_ln1_w': _L0_tok_in['ln1_w'], 'L0_tok_ln1_b': _L0_tok_in['ln1_b'], 'L0_tok_lin_w': _L0_tok_in['lin_w'], 'L0_tok_lin_b': _L0_tok_in['lin_b'], 'L0_tok_ln2_w': _L0_tok_in['ln2_w'], 'L0_tok_ln2_b': _L0_tok_in['ln2_b'], 'L0_tok_pos_embedding': _L0_tok_in['pos_embedding'], 'L0_tok_cls_token': _L0_tok_in['cls_token'], 'L0_attn_Wq': _L0_attn_in['Wq'], 'L0_attn_bq': _L0_attn_in['bq'], 'L0_attn_Wkv': _L0_attn_in['Wkv'], 'L0_attn_bkv': _L0_attn_in['bkv'], 'L0_attn_Wo': _L0_attn_in['Wo'], 'L0_attn_bo': _L0_attn_in['bo'], 'L0_ffn_gate_w': _L0_ffn_in['gate_w'], 'L0_ffn_gate_bias': _L0_ffn_in['gate_bias'], 'L0_ffn_w_gate': _L0_ffn_in['w_gate'], 'L0_ffn_w_up': _L0_ffn_in['w_up'], 'L0_ffn_w_down': _L0_ffn_in['w_down'], 'L0_ffn_sw_gate': _L0_ffn_in['sw_gate'], 'L0_ffn_sw_up': _L0_ffn_in['sw_up'], 'L0_ffn_sw_down': _L0_ffn_in['sw_down'], 'L1_attn_Wq': _L1_attn_in['Wq'], 'L1_attn_bq': _L1_attn_in['bq'], 'L1_attn_Wk': _L1_attn_in['Wk'], 'L1_attn_Wv': _L1_attn_in['Wv'], 'L1_attn_bv': _L1_attn_in['bv'], 'L1_attn_Wo': _L1_attn_in['Wo'], 'L1_attn_bo': _L1_attn_in['bo'], 'L1_attn_lna_w': _L1_attn_in['lna_w'], 'L1_attn_lnc_w': _L1_attn_in['lnc_w'], 'L1_attn_lnd_w': _L1_attn_in['lnd_w'], 'L1_attn_Wlq': _L1_attn_in['Wlq'], 'L1_attn_blq': _L1_attn_in['blq'], 'L1_attn_Wlk': _L1_attn_in['Wlk'], 'L1_attn_blk': _L1_attn_in['blk'], 'L1_attn_Wlv': _L1_attn_in['Wlv'], 'L1_attn_blv': _L1_attn_in['blv'], 'L1_attn_temp': _L1_attn_in['temp'], 'L1_attn_threshold': _L1_attn_in['threshold'], 'L1_attn_factor': _L1_attn_in['factor'], 'L1_ffn_w_gate': _L1_ffn_in['w_gate'], 'L1_ffn_w_up': _L1_ffn_in['w_up'], 'L1_ffn_w_down': _L1_ffn_in['w_down']}

def reference(x, L0_tok_ln1_w, L0_tok_ln1_b, L0_tok_lin_w, L0_tok_lin_b, L0_tok_ln2_w, L0_tok_ln2_b, L0_tok_pos_embedding, L0_tok_cls_token, L0_attn_Wq, L0_attn_bq, L0_attn_Wkv, L0_attn_bkv, L0_attn_Wo, L0_attn_bo, L0_ffn_gate_w, L0_ffn_gate_bias, L0_ffn_w_gate, L0_ffn_w_up, L0_ffn_w_down, L0_ffn_sw_gate, L0_ffn_sw_up, L0_ffn_sw_down, L1_attn_Wq, L1_attn_bq, L1_attn_Wk, L1_attn_Wv, L1_attn_bv, L1_attn_Wo, L1_attn_bo, L1_attn_lna_w, L1_attn_lnc_w, L1_attn_lnd_w, L1_attn_Wlq, L1_attn_blq, L1_attn_Wlk, L1_attn_blk, L1_attn_Wlv, L1_attn_blv, L1_attn_temp, L1_attn_threshold, L1_attn_factor, L1_ffn_w_gate, L1_ffn_w_up, L1_ffn_w_down):
    import jax
    import jax.numpy as jnp

    def _L0_tok_ref(x, ln1_w, ln1_b, lin_w, lin_b, ln2_w, ln2_b, pos_embedding, cls_token):
        import jax, jax.numpy as jnp
        import numpy as np
        EPS = 1e-05

        def _layernorm(x, w, b):
            mu = jnp.mean(x, axis=-1, keepdims=True)
            var = jnp.mean(jnp.square(x - mu), axis=-1, keepdims=True)
            return (x - mu) * jax.lax.rsqrt(var + EPS) * w + b
        B, C, H, W = x.shape
        P = 16
        h, w = (H // P, W // P)
        patches = x.reshape(B, C, h, P, w, P)
        patches = patches.transpose(0, 2, 4, 3, 5, 1)
        patches = patches.reshape(B, h * w, P * P * C)
        y = _layernorm(patches, ln1_w, ln1_b)
        y = jnp.einsum('bnp,pd->bnd', y, lin_w) + lin_b
        y = _layernorm(y, ln2_w, ln2_b)
        cls = jnp.broadcast_to(cls_token, (B, 1, y.shape[-1]))
        y = jnp.concatenate([cls, y], axis=1)
        n = h * w
        y = y + pos_embedding[:, :n + 1]
        return y

    def _L0_attn_ref(x, Wq, bq, Wkv, bkv, Wo, bo):
        import jax, jax.numpy as jnp
        import numpy as np
        EMBED_DIM = 256
        NUM_HEADS = 16
        HEAD_DIM = EMBED_DIM // NUM_HEADS
        B, T = (2, 512)
        bsz, tgt_len, _ = x.shape
        scaling = HEAD_DIM ** (-0.5)
        q = (jnp.einsum('bte,oe->bto', x, Wq) + bq) * scaling
        kv = jnp.einsum('bte,oe->bto', x, Wkv) + bkv
        k, v = (kv[..., :HEAD_DIM], kv[..., HEAD_DIM:])
        qr = q.reshape(bsz, NUM_HEADS * tgt_len, HEAD_DIM)
        attn_weights = jnp.einsum('brd,bsd->brs', qr, k)
        attn_probs = jax.nn.softmax(attn_weights, axis=-1)
        attn_output = jnp.einsum('brs,bsd->brd', attn_probs, v)
        attn_output = attn_output.reshape(bsz, NUM_HEADS, tgt_len, HEAD_DIM)
        attn_output = attn_output.transpose(0, 2, 1, 3).reshape(bsz, tgt_len, EMBED_DIM)
        out = jnp.einsum('bte,oe->bto', attn_output, Wo) + bo
        return out

    def _L0_ffn_ref(x, gate_w, gate_bias, w_gate, w_up, w_down, sw_gate, sw_up, sw_down):
        import jax, jax.numpy as jnp
        import numpy as np
        TOP_K = 2
        N_GROUP = 4
        TOPK_GROUP = 2
        ROUTED_SCALE = 2.5

        def _gate(xf, gate_w, gate_bias):
            logits = xf.astype(jnp.float32) @ gate_w.astype(jnp.float32)
            scores = jax.nn.sigmoid(logits)
            sfc = scores + gate_bias.astype(jnp.float32)[None]
            T, E = sfc.shape
            e_g = E // N_GROUP
            group_feat = sfc.reshape(T, N_GROUP, e_g)
            group_scores = jax.lax.top_k(group_feat, 2)[0].sum(axis=-1)
            _, group_idx = jax.lax.top_k(group_scores, TOPK_GROUP)
            group_mask = jax.nn.one_hot(group_idx, N_GROUP, dtype=sfc.dtype).sum(axis=1)
            score_mask = jnp.broadcast_to(group_mask[..., None], (T, N_GROUP, e_g)).reshape(T, E)
            tmp_scores = jnp.where(score_mask > 0, sfc, 0.0)
            _, topk_idx = jax.lax.top_k(tmp_scores, TOP_K)
            topk_w = jnp.take_along_axis(sfc, topk_idx, axis=-1)
            topk_w = topk_w / (topk_w.sum(axis=-1, keepdims=True) + 1e-20)
            return (topk_idx, topk_w * ROUTED_SCALE)
        B, N, H = x.shape
        xf = x.reshape(-1, H)
        topk_idx, topk_w = _gate(xf, gate_w, gate_bias)
        g = jax.nn.silu(jnp.einsum('th,ehi->tei', xf, w_gate))
        u = jnp.einsum('th,ehi->tei', xf, w_up)
        experts_y = jnp.einsum('tei,eih->teh', g * u, w_down)
        masked_y = jnp.take_along_axis(experts_y, topk_idx[:, :, None], axis=1)
        y = jnp.einsum('tkh,tk->th', masked_y, topk_w.astype(x.dtype)).reshape(B, N, H)
        shared = jax.nn.silu(x @ sw_gate) * (x @ sw_up) @ sw_down
        return y + shared

    def _L1_attn_ref(x, Wq, bq, Wk, Wv, bv, Wo, bo, lna_w, lnc_w, lnd_w, Wlq, blq, Wlk, blk, Wlv, blv, temp, threshold, factor):
        import jax, jax.numpy as jnp
        import numpy as np
        DIMS, HEAD = (256, 16)
        HD = DIMS // HEAD
        MAX_ITER = 3
        B, T = (4, 512)

        def _ln(x, w, eps=1e-05):
            m = jnp.mean(x, axis=-1, keepdims=True)
            v = jnp.var(x, axis=-1, keepdims=True)
            return (x - m) * jax.lax.rsqrt(v + eps) * w
        Bn, Tn, D = x.shape
        H, hd = (HEAD, HD)
        temp0 = jax.lax.stop_gradient(temp)
        thr = jax.lax.stop_gradient(threshold)
        fac = jax.lax.stop_gradient(factor)
        scale = hd ** (-0.25)
        xn = _ln(x, lna_w)
        q = (xn @ Wq.T + bq) * scale
        k = xn @ Wk.T * scale
        v = xn @ Wv.T + bv
        shp = lambda t: t.reshape(Bn, Tn, H, hd).transpose(0, 2, 1, 3)
        q, k, v = (shp(q), shp(k), shp(v))
        E = H
        sm_scale = 1.0 / float(np.sqrt(hd))
        qcur, kcur, vcur = (q, k, v)
        prev = jnp.zeros_like(q)
        attn_out = jnp.zeros_like(q)
        done = jnp.asarray(False)
        for it in range(MAX_ITER):
            ql = qcur[:, :, :E] @ Wlq.T + blq
            kl = kcur[:, :, :E] @ Wlk.T + blk
            vl = vcur[:, :, :E] @ Wlv.T + blv
            t_it = temp0 + 0.005 * it
            tscale = jnp.where((t_it != 1.0) & (t_it > 0), jax.lax.rsqrt(t_it), 1.0)
            qs = _ln(ql, lnc_w) * tscale
            ks_ = _ln(kl, lnd_w)
            logits = jnp.einsum('bhqd,bhkd->bhqk', qs, ks_) * sm_scale
            ai = jnp.einsum('bhqk,bhkd->bhqd', jax.nn.softmax(logits, axis=-1), vl)
            iter_out = jnp.zeros_like(qcur).at[:, :, :E].set(ai)
            diff = jnp.mean(jnp.abs(iter_out - prev))
            attn_out = jnp.where(done, attn_out, iter_out)
            done = done | (diff < thr + fac * diff) & (it > 0)
            prev = iter_out
            qcur = qcur + iter_out
            kcur, vcur = (kl, vl)
        out = attn_out.transpose(0, 2, 1, 3).reshape(Bn, Tn, D)
        return out @ Wo.T + bo

    def _L1_ffn_ref(x, w_gate, w_up, w_down):
        import jax, jax.numpy as jnp
        import numpy as np
        BLOCK = 32
        W_BITS = 4
        ACT_BITS = 16

        def act_qdq(x):
            qmax = 2.0 ** (ACT_BITS - 1) - 1.0
            scale = jnp.maximum(jnp.max(jnp.abs(x)) / qmax, 1e-12)
            return jnp.clip(jnp.round(x / scale), -qmax - 1.0, qmax) * scale

        def fixed_qdq_u16(x):
            scale = 1.0 / 65536.0
            return jnp.clip(jnp.round(x / scale), 0.0, 65535.0) * scale

        def lpbq_dequant(w):
            O, I = w.shape
            qmax = 2.0 ** (W_BITS - 1) - 1.0
            wb = w.reshape(O, I // BLOCK, BLOCK)
            s = jnp.maximum(jnp.max(jnp.abs(wb), axis=-1, keepdims=True) / qmax, 1e-12)
            wq = jnp.clip(jnp.round(wb / s), -qmax - 1.0, qmax) * s
            return wq.reshape(O, I)
        x = act_qdq(x)
        up = act_qdq(x @ lpbq_dequant(w_up).T)
        gate = act_qdq(x @ lpbq_dequant(w_gate).T)
        sig = fixed_qdq_u16(jax.nn.sigmoid(gate))
        gate = act_qdq(gate * sig)
        o = act_qdq(gate * up)
        return o @ lpbq_dequant(w_down).T
    h = _L0_tok_ref(x, L0_tok_ln1_w, L0_tok_ln1_b, L0_tok_lin_w, L0_tok_lin_b, L0_tok_ln2_w, L0_tok_ln2_b, L0_tok_pos_embedding, L0_tok_cls_token)
    h = h + _L0_attn_ref(_layernorm(h, axis=-1), L0_attn_Wq, L0_attn_bq, L0_attn_Wkv, L0_attn_bkv, L0_attn_Wo, L0_attn_bo)
    h = h + _L0_ffn_ref(_layernorm(h, axis=-1), L0_ffn_gate_w, L0_ffn_gate_bias, L0_ffn_w_gate, L0_ffn_w_up, L0_ffn_w_down, L0_ffn_sw_gate, L0_ffn_sw_up, L0_ffn_sw_down)
    h = h + _L1_attn_ref(_layernorm(h, axis=-1), L1_attn_Wq, L1_attn_bq, L1_attn_Wk, L1_attn_Wv, L1_attn_bv, L1_attn_Wo, L1_attn_bo, L1_attn_lna_w, L1_attn_lnc_w, L1_attn_lnd_w, L1_attn_Wlq, L1_attn_blq, L1_attn_Wlk, L1_attn_blk, L1_attn_Wlv, L1_attn_blv, L1_attn_temp, L1_attn_threshold, L1_attn_factor)
    h = h + _L1_ffn_ref(_layernorm(h, axis=-1), L1_ffn_w_gate, L1_ffn_w_up, L1_ffn_w_down)
    return h

_drawn_inputs = setup_inputs


def setup_inputs(seed=0):
    import zlib

    import numpy as np

    out = dict(_drawn_inputs(seed))
    spreads = {'L0_tok_ln1_w': (1.0, 0.2),
     'L0_tok_ln1_b': (0.0, 0.1),
     'L0_tok_lin_b': (0.0, 0.1),
     'L0_tok_ln2_w': (1.0, 0.2),
     'L0_tok_ln2_b': (0.0, 0.1),
     'L1_attn_bq': (0.0, 2.0),
     'L1_attn_bv': (0.0, 0.8),
     'L1_attn_bo': (0.0, 0.282),
     'L1_attn_lna_w': (1.0, 0.6),
     'L1_attn_lnc_w': (1.0, 0.6),
     'L1_attn_lnd_w': (1.0, 0.6),
     'L1_attn_blq': (0.0, 2.0),
     'L1_attn_blk': (0.0, 0.8),
     'L1_attn_blv': (0.0, 0.489)}
    factors = {'L0_attn_Wq': 8.0,
     'L0_attn_bq': 8.0,
     'L0_attn_Wkv': 3.72,
     'L0_attn_bkv': 8.0,
     'L0_attn_Wo': 3.235,
     'L0_attn_bo': 3.935,
     'L0_ffn_gate_w': 4.691,
     'L0_ffn_gate_bias': 8.0,
     'L0_ffn_w_gate': 3.999,
     'L0_ffn_w_up': 3.874,
     'L0_ffn_w_down': 3.923,
     'L0_ffn_sw_gate': 4.868,
     'L0_ffn_sw_up': 4.834,
     'L0_ffn_sw_down': 4.825,
     'L1_attn_Wq': 24.857,
     'L1_attn_Wk': 8.0,
     'L1_attn_Wv': 8.0,
     'L1_attn_Wo': 3.313,
     'L1_attn_Wlq': 8.0,
     'L1_attn_Wlk': 8.0,
     'L1_attn_Wlv': 8.0,
     'L1_ffn_w_gate': 6.396,
     'L1_ffn_w_up': 6.365,
     'L1_ffn_w_down': 6.301}
    for name, (base, spread) in spreads.items():
        noise = np.random.default_rng([zlib.crc32(name.encode()), seed]).standard_normal(out[name].shape)
        drawn = base * np.exp(spread * noise) if base else spread * noise
        out[name] = jnp.asarray(drawn.astype(out[name].dtype))
    for name, factor in factors.items():
        out[name] = (out[name] * factor).astype(out[name].dtype)
    return out
```

```python
from contextlib import ExitStack

import concourse.bass as bass
from concourse import mybir

F32 = mybir.dt.float32
ALU = mybir.AluOpType
ACT = mybir.ActivationFunctionType
AX = mybir.AxisListType

P = 128
B = 16
NG = 6
T = NG * NG + 1
PS = 16
NC = 3
D = 256
KD = D // P
HD = 16
NH = 8
NT = B * T
TT = 5
LAST = NT - (TT - 1) * P
NP = TT * P
CB = B // 2
CH = CB * T
QW = CH + 28
KW = NH * T
VW = HD + 1
G3 = 3 * T
NE = 8
EI = 128
NX = NE + 2
FI = 768
FC = FI // P
BLK = 32
NB = D // BLK
EPS = 1e-5
SM = HD ** -0.5
MAGIC = 1.5 * 2.0 ** 23
QA = 32767.0
QWT = 7.0
TINY = 1e-12
HP = NP // 2
TF = 2 * NH
CF = B * TF
KSCALE = HD ** -0.25
GROUP_AT = (0, 3, 5)
N_CONSTS = 1
N_COLS = 2 * NC + 4 + 4 + 3
N_ATTN_W = 6 + 1 + 6 + 1


def fills():
    f = []
    for g in range(2):
        for k in range(6):
            f.append((("xp", k, g), "act" if k % 2 else "dve"))
    for i in range(3):
        f.append((("y", i), "dve"))
    for n in ("q0", "o0", "q1", "k1", "v1", "o1"):
        f.append((("wT", n), "act"))
    f.append((("wkvT",), "act"))
    f.append((("wl",), "dve"))
    f.append((("bl",), "dve"))
    for i in range(3):
        f.append((("xT", 0, i), "act"))
    for c in range(2):
        f.append((("k0", c), "act"))
        f.append((("v0", c), "act"))
        for hf in range(KD):
            f.append((("q0", hf, c), "act"))
    for c in range(2):
        for j in range(2):
            f.append((("vb", c, j), "dve"))

    for s in range(B // 2 + 2):
        if s < B // 2:
            f.extend(((("S", s, hf), "dve") for hf in range(KD)))
        if 0 <= s - 1 < B // 2:
            f.extend(((("PT", s - 1, hf), "act") for hf in range(KD)))
        if 0 <= s - 2 < B // 2:
            f.append((("PV", s - 2), "dve"))
    for p in range(B // 2):
        f.append((("AT", p), "act"))
    for i in range(3):
        f.append((("wo", 0, i), "dve"))
    for i in range(3):
        f.append((("xT", 1, i), "act"))
    f.append((("lg",), "act"))
    for e in range(NX + 1):
        if e < NX:
            for c in range(2):
                f.append((("g", e, c), "act"))
                f.append((("u", e, c), "dve"))
        if 1 <= e <= NE or e == NX:
            for i in range(3):
                f.append((("d", min(e - 1, NE), i), "dve"))
        if 1 <= e <= 9:
            f.append((("fw", e - 1), "act"))
    for i in range(3):
        f.append((("xT", 2, i), "act"))
    halves = range(KD)
    for w in ("k", "q", "v"):
        f.extend(((w + "1", hf), "act") for hf in halves)
    f.extend((("nc", "k", 1, hf), "act") for hf in halves)
    f.extend((("kr", 1, hf), "act") for hf in halves)
    f.extend((("nv", "k", 1, hf), "act") for hf in halves)
    f.extend((("vr", 1, hf), "act") for hf in halves)
    for a in (1, 2, 3):
        f.extend((("nc", "q", a, hf), "act") for hf in halves)
        f.extend((("fvb", a, 0, j), "dve") for j in range(2))
        f.extend((("nv", "q", a, hf), "act") for hf in halves)
        f.extend((("fvb", a, 0, j), "dve") for j in range(2, 4))
        f.extend((("ST", a, hf), "act") for hf in halves)
        if a < 3:
            f.extend((("nc", "k", a + 1, hf), "act") for hf in halves)
        f.extend((("SQ", a, hf), "dve") for hf in halves)
        f.extend((("fvb", a, 1, j), "dve") for j in range(4))
        if a < 3:
            if a < 2:
                f.extend((("kr", a + 1, hf), "act") for hf in halves)
            f.extend((("nv", "k", a + 1, hf), "act") for hf in halves)
        else:
            f.append((("df",), "dve"))
        f.extend((("fPT", a, hf), "act") for hf in halves)
        if a < 3:
            f.extend((("vr", a + 1, hf), "act") for hf in halves)
        f.extend((("O", a, hf), "dve") for hf in halves)
    for i in range(3):
        f.append((("wo", 1, i), "dve"))
    f.extend(max_fills(0))
    for i in range(3):
        f.append((("xT", 3, i), "act"))
    for w in ("ga", "up"):
        for o in range(FC):
            for c in range(2):
                f.append(((w, o, c), "act"))
            if (w, o) == ("up", 1):
                f.extend(max_fills(1))
    f.extend(max_fills(2))
    f.extend(max_fills(3))
    f.extend(max_fills(4))
    for t in range(TT):
        f.append((("dn", t), "dve"))
    return f


def max_fills(n):
    return [(("mxT", n), "dve"), (("mxB", n), "dve")]


FILLS = fills()
FILL = {key: n for n, (key, _) in enumerate(FILLS)}
assert len(FILL) == len(FILLS)
NTH = {}
for _who in ("act", "dve"):
    for _n, _key in enumerate(k for k, w in FILLS if w == _who):
        NTH[_key] = (_who, _n + 1)
NORMS = {key[1:]: n for n, key in enumerate(k for k, _ in FILLS if k[0] == "nc")}


def build(nc, i, out):
    with ExitStack() as ctx:
        def sb(name, *shape):
            return ctx.enter_context(nc.sbuf_tensor(name, list(shape), F32))

        def sem(name):
            return ctx.enter_context(nc.semaphore(name))

        h_dram = nc.dram_tensor("h_scratch", (NT, D), F32).ap()
        o_dram = nc.dram_tensor("o_scratch", (B, T * D), F32).ap()

        QK = CB * KW
        QV = CB * NH * VW
        XI = NC * PS * NG * PS
        BIG = 2 * XI + 6 * NG * 96 + 6 * D
        big = sb("big", P, BIG)
        small = sb("small", P, 2 * QV + 3 * FC * D)
        kexp = [big[:, n * QK:(n + 1) * QK].rearrange("p (b h k) -> p b h k", b=CB, h=NH) for n in range(2)]
        vals = [small[:, n * QV:(n + 1) * QV].rearrange("p (b h v) -> p b h v", b=CB, h=NH) for n in range(2)]
        at = [0]

        def cut(region, n):
            at[0] += n
            return region[:, at[0] - n:at[0]]

        img = cut(big, XI)
        patches = cut(big, XI)
        patT = cut(big, 6 * NG * 96).rearrange("p (k w t) -> p k w t", k=6, w=NG)
        lin_w = cut(big, 6 * D).rearrange("p (k n) -> p k n", k=6)
        at[0] = 2 * QK
        w_eg = cut(big, KD * NE * EI).rearrange("p (k e i) -> p k e i", k=KD, e=NE)
        w_eu = cut(big, KD * NE * EI).rearrange("p (k e i) -> p k e i", k=KD, e=NE)
        w_ed = cut(big, NE * D).rearrange("p (e n) -> p e n", e=NE)
        w_sg = cut(big, KD * D).rearrange("p (k i) -> p k i", k=KD)
        w_su = cut(big, KD * D).rearrange("p (k i) -> p k i", k=KD)
        w_sd = cut(big, KD * D).rearrange("p (k n) -> p k n", k=KD)
        assert at[0] <= BIG
        at[0] = 0
        fkeys = cut(big, KD * B * P).rearrange("p (f b h k) -> p f b h k", f=KD, b=B, h=NH)
        fvals = cut(big, KD * B * P).rearrange("p (f b h k) -> p f b h k", f=KD, b=B, h=NH)
        fvalsT = cut(big, KD * B * P).rearrange("p (f b m) -> p f b m", f=KD, b=B)
        assert at[0] <= BIG
        at[0] = 0
        gate = cut(big, FC * NP)
        up = cut(big, FC * NP)
        sig = cut(big, FC * NP)
        at[0] = 0
        raw = {n: cut(small, KD * D).rearrange("p (o i) -> p o i", o=KD) for n in ("q0", "o0", "q1", "k1", "v1", "o1")}
        raw_kv = cut(small, D)
        at[0] = 2 * QV
        fraw = [cut(small, FC * D) for _ in range(3)]

        h = sb("h", P, TT, D)
        xn = sb("xn", P, TT, D)
        xT = sb("xT", P, KD, NP)
        att = sb("att", P, 2 * 3 * CH)
        attT = att[:, 0:KD * NP].rearrange("p (k t) -> p k t", k=KD)
        values3 = att[:, :].rearrange("p (n b m) -> p n b m", n=2, b=CB)
        wT = {n: sb("wT_" + n, P, KD, D) for n in raw}
        wkT = sb("wkT", P, KD, P)
        wvT = sb("wvT", P, KD, P)
        fT = [sb("fT0", P, KD, FI), sb("fT1", P, KD, FI), sb("fT2", P, FC, D)]
        qsT = sb("qsT", P, KD, 2, QW)
        cur = sb("cur", P, B // 2 * D)
        q_cur, k_cur, v_cur = (cur[:, n * KD * CF:(n + 1) * KD * CF].rearrange("p (k t) -> p k t", k=KD) for n in range(3))
        regrouped = cur[:, 0:B // 2 * D].rearrange("p (s n) -> p s n", n=D)
        hid = cur[:, 0:3 * NP].rearrange("p (n t) -> p n t", n=3)
        passes = sb("passes", P, NG * D)
        pass_out = [passes[:, n * KD * CF:(n + 1) * KD * CF].rearrange("p (k t) -> p k t", k=KD) for n in range(2)]
        pos = passes[0:96, 0:NG * D].rearrange("p (w n) -> p w n", w=NG)
        keys_n = sb("keys_n", P, 2, CH)
        NR = 4
        cen_all = sb("cen", P, NR * CF)
        cen = cen_all[:, :].rearrange("p (n t) -> p n t", n=NR)
        silu = cen_all[:, 0:2 * HP].rearrange("p (c t) -> p c t", c=2)
        sqr_all = sb("sqr", P, NR * CF)
        sqr = sqr_all[:, :].rearrange("p (n t) -> p n t", n=NR)
        r_lin, r_ln2w, r_ln2b = (sqr_all[:, n * D:(n + 1) * D] for n in range(3))
        rsd_all = sb("rsd", P, NR * CF)
        rsd = rsd_all[:, :].rearrange("p (n t) -> p n t", n=NR)
        cls = rsd_all[0:B, 0:2 * D].rearrange("p (j n) -> p j n", j=2)
        cmpa, cmpb = (rsd_all[:, n * TT * NE * NE:(n + 1) * TT * NE * NE].rearrange(
            "p (t i j) -> p t i j", t=TT, i=NE) for n in range(2))
        probs_all = sb("probs", P, 3 * KD * KW)
        probs = probs_all[:, :].rearrange("p (n k w) -> p n k w", n=3, k=KD)
        y = probs_all[0:96, 0:NG * D].rearrange("p (w n) -> p w n", w=NG)
        fscores, fprobs, fprobsT = (probs_all[:, n * KD * CF:(n + 1) * KD * CF].rearrange(
            "p (f t) -> p f t", f=KD) for n in range(3))
        probsT = sb("probsT", G3, 2, KD, 3 * P)
        queries_n = sb("queries_n", P, KD, CF)
        fmax = sb("fmax", P, KD, B)
        fsum = sb("fsum", P, KD, B)
        heads = sb("heads", P, 2, KD, NH, HD)
        head_max = sb("head_max", P, KD, NH)
        head_rec = sb("head_rec", P, KD, NH)
        ident = sb("ident", P, P)
        ones = sb("ones", P, P)
        head_of = sb("head_of", P, NH)
        key_of = sb("key_of", G3, NH)
        mean_m = sb("mean_m", P, NH, HD)
        rep_i = sb("rep_i", HD, NH, HD)
        rep_c = sb("rep_c", HD, NH, HD)
        low = sb("low", P, NE, NE)
        eps_c = sb("eps_c", P, 1)
        nhalf = sb("nhalf", P, 8)
        magic_c = sb("magic_c", P, 1)
        wl = sb("wl", HD, 3, HD)
        wl8 = sb("wl8", HD, 3, NH, HD)
        blr = sb("blr", HD, 3)
        wlT = sb("wlT", P, 4, P)
        bl = sb("bl", P, 4)
        cols = sb("cols", P, 40)
        c_ln1w, c_ln1b = cols[:, 0:6], cols[:, 6:12]
        c_bq0, c_bq1, c_bv1, c_lna = cols[:, 12:14], cols[:, 14:16], cols[:, 16:18], cols[:, 18:20]
        c_bk0, c_bv0 = cols[:, 20:21], cols[:, 21:22]
        c_lnc, c_lnd, c_temp, c_thr, c_fac = (cols[:, n:n + 1] for n in range(22, 27))
        c_hbq1 = cols[:, 28:30]
        q_w = sb("q_w", P, 3)
        k_w = sb("k_w", P, NH)
        temps = sb("temps", P, 4, 3)
        r_bo = [sb("r_bo0", P, D), sb("r_bo1", P, D)]
        r_gb = sb("r_gb", P, NE)
        gate_w = sb("gate_w", P, KD, NE)
        st = sb("st", P, 18, 6)
        mv = sb("mv", P, NG, 2)
        var = sb("var", P, 8)
        rstd = sb("rstd", P, 8)
        sc = sb("sc", P, TT, NE)
        rt = sb("rt", P, 6, TT * NE)
        route = sb("route", P, TT, NE)
        bs = sb("bs", P, 3, FC * NB)
        bi = sb("bi", P, 3, FC * NB)
        mx = sb("mx", P, 8)
        gmx = sb("gmx", 1, 8)
        part = sb("part", P, 2 * FC)
        qs = sb("qs", P, 5, 2)
        dfs = sb("dfs", P, 8)

        banks = [ctx.enter_context(nc.psum_tensor(f"bank{n}", [P, 512], F32)) for n in range(8)]

        bank_filled = sem("bank_filled")
        emptied_by = {"act": sem("act_emptied"), "dve": sem("dve_emptied")}
        dve_chain, act_chain, pool_chain = sem("dve_chain"), sem("act_chain"), sem("pool_chain")
        images_in = [sem(f"images_in{n}") for n in range(NC)]
        (patch_w_in, cols_in, attn_w_in, rows_in, pos_in, moe_in, ffn_in, h_stored, h_in, out_stored) = (
            sem(n) for n in ("patch_w_in", "cols_in", "attn_w_in", "rows_in", "pos_in", "moe_in", "ffn_in",
                             "h_stored", "h_in", "out_stored"))
        o_stored = [sem(f"o_stored{n}") for n in range(B // 2)]
        regrouped_in = [sem(f"regrouped_in{n}") for n in range(B // 2)]
        consts_ready = sem("consts_ready")
        derived_ready = sem("derived_ready")
        var_ready = sem("var_ready")
        rstd_ready = sem("rstd_ready")
        patches_ready = sem("patches_ready")
        y_ready = sem("y_ready")
        xn_ready = sem("xn_ready")
        exp_done = sem("exp_done")
        root_done = sem("root_done")
        normed = sem("normed")
        keys_spread = sem("keys_spread")
        fkeys_spread = sem("fkeys_spread")
        fvals_spread = sem("fvals_spread")
        attT_cleared = sem("attT_cleared")
        fexp_done = sem("fexp_done")
        fprobs_ready = sem("fprobs_ready")
        fw_ready = sem("fw_ready")
        mx_ready = sem("mx_ready")
        wl8_ready = sem("wl8_ready")
        gate_ready = sem("gate_ready")
        temps_ready = sem("temps_ready")
        temps_rooted = sem("temps_rooted")
        sig_done = sem("sig_done")
        o_ready = sem("o_ready")
        df_ready = sem("df_ready")
        scales_in_use = sem("scales_in_use")

        def filled(eng, key):
            eng.wait_ge(bank_filled, FILL[key] + 1)

        def emptied(eng, key):
            who, nth = NTH[key]
            eng.wait_ge(emptied_by[who], nth)

        def bank_of(key):
            return banks[FILL[key] % 8]

        def take(eng, key):
            filled(eng, key)
            return bank_of(key)

        block = ctx.enter_context(nc.Block())

        @block.sync
        def _(sp):
            im = i["x"].rearrange("b c (g r) w -> c b g (r w)", g=NG)
            imv = img.rearrange("p (c n) -> p c n", c=NC)
            for c in range(NC):
                sp.dma_start(imv[0:96, c, :], im[c]).then_inc(images_in[c], 16)
            lw = i["L0_tok_lin_w"].rearrange("(k p c) n -> c p k n", k=2, p=P)
            for c in range(NC):
                sp.dma_start(lin_w[:, 2 * c:2 * c + 2, :], lw[c]).then_inc(patch_w_in, 16)
            for col, name in ((c_ln1w, "L0_tok_ln1_w"), (c_ln1b, "L0_tok_ln1_b")):
                v = i[name].rearrange("(k p c) -> c p k", k=2, p=P)
                for c in range(NC):
                    sp.dma_start(col[:, 2 * c:2 * c + 2], v[c], allow_slow_non_contiguous=True).then_inc(cols_in, 16)
            for col, name in ((c_bq0, "L0_attn_bq"), (c_bq1, "L1_attn_bq"), (c_bv1, "L1_attn_bv"), (c_lna, "L1_attn_lna_w")):
                sp.dma_start(col, i[name].rearrange("(k p) -> p k", k=KD), allow_slow_non_contiguous=True).then_inc(cols_in, 16)
            kv = i["L0_attn_bkv"]
            for col, v in ((c_bk0, kv[0:HD]), (c_bv0, kv[HD:2 * HD]), (c_lnc, i["L1_attn_lnc_w"]), (c_lnd, i["L1_attn_lnd_w"])):
                sp.dma_start(col, v.unsqueeze(0).to_broadcast([NH, HD]).unsqueeze(2)).then_inc(cols_in, 16)
            for col, name in ((c_temp, "L1_attn_temp"), (c_thr, "L1_attn_threshold"), (c_fac, "L1_attn_factor")):
                sp.dma_start(col, i[name].partition_broadcast(P)).then_inc(cols_in, 16)
            for col, name in ((r_lin, "L0_tok_lin_b"), (r_ln2w, "L0_tok_ln2_w"), (r_ln2b, "L0_tok_ln2_b"),
                              (r_bo[0], "L0_attn_bo"), (r_bo[1], "L1_attn_bo"), (r_gb, "L0_ffn_gate_bias")):
                sp.dma_start(col[:, :], i[name].partition_broadcast(P)).then_inc(rows_in, 16)
            pe = i["L0_tok_pos_embedding"]
            band = pe[0, 1:T, :].rearrange("(g w) n -> g (w n)", g=NG)
            sp.dma_start(pos.rearrange("p w n -> p (w n)"),
                         band.unsqueeze(0).to_broadcast([B, NG, NG * D])).then_inc(pos_in, 16)
            sp.dma_start(cls[:, 0, :], i["L0_tok_cls_token"][0, 0, :].partition_broadcast(B)).then_inc(pos_in, 16)
            sp.dma_start(cls[:, 1, :], pe[0, 0, :].partition_broadcast(B)).then_inc(pos_in, 16)
            hv = h_dram.rearrange("(b t) n -> b t n", b=B)
            sp.wait_ge(y_ready, 1)
            sp.dma_start(hv[:, 0, :], cls[:, 0, :]).then_inc(h_stored, 16)
            sp.wait_ge(y_ready, 2)
            sp.dma_start(hv[:, 1:T, :].rearrange("b (g w) n -> b g (w n)", g=NG),
                         y.rearrange("p w n -> p (w n)")).then_inc(h_stored, 16)
            sp.wait_ge(h_stored, 32)
            sp.wait_ge(consts_ready, N_CONSTS)
            sp.dma_start(h[:, 0:TT - 1, :], h_dram[0:(TT - 1) * P, :].rearrange("(t p) n -> p t n", p=P)).then_inc(h_in, 16)
            sp.dma_start(h[0:LAST, TT - 1, :], h_dram[(TT - 1) * P:NT, :]).then_inc(h_in, 16)
            filled(sp, ("bl",))
            for n, name in enumerate(("w_gate", "w_up")):
                sp.dma_start(fraw[n].rearrange("p (o i) -> p o i", o=FC),
                             i["L1_ffn_" + name].rearrange("(o p) i -> p o i", p=P)).then_inc(ffn_in, 16)
            sp.dma_start(fraw[2].rearrange("p (o i) -> p o i", o=KD),
                         i["L1_ffn_w_down"].rearrange("(o p) i -> p o i", p=P)).then_inc(ffn_in, 16)
            filled(sp, ("y", 2))
            for k in range(KD):
                rows = slice(k * P, (k + 1) * P)
                sp.dma_start(w_eg[:, k, :, :], i["L0_ffn_w_gate"][:, rows, :].rearrange("e p i -> p e i")).then_inc(moe_in, 16)
                sp.dma_start(w_eu[:, k, :, :], i["L0_ffn_w_up"][:, rows, :].rearrange("e p i -> p e i")).then_inc(moe_in, 16)
            sp.dma_start(w_ed, i["L0_ffn_w_down"].rearrange("e p n -> p e n")).then_inc(moe_in, 16)
            for dst, name in ((w_sg, "sw_gate"), (w_su, "sw_up"), (w_sd, "sw_down")):
                sp.dma_start(dst, i["L0_ffn_" + name].rearrange("(k p) n -> p k n", p=P)).then_inc(moe_in, 16)
            ov = o_dram.rearrange("b (h t d) -> b t h d", t=T, d=HD)

            def regroup(p):
                sp.wait_ge(o_stored[p], 32)
                for j in range(2):
                    sp.dma_start(regrouped[64 * j:64 * j + T, p, :].rearrange("p (h d) -> p h d", d=HD),
                                 ov[2 * p + j]).then_inc(regrouped_in[p], 16)

            for p in range(B // 2):
                emptied(sp, ("PV", p))
                for j in range(2):
                    sp.dma_start(o_dram[2 * p + j].rearrange("(t n) -> t n", t=T),
                                 heads[64 * j:64 * j + T, p % 2, :, :, :].rearrange("p k h d -> p (k h d)")
                                 ).then_inc(o_stored[p], 16)
                if p:
                    regroup(p - 1)
            regroup(B // 2 - 1)
            ot = out.rearrange("b t n -> (b t) n")
            for t in range(TT):
                n = P if t < TT - 1 else LAST
                emptied(sp, ("dn", t))
                sp.dma_start(ot[t * P:t * P + n, :], h[0:n, t, :]).then_inc(out_stored, 16)
            sp.wait_ge(out_stored, 16 * TT)

        @block.gpsimd
        def _(pool):
            links = [0]

            def link(ins):
                links[0] += 1
                ins.then_inc(pool_chain, 1)
                pool.wait_ge(pool_chain, links[0])

            pool.memset(ident[:, :], 0.0)
            pool.memset(head_of[:, :], 1.0)
            pool.memset(key_of[:, :], 1.0)
            pool.memset(low[:, :, :], 1.0)
            pool.memset(ones[:, :], 1.0)
            pool.memset(eps_c[:, :], EPS)
            pool.memset(nhalf[:, :], -0.5)
            link(pool.memset(magic_c[:, :], MAGIC))
            pool.affine_select(out=ident[:, :], in_=ident[:, :], compare_op=ALU.not_equal, fill=1.0, base=0,
                               pattern=[[-1, P]], channel_multiplier=1)
            pool.affine_select(out=low[:, :, :], in_=low[:, :, :], compare_op=ALU.is_ge, fill=0.0, base=-1,
                               pattern=[[1, NE], [-1, NE]], channel_multiplier=0)
            pool.affine_select(out=head_of[:, :], in_=head_of[:, :], compare_op=ALU.is_ge, fill=0.0, base=0,
                               pattern=[[-HD, NH]], channel_multiplier=1)
            k6 = key_of[:, 0:6].rearrange("p (g j) -> p g j", g=2)
            link(pool.affine_select(out=k6, in_=k6, compare_op=ALU.is_ge, fill=0.0, base=0,
                                    pattern=[[0, 2], [-T, 3]], channel_multiplier=1))
            link(pool.affine_select(out=head_of[:, :], in_=head_of[:, :], compare_op=ALU.is_ge, fill=0.0, base=HD - 1,
                                    pattern=[[HD, NH]], channel_multiplier=-1))
            link(pool.affine_select(out=k6, in_=k6, compare_op=ALU.is_ge, fill=0.0, base=T - 1,
                                    pattern=[[0, 2], [T, 3]], channel_multiplier=-1))
            link(pool.affine_select(out=key_of[:, 6:8], in_=key_of[:, 6:8], compare_op=ALU.is_ge, fill=0.0, base=-T,
                                    pattern=[[-T, 2]], channel_multiplier=1))
            link(pool.affine_select(out=key_of[:, 6:8], in_=key_of[:, 6:8], compare_op=ALU.is_ge, fill=0.0, base=2 * T - 1,
                                    pattern=[[T, 2]], channel_multiplier=-1))
            link(pool.memset(h[64:P, TT - 1, :], 0.0))
            pool.memset(qsT[:, :, :, CH:QW], 0.0)
            pool.memset(regrouped[:, :, :], 0.0).then_inc(consts_ready, 1)

            def inverse_root(n, rows, cols):
                pool.wait_ge(var_ready, n + 1)
                pool.tensor_tensor(rstd[0:rows, 0:cols], var[0:rows, 0:cols], nhalf[0:rows, 0:cols],
                                   ALU.pow).then_inc(rstd_ready, 1)

            inverse_root(0, 96, NG)
            inverse_root(1, 96, NG)
            pool.wait_ge(temps_ready, 1)
            pool.tensor_tensor(temps[:, 0, :], temps[:, 3, :], nhalf[:, 0:3], ALU.pow).then_inc(temps_rooted, 1)
            inverse_root(2, P, TT)

            def spread(dst, src, scale, by):
                for n in range(NH):
                    ins = pool.tensor_scalar(dst[:, :, n, :], src, scale[:, n:n + 1], by, ALU.mult, ALU.mult)
                return ins

            for c in range(2):
                emptied(pool, ("k0", c))
                spread(kexp[c], keys_n[:, c, :].rearrange("p (b k) -> p b k", b=CB), head_of, SM).then_inc(keys_spread, 1)
            inverse_root(3, P, TT)
            filled(pool, ("wo", 0, 2))
            pool.memset(att[:, 0:KD * NP], 0.0).then_inc(attT_cleared, 1)
            for n in (4, 5):
                inverse_root(n, P, TT)
            pool.wait_ge(scales_in_use, 1)
            filled(pool, ("d", NE, 2))
            for a in (1, 2, 3):
                for hf in range(KD):
                    if a > 1:
                        filled(pool, ("ST", a - 1, hf))
                    pool.wait_ge(normed, NORMS["k", a, hf] + 1)
                    spread(fkeys[:, hf], keys_n[:, hf, 0:CF].rearrange("p (b k) -> p b k", b=B), k_w,
                           SM).then_inc(fkeys_spread, 1)
                for hf in range(KD):
                    if a > 1:
                        filled(pool, ("fvb", a - 1, hf, 3))
                    emptied(pool, ("vr", a, hf))
                    spread(fvals[:, hf], v_cur[:, hf, :].rearrange("p (b k) -> p b k", b=B), head_of,
                           1.0).then_inc(fvals_spread, 1)
            inverse_root(6, P, TT)

        @block.scalar
        def _(act):
            links = [0]

            def link(ins):
                links[0] += 1
                ins.then_inc(act_chain, 1)
                act.wait_ge(act_chain, links[0])

            def empty(ins):
                ins.then_inc(emptied_by["act"], 1)

            for name, arg in (("q0", "L0_attn_Wq"), ("o0", "L0_attn_Wo"), ("q1", "L1_attn_Wq"),
                              ("k1", "L1_attn_Wk"), ("v1", "L1_attn_Wv"), ("o1", "L1_attn_Wo")):
                act.dma_start(raw[name], i[arg].rearrange("(o p) i -> p o i", p=P)).then_inc(attn_w_in, 16)
            act.dma_start(raw_kv[0:2 * HD, :], i["L0_attn_Wkv"]).then_inc(attn_w_in, 16)
            for n, name in enumerate(("lq", "lk", "lv")):
                act.dma_start(wl[:, n, :], i["L1_attn_W" + name]).then_inc(attn_w_in, 16)
                act.dma_start(blr[:, n:n + 1], i["L1_attn_b" + name].unsqueeze(1), allow_slow_non_contiguous=True).then_inc(attn_w_in, 16)
            act.dma_start(gate_w[:, :, :], i["L0_ffn_gate_w"].rearrange("(k p) e -> p k e", p=P)).then_inc(attn_w_in, 16)
            act.wait_ge(cols_in, 16 * N_COLS)
            for g in range(2):
                for k in range(1, 6, 2):
                    b = take(act, ("xp", k, g))
                    empty(act.activation(patT[:, k, 3 * g:3 * g + 3, :].rearrange("p w t -> p (w t)"), b[:, 0:288],
                                         ACT.Identity, scale=c_ln1w[:, k:k + 1], bias=c_ln1b[:, k:k + 1]))

            for n in ("q0", "o0", "q1", "k1", "v1", "o1"):
                b = take(act, ("wT", n))
                empty(act.copy(wT[n].rearrange("p k o -> p (k o)"), b[:, :]))
            b = take(act, ("wkvT",))[:, 0:4 * HD].rearrange("p (k n) -> p k n", k=KD)
            for n, dst in enumerate((wkT, wvT)):
                for k in range(KD):
                    ins = act.copy(dst[:, k, :].rearrange("p (r d) -> p r d", d=HD),
                                   b[:, k, n * HD:(n + 1) * HD].unsqueeze(1).to_broadcast([P, NH, HD]))
            empty(ins)
            def turned(n, scales=None):
                for j in range(3):
                    b = take(act, ("xT", n, j))
                    tiles = 2 if j < 2 else 1
                    for k in range(KD):
                        dst = xT[:, k, 2 * j * P:(2 * j + tiles) * P].rearrange("p (t c) -> p t c", c=P)
                        src = b[:, 0:tiles * D].rearrange("p (t k c) -> p t k c", k=KD, c=P)[:, :, k, :]
                        if scales is None:
                            ins = act.copy(dst, src)
                        else:
                            ins = act.mul(dst, src, scales[:, k:k + 1])
                    empty(ins)

            def three_times(b, bias, m):
                for r in range(3):
                    ins = act.activation(values3[:, m % 2, :, r * T:(r + 1) * T],
                                         b[:, 0:CH].rearrange("p (b k) -> p b k", b=CB), ACT.Identity, bias=bias)
                empty(ins)

            turned(0)
            for c in range(2):
                b = take(act, ("k0", c))
                empty(act.activation(keys_n[:, c, :], b[:, 0:CH], ACT.Identity, bias=c_bk0))
                b = take(act, ("v0", c))
                three_times(b, c_bv0, c)
                for hf in range(KD):
                    b = take(act, ("q0", hf, c))
                    if (hf, c) == (0, 0):
                        act.wait_ge(consts_ready, N_CONSTS)
                    empty(act.activation(qsT[:, hf, c, 0:CH], b[:, 0:CH], ACT.Identity, bias=c_bq0[:, hf:hf + 1]))

            def exps(s):
                for hf in range(KD):
                    emptied(act, ("S", s, hf))
                    v = probs[:, s % 3, hf, :]
                    act.activation(v, v, ACT.Exp).then_inc(exp_done, 1)

            def probs_turned(s):
                if s >= 2:
                    filled(act, ("PV", s - 2))
                for hf in range(KD):
                    b = take(act, ("PT", s, hf))
                    empty(act.copy(probsT[:, s % 2, hf, :], b[0:G3, 0:3 * P]))

            def centred(key):
                r = NORMS[key]
                which = key[0]
                if r >= NR:
                    act.wait_ge(normed, r - NR + 1)
                b = take(act, ("nc", *key))
                bias = bl[:, 0:1] if which == "q" else bl[:, 1:2]
                act.activation(cen[:, r % NR, :], b[:, 0:CF], ACT.Identity, bias=bias)
                empty(act.activation(sqr[:, r % NR, :], b[:, 0:CF], ACT.Square, bias=bias))

            def inverse_root(key):
                r = NORMS[key]
                b = take(act, ("nv", *key))
                v = rsd[:, r % NR, :]
                ins = act.activation(v, b[:, 0:CF], ACT.Ln, bias=eps_c[:, 0:1])
                empty(ins)
                emptied(act, ("nv", *key))
                act.activation(v, v, ACT.Exp, scale=-0.5).then_inc(root_done, 1)

            for s in range(B // 2 + 1):
                if s < B // 2:
                    exps(s)
                if s:
                    probs_turned(s - 1)
            for p in range(B // 2):
                b = take(act, ("AT", p))
                empty(act.copy(attT[:, :, 2 * T * p:2 * T * (p + 1)].rearrange("p k (j t) -> p k j t", j=2),
                               b[:, 0:2 * P].rearrange("p (k j t) -> p k j t", k=KD, j=2)[:, :, :, 0:T]))
            turned(1)
            b = take(act, ("lg",))
            empty(act.activation(sc.rearrange("p t e -> p (t e)"), b[:, 0:TT * NE], ACT.Sigmoid))
            for e in range(NX + 1):
                if e < NX:
                    for c in range(2):
                        b = take(act, ("g", e, c))
                        if e:
                            emptied(act, ("u", e - 1, c))
                        empty(act.activation(silu[:, c, :], b[:, 0:HP], ACT.Silu))
                if 1 <= e <= 9:
                    w, j = (e - 1) // 3, (e - 1) % 3
                    b = take(act, ("fw", e - 1))
                    if w < 2:
                        empty(act.copy(fT[w][:, :, j * D:(j + 1) * D], b[:, :].rearrange("p (k o) -> p k o", k=KD)))
                    else:
                        empty(act.copy(fT[2][:, 2 * j:2 * j + 2, :], b[:, :].rearrange("p (c o) -> p c o", c=2)))
            turned(2, c_lna)
            act.wait_ge(scales_in_use, 1)
            halves = range(KD)
            for w, dst in (("k", k_cur), ("q", q_cur), ("v", v_cur)):
                for hf in halves:
                    b = take(act, (w + "1", hf))[:, 0:CF]
                    if w == "k":
                        empty(act.mul(dst[:, hf, :], b, KSCALE))
                    elif w == "q":
                        empty(act.activation(dst[:, hf, :], b, ACT.Identity, scale=KSCALE, bias=c_hbq1[:, hf:hf + 1]))
                    else:
                        empty(act.activation(dst[:, hf, :], b, ACT.Identity, bias=c_bv1[:, hf:hf + 1]))

            def refreshed(which, a, hf):
                dst, m = (k_cur, 2) if which == "kr" else (v_cur, 3)
                if which == "kr":
                    filled(act, ("kr", a, hf))
                elif a > 1:
                    act.wait_ge(fvals_spread, KD * (a - 2) + hf + 1)
                b = take(act, (which, a, hf))
                empty(act.activation(dst[:, hf, :], b[:, 0:CF], ACT.Identity, bias=bl[:, m:m + 1]))

            for hf in halves:
                centred(("k", 1, hf))
            for hf in halves:
                refreshed("kr", 1, hf)
            for hf in halves:
                inverse_root(("k", 1, hf))
            for hf in halves:
                refreshed("vr", 1, hf)
            for a in (1, 2, 3):
                for hf in halves:
                    centred(("q", a, hf))
                for hf in halves:
                    inverse_root(("q", a, hf))
                for hf in halves:
                    if a > 1:
                        filled(act, ("SQ", a - 1, hf))
                    b = take(act, ("ST", a, hf))
                    empty(act.copy(fscores[:, hf, :], b[:, 0:CF]))
                if a < 3:
                    for hf in halves:
                        centred(("k", a + 1, hf))
                for hf in halves:
                    emptied(act, ("SQ", a, hf))
                    act.activation(fprobs[:, hf, :], fprobs[:, hf, :], ACT.Exp).then_inc(fexp_done, 1)
                if a < 2:
                    for hf in halves:
                        refreshed("kr", a + 1, hf)
                if a < 3:
                    for hf in halves:
                        inverse_root(("k", a + 1, hf))
                for hf in halves:
                    if a > 1:
                        filled(act, ("O", a - 1, hf))
                    b = take(act, ("fPT", a, hf))
                    empty(act.copy(fprobsT[:, hf, :], b[:, 0:CF]))
                if a < 3:
                    for hf in halves:
                        refreshed("vr", a + 1, hf)
            turned(3)
            for w, dst in (("ga", gate), ("up", up)):
                for o in range(FC):
                    for c in range(2):
                        b = take(act, (w, o, c))
                        empty(act.copy(dst[:, o * NP + c * HP:o * NP + (c + 1) * HP], b[:, 0:HP]))
                    if (w, o) == ("up", 3):
                        act.wait_ge(gate_ready, 1)
                        act.activation(sig, gate, ACT.Sigmoid).then_inc(sig_done, 1)

        @block.vector
        def _(dve):
            links = [0]

            def link(ins):
                links[0] += 1
                ins.then_inc(dve_chain, 1)
                dve.wait_ge(dve_chain, links[0])

            def empty(ins):
                ins.then_inc(emptied_by["dve"], 1)

            def rows_of(t):
                return P if t < TT - 1 else LAST

            dve.wait_ge(consts_ready, N_CONSTS)
            dve.tensor_scalar(mean_m[:, :, :], head_of[:, :].unsqueeze(2).to_broadcast([P, NH, HD]), 1.0 / HD, None, ALU.mult)
            id16 = ident[0:HD, 0:HD].unsqueeze(1).to_broadcast([HD, NH, HD])
            dve.tensor_scalar(rep_i[:, :, :], id16, 0.0, None, ALU.add)
            dve.tensor_scalar(rep_c[:, :, :], id16, -1.0 / HD, None, ALU.add).then_inc(derived_ready, 1)

            pv = img[0:96, :].rearrange("p (c r w q) -> p c r w q", c=NC, r=PS, w=NG)
            for c in range(NC):
                dve.wait_ge(images_in[c], 16)
                for w in range(NG):
                    ins = dve.bn_stats(st[0:96, 3 * w + c, :], pv[:, c, :, w, :])
            link(ins)
            for w in range(NG):
                ins = dve.bn_aggr(mv[0:96, w, :], st[0:96, 3 * w:3 * w + 3, :].rearrange("p a b -> p (a b)"))
            link(ins)
            dve.tensor_scalar(var[0:96, 0:NG], mv[0:96, :, 1], EPS, None, ALU.add).then_inc(var_ready, 1)
            dve.wait_ge(rstd_ready, 1)
            po = patches[0:96, :].rearrange("p (w c r q) -> p w c r q", w=NG, c=NC, r=PS)
            for w in range(NG):
                for c in range(NC):
                    ins = dve.tensor_scalar(po[:, w, c, :, :], pv[:, c, :, w, :], mv[0:96, w, 0:1], rstd[0:96, w:w + 1],
                                            ALU.subtract, ALU.mult)
                if w % 3 == 2:
                    ins.then_inc(patches_ready, 1)
            dve.wait_ge(cols_in, 16 * N_COLS)
            for n in range(3):
                ins = dve.tensor_scalar(temps[:, 0, n:n + 1], c_temp, 0.005 * n, None, ALU.add)
            link(ins)
            dve.tensor_scalar(temps[:, 1, :], temps[:, 0, :], 0.0, None, ALU.is_gt)
            link(dve.tensor_scalar(temps[:, 2, :], temps[:, 0, :], 1.0, None, ALU.not_equal))
            dve.tensor_scalar(temps[:, 3, :], temps[:, 0, :], 1e-37, None, ALU.max).then_inc(temps_ready, 1)
            for g in range(2):
                for k in range(0, 6, 2):
                    b = take(dve, ("xp", k, g))
                    empty(dve.tensor_scalar(patT[:, k, 3 * g:3 * g + 3, :].rearrange("p w t -> p (w t)"), b[:, 0:288],
                                            c_ln1w[:, k:k + 1], c_ln1b[:, k:k + 1], ALU.mult, ALU.add))
            dve.wait_ge(pos_in, 48)
            dve.wait_ge(rows_in, 96)
            dve.tensor_tensor(cls[:, 0, :], cls[:, 0, :], cls[:, 1, :], ALU.add).then_inc(y_ready, 1)
            link(dve.tensor_tensor(pos[:, :, :], pos[:, :, :], r_ln2b[0:96, :].unsqueeze(1).to_broadcast([96, NG, D]), ALU.add))
            for j in range(3):
                b = take(dve, ("y", j))
                v = y[:, 2 * j:2 * j + 2, :]
                empty(dve.tensor_tensor(v, b[0:96, :].rearrange("p (w n) -> p w n", w=2),
                                        r_lin[0:96, :].unsqueeze(1).to_broadcast([96, 2, D]), ALU.add))
                emptied(dve, ("y", j))
                for w in (2 * j, 2 * j + 1):
                    ins = dve.bn_stats(st[0:96, w, :], y[:, w, :])
            link(ins)
            for w in range(NG):
                ins = dve.bn_aggr(mv[0:96, w, :], st[0:96, w, :])
            link(ins)
            dve.tensor_scalar(var[0:96, 0:NG], mv[0:96, :, 1], EPS, None, ALU.add).then_inc(var_ready, 1)
            dve.wait_ge(rstd_ready, 2)
            for w in range(NG):
                ins = dve.tensor_scalar(y[:, w, :], y[:, w, :], mv[0:96, w, 0:1], rstd[0:96, w:w + 1],
                                        ALU.subtract, ALU.mult)
            link(ins)
            link(dve.tensor_tensor(y[:, :, :], y[:, :, :], r_ln2w[0:96, :].unsqueeze(1).to_broadcast([96, NG, D]), ALU.mult))
            dve.tensor_tensor(y[:, :, :], y[:, :, :], pos[:, :, :], ALU.add).then_inc(y_ready, 1)
            dve.wait_ge(attn_w_in, 16 * N_ATTN_W)
            dve.tensor_copy(wl8[:, :, :, :], wl[:, :, :].unsqueeze(2).to_broadcast([HD, 3, NH, HD])).then_inc(wl8_ready, 1)
            b = take(dve, ("wl",))
            empty(dve.tensor_tensor(wlT.rearrange("p m (h d) -> p m h d", h=NH),
                                    b[:, :].rearrange("p (m h d) -> p m h d", m=4, h=NH),
                                    head_of[:, :].unsqueeze(1).unsqueeze(3).to_broadcast([P, 4, NH, HD]), ALU.mult))
            b = take(dve, ("bl",))
            empty(dve.tensor_copy(bl[:, :], b[:, 0:4]))
            dve.wait_ge(temps_rooted, 1)
            link(dve.tensor_scalar(temps[:, 0, :], temps[:, 0, :], -1.0, None, ALU.add))
            link(dve.tensor_tensor(temps[:, 1, :], temps[:, 1, :], temps[:, 2, :], ALU.mult))
            link(dve.tensor_tensor(temps[:, 0, :], temps[:, 0, :], temps[:, 1, :], ALU.mult))
            dve.tensor_scalar(q_w[:, :], temps[:, 0, :], 1.0, c_lnc, ALU.add, ALU.mult)
            dve.tensor_scalar(k_w[:, :], head_of[:, :], c_lnd, None, ALU.mult)
            dve.tensor_scalar(c_hbq1, c_bq1, KSCALE, None, ALU.mult).then_inc(scales_in_use, 1)

            def layer_norm(n, src):
                if n > 2:
                    dve.wait_ge(xn_ready, n - 2)
                for t in range(TT):
                    ins = dve.bn_stats(st[:, t, :], src[:, t, :])
                link(ins)
                for t in range(TT):
                    ins = dve.bn_aggr(mv[:, t, :], st[:, t, :])
                link(ins)
                dve.tensor_scalar(var[:, 0:TT], mv[:, 0:TT, 1], EPS, None, ALU.add).then_inc(var_ready, 1)
                dve.wait_ge(rstd_ready, n + 1)
                for t in range(TT):
                    ins = dve.tensor_scalar(xn[:, t, :], src[:, t, :], mv[:, t, 0:1], rstd[:, t:t + 1],
                                            ALU.subtract, ALU.mult)
                ins.then_inc(xn_ready, 1)

            def add_projection(n):
                dve.wait_ge(xn_ready, 1 if n == 0 else 4)
                dve.tensor_tensor(h[:, 0:TT - 1, :], h[:, 0:TT - 1, :],
                                  r_bo[n][:, :].unsqueeze(1).to_broadcast([P, TT - 1, D]), ALU.add)
                link(dve.tensor_tensor(h[0:LAST, TT - 1, :], h[0:LAST, TT - 1, :], r_bo[n][0:LAST, :], ALU.add))
                for j in range(3):
                    b = take(dve, ("wo", n, j))
                    if j < 2:
                        v = h[:, 2 * j:2 * j + 2, :]
                        empty(dve.tensor_tensor(v, b[:, :].rearrange("p (t n) -> p t n", t=2), v, ALU.add))
                    else:
                        v = h[0:LAST, TT - 1, :]
                        empty(dve.tensor_tensor(v, b[0:LAST, 0:D], v, ALU.add))
                emptied(dve, ("wo", n, 2))

            def values_by_key(c):
                dve.tensor_copy(vals[c][0:G3, :, :, HD], key_of[:, :].unsqueeze(1).to_broadcast([G3, CB, NH]))
                for j in range(2):
                    b = take(dve, ("vb", c, j))
                    empty(dve.tensor_tensor(vals[c][0:G3, 4 * j:4 * j + 4, :, 0:HD],
                                            b[0:G3, :].rearrange("p (b h d) -> p b h d", b=4, h=NH),
                                            key_of[:, :].unsqueeze(1).unsqueeze(3).to_broadcast([G3, 4, NH, HD]), ALU.mult))

            def scores(s):
                for hf in range(KD):
                    if s >= 1:
                        emptied(dve, ("S", s - 1, hf))
                    if s >= 3:
                        filled(dve, ("PT", s - 3, hf))
                    b = take(dve, ("S", s, hf))[:, 0:KW].rearrange("p (h k) -> p h k", h=NH)
                    link(dve.tensor_reduce(head_max[:, hf, :], b, AX.X, ALU.max))
                    empty(dve.tensor_tensor(probs[:, s % 3, hf, :].rearrange("p (h k) -> p h k", h=NH), b,
                                            head_max[:, hf, :].unsqueeze(2).to_broadcast([P, NH, T]), ALU.subtract))

            def weighted(s):
                if s >= 2:
                    dve.wait_ge(o_stored[s - 2], 32)
                if s:
                    emptied(dve, ("PV", s - 1))
                b = take(dve, ("PV", s))[:, 0:KD * NH * VW].rearrange("p (k h v) -> p k h v", k=KD, h=NH)
                link(dve.reciprocal(head_rec[:, :, :], b[:, :, :, HD]))
                empty(dve.tensor_tensor(heads[:, s % 2, :, :, :], b[:, :, :, 0:HD],
                                        head_rec[:, :, :].unsqueeze(3).to_broadcast([P, KD, NH, HD]), ALU.mult))

            def normalised(key, dst, scale):
                r = NORMS[key]
                dve.wait_ge(root_done, r + 1)
                dve.scalar_tensor_tensor(out=dst, in0=cen[:, r % NR, :], scalar=scale, in1=rsd[:, r % NR, :],
                                         op0=ALU.mult, op1=ALU.mult).then_inc(normed, 1)

            def normalised_keys(a, hf):
                if a > 1:
                    dve.wait_ge(fkeys_spread, KD * (a - 2) + hf + 1)
                normalised(("k", a, hf), keys_n[:, hf, 0:CF], 1.0)

            dve.wait_ge(h_in, 32)
            layer_norm(2, h)
            for c in range(2):
                values_by_key(c)
            for s in range(B // 2 + 2):
                if s < B // 2:
                    scores(s)
                if s >= 2:
                    weighted(s - 2)

            def dequantise(w):
                v = fraw[w].rearrange("p (n k) -> p n k", k=BLK)
                s_ = bs[:, w, :].unsqueeze(2).to_broadcast([P, FC * NB, BLK])
                i_ = bi[:, w, :].unsqueeze(2).to_broadcast([P, FC * NB, BLK])
                link(dve.tensor_reduce(bs[:, w, :], v, AX.X, ALU.max, apply_absolute_value=True))
                link(dve.tensor_scalar(bs[:, w, :], bs[:, w, :], 1.0 / QWT, TINY, ALU.mult, ALU.max))
                link(dve.reciprocal(bi[:, w, :], bs[:, w, :]))
                link(dve.tensor_tensor(v, v, i_, ALU.mult))
                link(dve.tensor_scalar(fraw[w], fraw[w], MAGIC, MAGIC, ALU.add, ALU.subtract))
                dve.tensor_tensor(v, v, s_, ALU.mult).then_inc(fw_ready, 1)

            dve.wait_ge(ffn_in, 48)
            dequantise(0)
            add_projection(0)

            layer_norm(3, h)
            filled(dve, ("lg",))
            emptied(dve, ("lg",))
            sfc = rt[:, 0, :].rearrange("p (t e) -> p t e", t=TT)
            grp = rt[:, 1, 0:TT * 4].rearrange("p (t g) -> p t g", t=TT)
            grk = rt[:, 2, 0:TT * 4].rearrange("p (t g) -> p t g", t=TT)
            tmp = rt[:, 3, :].rearrange("p (t e) -> p t e", t=TT)
            erk = rt[:, 4, :].rearrange("p (t e) -> p t e", t=TT)
            den = rt[:, 5, 0:TT]

            def top2(values, rank, n):
                other = values.unsqueeze(2).to_broadcast([P, TT, n, n])
                own = values.unsqueeze(3).to_broadcast([P, TT, n, n])
                ga, gb = cmpa[:, :, 0:n, 0:n], cmpb[:, :, 0:n, 0:n]
                dve.tensor_tensor(ga, other, own, ALU.is_gt)
                link(dve.tensor_tensor(gb, other, own, ALU.is_equal))
                link(dve.tensor_tensor(gb, gb, low[:, 0:n, 0:n].unsqueeze(1).to_broadcast([P, TT, n, n]), ALU.mult))
                link(dve.tensor_tensor(ga, ga, gb, ALU.add))
                link(dve.tensor_reduce(rank, ga, AX.X, ALU.add))
                link(dve.tensor_scalar(rank, rank, 2.0, None, ALU.is_lt))

            link(dve.tensor_tensor(sfc, sc[:, :, :], r_gb[:, :].unsqueeze(1).to_broadcast([P, TT, NE]), ALU.add))
            pair = sfc.rearrange("p t (g j) -> p t g j", j=2)
            link(dve.tensor_tensor(grp, pair[:, :, :, 0], pair[:, :, :, 1], ALU.add))
            top2(grp, grk, 4)
            link(dve.tensor_tensor(tmp.rearrange("p t (g j) -> p t g j", j=2), pair,
                                   grk.unsqueeze(3).to_broadcast([P, TT, 4, 2]), ALU.mult))
            top2(tmp, erk, NE)
            link(dve.tensor_tensor(route[:, :, :], erk, sfc, ALU.mult))
            link(dve.tensor_reduce(den, route[:, :, :], AX.X, ALU.add))
            link(dve.tensor_scalar(den, den, 1e-20, None, ALU.add))
            link(dve.reciprocal(den, den))
            link(dve.tensor_tensor(route[:, :, :], route[:, :, :], den.unsqueeze(2).to_broadcast([P, TT, NE]), ALU.mult))
            link(dve.tensor_scalar(route[:, :, :], route[:, :, :], 2.5, None, ALU.mult))

            def hidden(e):
                for c in range(2):
                    emptied(dve, ("g", e, c))
                    if e >= 3:
                        filled(dve, ("d", e - 3, 2))
                    b = take(dve, ("u", e, c))
                    empty(dve.tensor_tensor(hid[:, e % 3, c * HP:(c + 1) * HP], silu[:, c, :], b[:, 0:HP], ALU.mult))

            def add_expert(e):
                for j in range(3):
                    if e:
                        emptied(dve, ("d", e - 1, j))
                    b = take(dve, ("d", e, j))
                    for t in range(2 * j, min(2 * j + 2, TT)):
                        n = rows_of(t)
                        v = h[0:n, t, :]
                        src = b[0:n, (t % 2) * D:(t % 2 + 1) * D]
                        if e < NE:
                            ins = dve.scalar_tensor_tensor(out=v, in0=src, scalar=route[0:n, t, e:e + 1], in1=v,
                                                           op0=ALU.mult, op1=ALU.add)
                        else:
                            ins = dve.tensor_tensor(v, src, v, ALU.add)
                    empty(ins)

            for e in range(NX + 1):
                if e < NX:
                    hidden(e)
                if 1 <= e <= NE or e == NX:
                    add_expert(min(e - 1, NE))
                if e in (1, 4):
                    dequantise(1 if e == 1 else 2)
            emptied(dve, ("d", NE, 2))

            layer_norm(4, h)
            layer_norm(5, xn)
            def convergence():
                b = take(dve, ("df",))
                empty(dve.tensor_scalar(dfs[:, 1:2], b[:, 0:1], 1.0 / (NT * D), None, ALU.mult))
                emptied(dve, ("df",))
                link(dve.tensor_scalar(dfs[:, 2:3], dfs[:, 1:2], c_fac, c_thr, ALU.mult, ALU.add))
                link(dve.tensor_tensor(dfs[:, 3:4], dfs[:, 1:2], dfs[:, 2:3], ALU.is_lt))
                dve.tensor_scalar(dfs[:, 4:5], dfs[:, 3:4], -1.0, 1.0, ALU.mult, ALU.add)
                link(dve.tensor_scalar(pass_out[1][:, :, :], pass_out[1][:, :, :], dfs[:, 3:4], None, ALU.mult))

            def turned_values(a, hf, js):
                for j in js:
                    if a > 1:
                        filled(dve, ("O", a - 1, hf))
                    b = take(dve, ("fvb", a, hf, j))
                    empty(dve.tensor_copy(fvalsT[:, hf, 4 * j:4 * j + 4, :].rearrange("p b m -> p (b m)"), b[:, :]))

            halves = range(KD)
            for hf in halves:
                normalised_keys(1, hf)
            for a in (1, 2, 3):
                turned_values(a, 0, (0, 1))
                for hf in halves:
                    if a > 1:
                        filled(dve, ("ST", a - 1, hf))
                    normalised(("q", a, hf), queries_n[:, hf, :], q_w[:, a - 1:a])
                turned_values(a, 0, (2, 3))
                for hf in halves:
                    if a > 1:
                        filled(dve, ("fPT", a - 1, hf))
                    b = take(dve, ("SQ", a, hf))[:, 0:CF].rearrange("p (n k) -> p n k", k=TF)
                    link(dve.tensor_reduce(fmax[:, hf, :], b, AX.X, ALU.max))
                    empty(dve.tensor_tensor(fprobs[:, hf, :].rearrange("p (n k) -> p n k", k=TF), b,
                                            fmax[:, hf, :].unsqueeze(2).to_broadcast([P, B, TF]), ALU.subtract))
                if a == 3:
                    d = pass_out[0]
                    link(dve.tensor_tensor(d[:, :, :], pass_out[1][:, :, :], d[:, :, :], ALU.subtract))
                    dve.tensor_reduce(dfs[:, 0:1], d[:, :, :], AX.XY, ALU.add, apply_absolute_value=True).then_inc(df_ready, 1)
                for hf in halves:
                    dve.wait_ge(fexp_done, KD * (a - 1) + hf + 1)
                    v = fprobs[:, hf, :].rearrange("p (n k) -> p n k", k=TF)
                    link(dve.tensor_reduce(fsum[:, hf, :], v, AX.X, ALU.add))
                    link(dve.reciprocal(fsum[:, hf, :], fsum[:, hf, :]))
                    dve.tensor_tensor(v, v, fsum[:, hf, :].unsqueeze(2).to_broadcast([P, B, TF]),
                                      ALU.mult).then_inc(fprobs_ready, 1)
                turned_values(a, 1, range(4))
                if a < 3:
                    for hf in halves:
                        normalised_keys(a + 1, hf)
                else:
                    convergence()
                for hf in halves:
                    b = take(dve, ("O", a, hf))[:, 0:CF]
                    if a < 3:
                        dve.tensor_copy(pass_out[a - 1][:, hf, :], b)
                        empty(dve.tensor_tensor(q_cur[:, hf, :], b, q_cur[:, hf, :], ALU.add))
                    else:
                        dve.wait_ge(attT_cleared, 1)
                        empty(dve.scalar_tensor_tensor(
                            out=attT[:, hf, 0:NT].rearrange("p (b t) -> p b t", t=T)[:, :, 0:TF],
                            in0=b.rearrange("p (b t) -> p b t", t=TF), scalar=dfs[:, 4:5],
                            in1=pass_out[1][:, hf, :].rearrange("p (b t) -> p b t", t=TF), op0=ALU.mult, op1=ALU.add))
            add_projection(1)

            layer_norm(6, h)
            dve.wait_ge(xn_ready, 5)

            def scale_from(n):
                b = take(dve, ("mxT", n))
                empty(dve.tensor_reduce(gmx[0:1, n:n + 1], b[0:1, 0:P], AX.X, ALU.max))
                b = take(dve, ("mxB", n))
                empty(dve.tensor_scalar(qs[:, n, 0:1], b[:, 0:1], 1.0 / QA, TINY, ALU.mult, ALU.max))
                emptied(dve, ("mxB", n))
                link(dve.reciprocal(qs[:, n, 1:2], qs[:, n, 0:1]))

            def quantise(v, n):
                link(dve.tensor_scalar(v, v, qs[:, n, 1:2], MAGIC, ALU.mult, ALU.add))
                return dve.tensor_scalar(v, v, MAGIC, qs[:, n, 0:1], ALU.subtract, ALU.mult)

            xf = xn.rearrange("p t n -> p (t n)")
            dve.tensor_reduce(mx[:, 0:1], xf, AX.X, ALU.max, apply_absolute_value=True).then_inc(mx_ready, 1)
            scale_from(0)
            quantise(xf, 0).then_inc(xn_ready, 1)

            def bank_maxima(w, buf, o):
                for c in range(2):
                    emptied(dve, (w, o, c))
                    n = 2 * o + c
                    ins = dve.tensor_reduce(part[:, n:n + 1], buf[:, o * NP + c * HP:o * NP + (c + 1) * HP], AX.X,
                                            ALU.max, apply_absolute_value=True)
                return ins

            for o in range(FC):
                ins = bank_maxima("ga", gate, o)
            link(ins)
            dve.tensor_reduce(mx[:, 1:2], part[:, :], AX.X, ALU.max).then_inc(mx_ready, 1)
            scale_from(1)
            quantise(gate, 1).then_inc(gate_ready, 1)
            dve.wait_ge(mx_ready, 2)
            for o in range(FC):
                ins = bank_maxima("up", up, o)
            link(ins)
            dve.tensor_reduce(mx[:, 2:3], part[:, :], AX.X, ALU.max).then_inc(mx_ready, 1)
            scale_from(2)
            link(quantise(up, 2))
            dve.wait_ge(sig_done, 1)
            link(dve.tensor_scalar(sig, sig, 65536.0, MAGIC, ALU.mult, ALU.add))
            link(dve.tensor_scalar(sig, sig, MAGIC, 65535.0, ALU.subtract, ALU.min))
            link(dve.scalar_tensor_tensor(out=gate, in0=sig, scalar=2.0 ** -16, in1=gate, op0=ALU.mult, op1=ALU.mult))
            dve.tensor_reduce(mx[:, 3:4], gate, AX.X, ALU.max, apply_absolute_value=True).then_inc(mx_ready, 1)
            scale_from(3)
            link(quantise(gate, 3))
            link(dve.tensor_tensor(gate, gate, up, ALU.mult))
            dve.tensor_reduce(mx[:, 4:5], gate, AX.X, ALU.max, apply_absolute_value=True).then_inc(mx_ready, 1)
            scale_from(4)
            quantise(gate, 4).then_inc(o_ready, 1)
            for t in range(TT):
                n = rows_of(t)
                b = take(dve, ("dn", t))
                empty(dve.tensor_tensor(h[0:n, t, :], b[0:n, 0:D], h[0:n, t, :], ALU.add))

        @block.tensor
        def _(pe):
            at_fill = [0]

            def fill(key):
                n = FILL[key]
                assert n == at_fill[0], key
                at_fill[0] += 1
                if n >= 8:
                    emptied(pe, FILLS[n - 8][0])
                return banks[n % 8]

            def full(ins):
                ins.then_inc(bank_filled, 1)

            def product(out_, pairs):
                for n, (a_, b_) in enumerate(pairs):
                    ins = pe.matmul(out_, a_, b_, start=(n == 0), stop=(n == len(pairs) - 1))
                return ins

            pe.wait_ge(consts_ready, N_CONSTS)
            pe.wait_ge(derived_ready, 1)
            pp = patches[0:96, :].rearrange("p (w k n) -> p w k n", w=NG, k=6)
            for g in range(2):
                pe.wait_ge(patches_ready, g + 1)
                for k in range(6):
                    b = fill(("xp", k, g))
                    for w in range(3):
                        ins = pe.transpose(b[:, 96 * w:96 * w + 96], pp[:, 3 * g + w, k, :], ident[0:96, 0:96])
                    full(ins)
            pe.wait_ge(patch_w_in, 16 * NC)
            for j in range(3):
                b = fill(("y", j))
                for w in (2 * j, 2 * j + 1):
                    for k in range(6):
                        emptied(pe, ("xp", k, w // 3))
                    ins = product(b[0:96, (w % 2) * D:(w % 2 + 1) * D], [(patT[:, k, w, :], lin_w[:, k, :]) for k in range(6)])
                full(ins)
            pe.wait_ge(attn_w_in, 16 * N_ATTN_W)
            for n in ("q0", "o0", "q1", "k1", "v1", "o1"):
                b = fill(("wT", n))
                for k in range(KD):
                    for o in range(KD):
                        ins = pe.transpose(b[:, k * D + o * P:k * D + (o + 1) * P], raw[n][:, o, k * P:(k + 1) * P], ident[:, :])
                full(ins)
            b = fill(("wkvT",))
            for k in range(KD):
                ins = pe.transpose(b[:, 2 * HD * k:2 * HD * (k + 1)], raw_kv[0:2 * HD, k * P:(k + 1) * P], ident[0:2 * HD, 0:2 * HD])
            full(ins)
            ci = rep_i.rearrange("p h d -> p (h d)")
            cc_ = rep_c.rearrange("p h d -> p (h d)")
            mats = ((0, cc_), (1, cc_), (1, ci), (2, ci))
            pe.wait_ge(wl8_ready, 1)
            b = fill(("wl",))
            for m, (n, c_) in enumerate(mats):
                ins = product(b[:, m * P:(m + 1) * P], [(wl8[:, n, :, :].rearrange("p h d -> p (h d)"), c_)])
            full(ins)
            b = fill(("bl",))
            for m, (n, c_) in enumerate(mats):
                ins = product(b[:, m:m + 1], [(c_, blr[:, n:n + 1])])
            full(ins)

            def turn(n, ready):
                pe.wait_ge(xn_ready, ready)
                for j in range(3):
                    b = fill(("xT", n, j))
                    for t in range(2 * j, min(2 * j + 2, TT)):
                        for k in range(KD):
                            at_ = (t % 2) * D + k * P
                            ins = pe.transpose(b[:, at_:at_ + P], xn[:, t, k * P:(k + 1) * P], ident[:, :])
                    full(ins)

            def columns(key, w, cols_):
                b = fill(key)
                n = cols_.stop - cols_.start
                full(product(b[:, 0:n], [(w(k), xT[:, k, cols_]) for k in range(KD)]))

            def half_cols(c):
                return slice(c * CH, (c + 1) * CH)

            def values_turned(c):
                emptied(pe, ("v0", c))
                for j in range(2):
                    b = fill(("vb", c, j))
                    for n in range(4):
                        ins = pe.transpose(b[0:G3, n * P:(n + 1) * P],
                                           values3[:, c, 4 * j + n, :], ident[:, :])
                    full(ins)

            turn(0, 1)
            emptied(pe, ("wkvT",))
            emptied(pe, ("xT", 0, 2))
            for c in range(2):
                columns(("k0", c), lambda k: wkT[:, k, :], half_cols(c))
                columns(("v0", c), lambda k: wvT[:, k, :], half_cols(c))
                for hf in range(KD):
                    columns(("q0", hf, c), lambda k: wT["q0"][:, k, hf * P:(hf + 1) * P], half_cols(c))
            for c in range(2):
                values_turned(c)

            def attention():
                for s in range(B // 2 + 2):
                    if s < B // 2:
                        c = s // (CB // 2)
                        for hf in range(KD):
                            pe.wait_ge(keys_spread, c + 1)
                            emptied(pe, ("q0", hf, c))
                            b = fill(("S", s, hf))
                            for j in range(2):
                                im_ = 2 * s + j - c * CB
                                ins = product(b[64 * j:64 * j + 64, 0:KW],
                                              [(qsT[:, hf, c, im_ * T:im_ * T + 64],
                                                kexp[c][:, im_, :, :].rearrange("p h k -> p (h k)"))])
                            full(ins)
                    if 0 <= s - 1 < B // 2:
                        for hf in range(KD):
                            pe.wait_ge(exp_done, KD * (s - 1) + hf + 1)
                            b = fill(("PT", s - 1, hf))
                            for g, at_ in enumerate(GROUP_AT):
                                ins = pe.transpose(b[0:G3, g * P:(g + 1) * P],
                                                   probs[:, (s - 1) % 3, hf, at_ * T:at_ * T + G3], ident[:, :])
                            full(ins)
                    if 0 <= s - 2 < B // 2:
                        q = s - 2
                        c = q // (CB // 2)
                        b = fill(("PV", q))
                        for hf in range(KD):
                            emptied(pe, ("PT", q, hf))
                            emptied(pe, ("vb", c, 1))
                            for j in range(2):
                                im_ = 2 * q + j - c * CB
                                for g, (h0, h1) in enumerate(((0, 3), (3, 6), (6, 8))):
                                    lo = (hf * NH + h0) * VW
                                    ins = product(b[64 * j:64 * j + 64, lo:lo + (h1 - h0) * VW],
                                                  [(probsT[:, q % 2, hf, g * P + 64 * j:g * P + 64 * j + 64],
                                                    vals[c][0:G3, im_, h0:h1, :].rearrange("p h v -> p (h v)"))])
                        full(ins)

            def project(n, w):
                for j in range(3):
                    b = fill(("wo", n, j))
                    for t in range(2 * j, min(2 * j + 2, TT)):
                        rows = P if t < TT - 1 else LAST
                        ins = product(b[0:rows, (t % 2) * D:(t % 2 + 1) * D],
                                      [(attT[:, k, t * P:t * P + rows], w[:, k, :]) for k in range(KD)])
                    full(ins)

            attention()
            for p in range(B // 2):
                pe.wait_ge(regrouped_in[p], 32)
                b = fill(("AT", p))
                for k in range(KD):
                    ins = pe.transpose(b[:, k * P:(k + 1) * P], regrouped[:, p, k * P:(k + 1) * P], ident[:, :])
                full(ins)
            emptied(pe, ("AT", B // 2 - 1))
            project(0, wT["o0"])
            turn(1, 2)
            emptied(pe, ("xT", 1, 2))
            b = fill(("lg",))
            for t in range(TT):
                ins = product(b[:, t * NE:(t + 1) * NE], [(xT[:, k, t * P:(t + 1) * P], gate_w[:, k, :]) for k in range(KD)])
            full(ins)
            pe.wait_ge(moe_in, 16 * 8)

            def down(e):
                parts = [(e % 3, w_ed[:, e, :])] if e < NE else [(e % 3, w_sd[:, 0, :]), ((e + 1) % 3, w_sd[:, 1, :])]
                emptied(pe, ("u", e if e < NE else e + 1, 1))
                for j in range(3):
                    b = fill(("d", e, j))
                    for t in range(2 * j, min(2 * j + 2, TT)):
                        ins = product(b[:, (t % 2) * D:(t % 2 + 1) * D], [(hid[:, s_, t * P:(t + 1) * P], w) for s_, w in parts])
                    full(ins)

            for e in range(NX + 1):
                if e < NX:
                    for c in range(2):
                        cols_ = slice(c * HP, (c + 1) * HP)
                        if e < NE:
                            columns(("g", e, c), lambda k: w_eg[:, k, e, :], cols_)
                            columns(("u", e, c), lambda k: w_eu[:, k, e, :], cols_)
                        else:
                            part_ = slice((e - NE) * P, (e - NE + 1) * P)
                            columns(("g", e, c), lambda k: w_sg[:, k, part_], cols_)
                            columns(("u", e, c), lambda k: w_su[:, k, part_], cols_)
                if 1 <= e <= NE or e == NX:
                    down(min(e - 1, NE))
                if 1 <= e <= 9:
                    w, j = (e - 1) // 3, (e - 1) % 3
                    pe.wait_ge(fw_ready, w + 1)
                    b = fill(("fw", e - 1))
                    for x in range(2):
                        for o in range(2):
                            if w < 2:
                                src = fraw[w][:, (2 * j + o) * D + x * P:(2 * j + o) * D + (x + 1) * P]
                            else:
                                src = fraw[w][:, o * FI + (2 * j + x) * P:o * FI + (2 * j + x + 1) * P]
                            ins = pe.transpose(b[:, x * D + o * P:x * D + (o + 1) * P], src, ident[:, :])
                    full(ins)
            turn(2, 4)
            emptied(pe, ("xT", 2, 2))
            halves = range(KD)
            xf = xT[:, :, 0:NT].rearrange("p k (b t) -> p k b t", t=T)
            for w in ("k", "q", "v"):
                for hf in halves:
                    b = fill((w + "1", hf))
                    full(product(b[:, 0:CF].rearrange("p (b t) -> p b t", t=TF),
                                 [(wT[w + "1"][:, k, hf * P:(hf + 1) * P], xf[:, k, :, 0:TF]) for k in range(KD)]))

            def head_product(key, m, src):
                b = fill(key)
                full(product(b[:, 0:CF], [(wlT[:, m, :], src[:, key[-1], :])]))

            def variance(key):
                emptied(pe, ("nc", *key))
                b = fill(("nv", *key))
                full(product(b[:, 0:CF], [(mean_m.rearrange("p h d -> p (h d)"), sqr[:, NORMS[key] % NR, :])]))

            def values_by_key(a, hf, js):
                pe.wait_ge(fvals_spread, KD * (a - 1) + hf + 1)
                for j in js:
                    b = fill(("fvb", a, hf, j))
                    for n in range(4):
                        ins = pe.transpose(b[:, n * P:(n + 1) * P], fvals[:, hf, 4 * j + n, :, :].rearrange("p h k -> p (h k)"),
                                           ident[:, :])
                    full(ins)

            for hf in halves:
                emptied(pe, ("k1", hf))
                head_product(("nc", "k", 1, hf), 1, k_cur)
            for hf in halves:
                head_product(("kr", 1, hf), 2, k_cur)
            for hf in halves:
                variance(("k", 1, hf))
            for hf in halves:
                emptied(pe, ("v1", hf))
                head_product(("vr", 1, hf), 3, v_cur)
            for a in (1, 2, 3):
                for hf in halves:
                    emptied(pe, ("q1", hf) if a == 1 else ("O", a - 1, hf))
                    head_product(("nc", "q", a, hf), 0, q_cur)
                values_by_key(a, 0, (0, 1))
                for hf in halves:
                    variance(("q", a, hf))
                values_by_key(a, 0, (2, 3))
                for hf in halves:
                    pe.wait_ge(fkeys_spread, KD * (a - 1) + hf + 1)
                    pe.wait_ge(normed, NORMS["q", a, hf] + 1)
                    b = fill(("ST", a, hf))
                    for n in range(B):
                        ins = product(b[:, n * TF:(n + 1) * TF], [(fkeys[:, hf, n, :, :].rearrange("p h k -> p (h k)"),
                                                                   queries_n[:, hf, n * TF:(n + 1) * TF])])
                    full(ins)
                if a < 3:
                    for hf in halves:
                        emptied(pe, ("kr", a, hf))
                        head_product(("nc", "k", a + 1, hf), 1, k_cur)
                for hf in halves:
                    emptied(pe, ("ST", a, hf))
                    b = fill(("SQ", a, hf))
                    for g in range(2):
                        ins = pe.transpose(b[:, g * P:(g + 1) * P], fscores[:, hf, g * P:(g + 1) * P], ident[:, :])
                    full(ins)
                values_by_key(a, 1, range(4))
                if a < 3:
                    if a < 2:
                        for hf in halves:
                            head_product(("kr", a + 1, hf), 2, k_cur)
                    for hf in halves:
                        variance(("k", a + 1, hf))
                else:
                    pe.wait_ge(df_ready, 1)
                    b = fill(("df",))
                    full(product(b[:, 0:1], [(ones[:, :], dfs[:, 0:1])]))
                for hf in halves:
                    pe.wait_ge(fprobs_ready, KD * (a - 1) + hf + 1)
                    b = fill(("fPT", a, hf))
                    for g in range(2):
                        ins = pe.transpose(b[:, g * P:(g + 1) * P], fprobs[:, hf, g * P:(g + 1) * P], ident[:, :])
                    full(ins)
                if a < 3:
                    for hf in halves:
                        emptied(pe, ("vr", a, hf))
                        head_product(("vr", a + 1, hf), 3, v_cur)
                for hf in halves:
                    emptied(pe, ("fPT", a, hf))
                    emptied(pe, ("fvb", a, hf, 3))
                    b = fill(("O", a, hf))
                    for n in range(B):
                        ins = product(b[:, n * TF:(n + 1) * TF], [(fvalsT[:, hf, n, :], fprobsT[:, hf, n * TF:(n + 1) * TF])])
                    full(ins)
            emptied(pe, ("O", 3, KD - 1))
            project(1, wT["o1"])

            def maximum(n):
                pe.wait_ge(mx_ready, n + 1)
                b = fill(("mxT", n))
                full(pe.transpose(b[0:1, 0:P], mx[:, n:n + 1], ident[:, :]))
                b = fill(("mxB", n))
                emptied(pe, ("mxT", n))
                full(product(b[:, 0:1], [(ones[0:1, :], gmx[0:1, n:n + 1])]))

            maximum(0)
            turn(3, 6)
            emptied(pe, ("xT", 3, 2))
            for n, w in enumerate(("ga", "up")):
                for o in range(FC):
                    for c in range(2):
                        columns((w, o, c), lambda k: fT[n][:, k, o * P:(o + 1) * P], slice(c * HP, (c + 1) * HP))
                    if (w, o) == ("up", 1):
                        maximum(1)
            for n in (2, 3, 4):
                maximum(n)
            pe.wait_ge(o_ready, 1)
            for t in range(TT):
                rows = P if t < TT - 1 else LAST
                b = fill(("dn", t))
                full(product(b[0:rows, 0:D], [(gate[:, o * NP + t * P:o * NP + t * P + rows], fT[2][:, o, :]) for o in range(FC)]))


_INS = ["x", "L0_tok_ln1_w", "L0_tok_ln1_b", "L0_tok_lin_w", "L0_tok_lin_b", "L0_tok_ln2_w", "L0_tok_ln2_b",
        "L0_tok_pos_embedding", "L0_tok_cls_token", "L0_attn_Wq", "L0_attn_bq", "L0_attn_Wkv", "L0_attn_bkv",
        "L0_attn_Wo", "L0_attn_bo", "L0_ffn_gate_w", "L0_ffn_gate_bias", "L0_ffn_w_gate", "L0_ffn_w_up",
        "L0_ffn_w_down", "L0_ffn_sw_gate", "L0_ffn_sw_up", "L0_ffn_sw_down", "L1_attn_Wq", "L1_attn_bq",
        "L1_attn_Wk", "L1_attn_Wv", "L1_attn_bv", "L1_attn_Wo", "L1_attn_bo", "L1_attn_lna_w", "L1_attn_lnc_w",
        "L1_attn_lnd_w", "L1_attn_Wlq", "L1_attn_blq", "L1_attn_Wlk", "L1_attn_blk", "L1_attn_Wlv", "L1_attn_blv",
        "L1_attn_temp", "L1_attn_threshold", "L1_attn_factor", "L1_ffn_w_gate", "L1_ffn_w_up", "L1_ffn_w_down"]


def kernel(**inputs):
    import numpy as _np
    import concourse.bacc as _bacc
    from concourse import mybir as _mybir
    from concourse.bass_utils import run_bass_kernel_spmd as _run

    nc = _bacc.Bacc("TRN2", target_bir_lowering=False, num_devices=1)
    arrays, args = {}, {}
    for name in _INS:
        a = _np.ascontiguousarray(inputs[name])
        if a.ndim == 0:
            a = a.reshape(1)
        arrays[f"in_{name}"] = a
        args[name] = nc.dram_tensor(f"in_{name}", a.shape, _mybir.dt.from_np(a.dtype), kind="ExternalInput").ap()
    out = nc.dram_tensor("out_tokens", (B, T, D), F32, kind="ExternalOutput").ap()
    build(nc, args, out)
    r = _run(nc, [arrays], core_ids=[0])
    return r.results[0]["out_tokens"]
```

```python
from contextlib import ExitStack

import concourse.bass as bass
from concourse import mybir

F32 = mybir.dt.float32
ALU = mybir.AluOpType
ACT = mybir.ActivationFunctionType
AX = mybir.AxisListType

P = 128
B = 16
NG = 6
T = NG * NG + 1
PS = 16
NC = 3
D = 256
KD = D // P
HD = 16
NH = 8
NT = B * T
TT = 5
LAST = NT - (TT - 1) * P
NP = TT * P
CB = B // 2
CH = CB * T
QW = CH + 28
KW = NH * T
VW = HD + 1
G3 = 3 * T
NE = 8
EI = 128
NX = NE + 2
FI = 768
FC = FI // P
BLK = 32
NB = D // BLK
EPS = 1e-5
SM = HD ** -0.5
MAGIC = 1.5 * 2.0 ** 23
QA = 32767.0
QWT = 7.0
TINY = 1e-12
HP = NP // 2
TF = 2 * NH
CF = B * TF
KSCALE = HD ** -0.25
GROUP_AT = (0, 3, 5)
N_CONSTS = 1
N_COLS = 2 * NC + 4 + 4 + 3
N_ATTN_W = 6 + 1 + 6 + 1


def fills():
    f = []
    for g in range(2):
        for k in range(6):
            f.append((("xp", k, g), "act" if k % 2 else "dve"))
    for i in range(3):
        f.append((("y", i), "dve"))
    for n in ("q0", "o0", "q1", "k1", "v1", "o1"):
        f.append((("wT", n), "act"))
    f.append((("wkvT",), "act"))
    f.append((("wl",), "dve"))
    f.append((("bl",), "dve"))
    for i in range(3):
        f.append((("xT", 0, i), "act"))
    for c in range(2):
        f.append((("k0", c), "act"))
        f.append((("v0", c), "act"))
        for hf in range(KD):
            f.append((("q0", hf, c), "act"))
    for c in range(2):
        for j in range(2):
            f.append((("vb", c, j), "dve"))

    for s in range(B // 2 + 2):
        if s < B // 2:
            f.extend(((("S", s, hf), "dve") for hf in range(KD)))
        if 0 <= s - 1 < B // 2:
            f.extend(((("PT", s - 1, hf), "act") for hf in range(KD)))
        if 0 <= s - 2 < B // 2:
            f.append((("PV", s - 2), "dve"))
    for p in range(B // 2):
        f.append((("AT", p), "act"))
    for i in range(3):
        f.append((("wo", 0, i), "dve"))
    for i in range(3):
        f.append((("xT", 1, i), "act"))
    f.append((("lg",), "act"))
    for e in range(NX + 1):
        if e < NX:
            for c in range(2):
                f.append((("g", e, c), "act"))
                f.append((("u", e, c), "dve"))
        if 1 <= e <= NE or e == NX:
            for i in range(3):
                f.append((("d", min(e - 1, NE), i), "dve"))
        if 1 <= e <= 9:
            f.append((("fw", e - 1), "act"))
    for i in range(3):
        f.append((("xT", 2, i), "act"))
    us = range(2)
    for w in ("k", "q", "v"):
        f.extend(((w + "1", u), "act") for u in us)
    f.extend((("nc", "k", 1, u), "act") for u in us)
    f.extend((("nc", "q", 1, u), "act") for u in us)
    f.extend((("nv", "k", 1, u), "act") for u in us)
    f.extend((("nv", "q", 1, u), "act") for u in us)
    f.extend((("vr", 1, u), "act") for u in us)
    f.extend((("kr", 1, u), "act") for u in us)
    for a in (1, 2, 3):
        if a > 1:
            f.extend((("nc", "q", a, u), "act") for u in us)
            f.extend((("fvb", a, 0, j), "dve") for j in range(2))
            f.extend((("nv", "q", a, u), "act") for u in us)
            f.extend((("fvb", a, 0, j), "dve") for j in range(2, 4))
        f.extend((("fS", a, u), "dve") for u in us)
        if a < 3:
            f.extend((("nc", "k", a + 1, u), "act") for u in us)
            if a < 2:
                f.extend((("kr", a + 1, u), "act") for u in us)
            f.extend((("nv", "k", a + 1, u), "act") for u in us)
        else:
            f.append((("df",), "dve"))
        if a == 1:
            f.extend((("fvb", a, 0, j), "dve") for j in range(4))
        f.extend((("fvb", a, 1, j), "dve") for j in range(4))
        f.extend((("fPT", a, u), "act") for u in us)
        if a < 3:
            f.extend((("vr", a + 1, u), "act") for u in us)
        f.extend((("O", a, u), "dve") for u in us)
    for i in range(3):
        f.append((("wo", 1, i), "dve"))
    f.extend(max_fills(0))
    for i in range(3):
        f.append((("xT", 3, i), "act"))
    for w in ("ga", "up"):
        for o in range(FC):
            for c in range(2):
                f.append(((w, o, c), "act"))
            if (w, o) == ("up", 1):
                f.extend(max_fills(1))
    f.extend(max_fills(2))
    f.extend(max_fills(3))
    f.extend(max_fills(4))
    for t in range(TT):
        f.append((("dn", t), "dve"))
    return f


def max_fills(n):
    return [(("mxT", n), "dve"), (("mxB", n), "dve")]


FILLS = fills()
FILL = {key: n for n, (key, _) in enumerate(FILLS)}
assert len(FILL) == len(FILLS)
NTH = {}
for _who in ("act", "dve"):
    for _n, _key in enumerate(k for k, w in FILLS if w == _who):
        NTH[_key] = (_who, _n + 1)
NORMS = {key[1:]: n for n, key in enumerate(k for k, _ in FILLS if k[0] == "nc")}


def build(nc, i, out):
    with ExitStack() as ctx:
        def sb(name, *shape):
            return ctx.enter_context(nc.sbuf_tensor(name, list(shape), F32))

        def sem(name):
            return ctx.enter_context(nc.semaphore(name))

        h_dram = nc.dram_tensor("h_scratch", (NT, D), F32).ap()
        o_dram = nc.dram_tensor("o_scratch", (B, T * D), F32).ap()

        QK = CB * KW
        QV = CB * NH * VW
        XI = NC * PS * NG * PS
        BIG = 2 * XI + 6 * NG * 96 + 6 * D
        big = sb("big", P, BIG)
        small = sb("small", P, 2 * QV + 3 * FC * D)
        kexp = [big[:, n * QK:(n + 1) * QK].rearrange("p (b h k) -> p b h k", b=CB, h=NH) for n in range(2)]
        vals = [small[:, n * QV:(n + 1) * QV].rearrange("p (b h v) -> p b h v", b=CB, h=NH) for n in range(2)]
        at = [0]

        def cut(region, n):
            at[0] += n
            return region[:, at[0] - n:at[0]]

        img = cut(big, XI)
        patches = cut(big, XI)
        patT = cut(big, 6 * NG * 96).rearrange("p (k w t) -> p k w t", k=6, w=NG)
        lin_w = cut(big, 6 * D).rearrange("p (k n) -> p k n", k=6)
        at[0] = 2 * QK
        w_eg = cut(big, KD * NE * EI).rearrange("p (k e i) -> p k e i", k=KD, e=NE)
        w_eu = cut(big, KD * NE * EI).rearrange("p (k e i) -> p k e i", k=KD, e=NE)
        w_ed = cut(big, NE * D).rearrange("p (e n) -> p e n", e=NE)
        w_sg = cut(big, KD * D).rearrange("p (k i) -> p k i", k=KD)
        w_su = cut(big, KD * D).rearrange("p (k i) -> p k i", k=KD)
        w_sd = cut(big, KD * D).rearrange("p (k n) -> p k n", k=KD)
        assert at[0] <= BIG
        at[0] = 0
        fkeys = cut(big, KD * B * P).rearrange("p (u m h k) -> p u m h k", u=2, m=B, h=NH)
        fvals = cut(big, KD * B * P).rearrange("p (u m h k) -> p u m h k", u=2, m=B, h=NH)
        fvalsT = cut(big, KD * B * P).rearrange("p (u m n) -> p u m n", u=2, m=B)
        assert at[0] <= BIG
        at[0] = 0
        gate = cut(big, FC * NP)
        up = cut(big, FC * NP)
        sig = cut(big, FC * NP)
        at[0] = 0
        raw = {n: cut(small, KD * D).rearrange("p (o i) -> p o i", o=KD) for n in ("q0", "o0", "q1", "k1", "v1", "o1")}
        raw_kv = cut(small, D)
        at[0] = 2 * QV
        fraw = [cut(small, FC * D) for _ in range(3)]

        h = sb("h", P, TT, D)
        xn = sb("xn", P, TT, D)
        xT = sb("xT", P, KD, NP)
        att = sb("att", P, 2 * 3 * CH)
        attT = att[:, 0:KD * NP].rearrange("p (k t) -> p k t", k=KD)
        values3 = att[:, :].rearrange("p (n b m) -> p n b m", n=2, b=CB)
        wT = {n: sb("wT_" + n, P, KD, D) for n in raw}
        wkT = sb("wkT", P, KD, P)
        wvT = sb("wvT", P, KD, P)
        fT = [sb("fT0", P, KD, FI), sb("fT1", P, KD, FI), sb("fT2", P, FC, D)]
        qsT = sb("qsT", P, KD, 2, QW)
        cur = sb("cur", P, B // 2 * D)
        q_cur, k_cur, v_cur = (cur[:, n * KD * CF:(n + 1) * KD * CF].rearrange("p (k t) -> p k t", k=KD) for n in range(3))
        regrouped = cur[:, 0:B // 2 * D].rearrange("p (s n) -> p s n", n=D)
        hid = cur[:, 0:3 * NP].rearrange("p (n t) -> p n t", n=3)
        passes = sb("passes", P, NG * D)
        pass_out = [passes[:, n * KD * CF:(n + 1) * KD * CF].rearrange("p (k t) -> p k t", k=KD) for n in range(2)]
        pos = passes[0:96, 0:NG * D].rearrange("p (w n) -> p w n", w=NG)
        keys_n = sb("keys_n", P, 2, CH)
        NR = 4
        cen_all = sb("cen", P, NR * CF)
        cen = cen_all[:, :].rearrange("p (n t) -> p n t", n=NR)
        silu = cen_all[:, 0:2 * HP].rearrange("p (c t) -> p c t", c=2)
        sqr_all = sb("sqr", P, NR * CF)
        sqr = sqr_all[:, :].rearrange("p (n t) -> p n t", n=NR)
        r_lin, r_ln2w, r_ln2b = (sqr_all[:, n * D:(n + 1) * D] for n in range(3))
        rsd_all = sb("rsd", P, NR * CF)
        rsd = rsd_all[:, :].rearrange("p (n t) -> p n t", n=NR)
        cls = rsd_all[0:B, 0:2 * D].rearrange("p (j n) -> p j n", j=2)
        cmpa, cmpb = (rsd_all[:, n * TT * NE * NE:(n + 1) * TT * NE * NE].rearrange(
            "p (t i j) -> p t i j", t=TT, i=NE) for n in range(2))
        probs_all = sb("probs", P, 3 * KD * KW)
        probs = probs_all[:, :].rearrange("p (n k w) -> p n k w", n=3, k=KD)
        y = probs_all[0:96, 0:NG * D].rearrange("p (w n) -> p w n", w=NG)
        fprobs, fprobsT = (probs_all[:, n * 2 * CF:(n + 1) * 2 * CF].rearrange(
            "p (u t) -> p u t", u=2) for n in range(2))
        probsT = sb("probsT", G3, 2, KD, 3 * P)
        queries_n = sb("queries_n", P, 2, 2 * CF + TF)
        fmax = sb("fmax", P, 2, B)
        fsum = sb("fsum", P, 2, B)
        heads = sb("heads", P, 2, KD, NH, HD)
        head_max = sb("head_max", P, KD, NH)
        head_rec = sb("head_rec", P, KD, NH)
        ident = sb("ident", P, P)
        ones = sb("ones", P, P)
        head_of = sb("head_of", P, NH)
        key_of = sb("key_of", G3, NH)
        mean_m = sb("mean_m", P, NH, HD)
        rep_i = sb("rep_i", HD, NH, HD)
        rep_c = sb("rep_c", HD, NH, HD)
        low = sb("low", P, NE, NE)
        eps_c = sb("eps_c", P, 1)
        nhalf = sb("nhalf", P, 8)
        two_16 = sb("two_16", P, 1)
        wl = sb("wl", HD, 3, HD)
        wl8 = sb("wl8", HD, 3, NH, HD)
        blr = sb("blr", HD, 3)
        wlT = sb("wlT", P, 4, P)
        bl = sb("bl", P, 4)
        cols = sb("cols", P, 40)
        c_ln1w, c_ln1b = cols[:, 0:6], cols[:, 6:12]
        c_bq0, c_bq1, c_bv1, c_lna = cols[:, 12:14], cols[:, 14:16], cols[:, 16:18], cols[:, 18:20]
        c_bk0, c_bv0 = cols[:, 20:21], cols[:, 21:22]
        c_lnc, c_lnd, c_temp, c_thr, c_fac = (cols[:, n:n + 1] for n in range(22, 27))
        c_hbq1 = cols[:, 28:30]
        q_w = sb("q_w", P, 3)
        k_w = sb("k_w", P, NH)
        temps = sb("temps", P, 4, 3)
        r_bo = [sb("r_bo0", P, D), sb("r_bo1", P, D)]
        r_gb = sb("r_gb", P, NE)
        gate_w = sb("gate_w", P, KD, NE)
        st = sb("st", P, 18, 6)
        mv = sb("mv", P, NG, 2)
        var = sb("var", P, 8)
        rstd = sb("rstd", P, 8)
        root = sb("root", P, TT)
        root2 = sb("root2", P, TT)
        sc = sb("sc", P, TT, NE)
        rt = sb("rt", P, 6, TT * NE)
        route = sb("route", P, TT, NE)
        bs = sb("bs", P, 3, FC * NB)
        bi = sb("bi", P, 3, FC * NB)
        mx = sb("mx", P, 8)
        gmx = sb("gmx", 1, 8)
        part = sb("part", P, 2 * FC)
        qs = sb("qs", P, 6, 2)
        dfs = sb("dfs", P, 8)

        banks = [ctx.enter_context(nc.psum_tensor(f"bank{n}", [P, 512], F32)) for n in range(8)]

        bank_filled = sem("bank_filled")
        emptied_by = {"act": sem("act_emptied"), "dve": sem("dve_emptied")}
        dve_chain, act_chain, pool_chain = sem("dve_chain"), sem("act_chain"), sem("pool_chain")
        images_in = [sem(f"images_in{n}") for n in range(NC)]
        (patch_w_in, cols_in, attn_w_in, rows_in, pos_in, moe_in, ffn_in, h_stored, h_in, out_stored) = (
            sem(n) for n in ("patch_w_in", "cols_in", "attn_w_in", "rows_in", "pos_in", "moe_in", "ffn_in",
                             "h_stored", "h_in", "out_stored"))
        o_stored = [sem(f"o_stored{n}") for n in range(B // 2)]
        regrouped_in = [sem(f"regrouped_in{n}") for n in range(B // 2)]
        consts_ready = sem("consts_ready")
        derived_ready = sem("derived_ready")
        var_ready = sem("var_ready")
        rstd_ready = sem("rstd_ready")
        patches_ready = sem("patches_ready")
        y_ready = sem("y_ready")
        xn_ready = sem("xn_ready")
        exp_done = sem("exp_done")
        root_done = sem("root_done")
        normed = sem("normed")
        keys_spread = sem("keys_spread")
        fkeys_spread = sem("fkeys_spread")
        fvals_spread = sem("fvals_spread")
        attT_cleared = sem("attT_cleared")
        fexp_done = sem("fexp_done")
        fprobs_ready = sem("fprobs_ready")
        fw_ready = sem("fw_ready")
        mx_ready = sem("mx_ready")
        wl8_ready = sem("wl8_ready")
        gate_ready = sem("gate_ready")
        temps_ready = sem("temps_ready")
        temps_rooted = sem("temps_rooted")
        sig_done = sem("sig_done")
        silu_ready = sem("silu_ready")
        o_ready = sem("o_ready")
        df_ready = sem("df_ready")
        scales_in_use = sem("scales_in_use")

        def filled(eng, key):
            eng.wait_ge(bank_filled, FILL[key] + 1)

        def emptied(eng, key):
            who, nth = NTH[key]
            eng.wait_ge(emptied_by[who], nth)

        def bank_of(key):
            return banks[FILL[key] % 8]

        def take(eng, key):
            filled(eng, key)
            return bank_of(key)

        block = ctx.enter_context(nc.Block())

        @block.sync
        def _(sp):
            im = i["x"].rearrange("b c (g r) w -> c b g (r w)", g=NG)
            imv = img.rearrange("p (c n) -> p c n", c=NC)
            for c in range(NC):
                sp.dma_start(imv[0:96, c, :], im[c]).then_inc(images_in[c], 16)
            lw = i["L0_tok_lin_w"].rearrange("(k p c) n -> c p k n", k=2, p=P)
            for c in range(NC):
                sp.dma_start(lin_w[:, 2 * c:2 * c + 2, :], lw[c]).then_inc(patch_w_in, 16)
            for col, name in ((c_ln1w, "L0_tok_ln1_w"), (c_ln1b, "L0_tok_ln1_b")):
                v = i[name].rearrange("(k p c) -> c p k", k=2, p=P)
                for c in range(NC):
                    sp.dma_start(col[:, 2 * c:2 * c + 2], v[c], allow_slow_non_contiguous=True).then_inc(cols_in, 16)
            for col, name in ((c_bq0, "L0_attn_bq"), (c_bq1, "L1_attn_bq"), (c_bv1, "L1_attn_bv"), (c_lna, "L1_attn_lna_w")):
                sp.dma_start(col, i[name].rearrange("(k p) -> p k", k=KD), allow_slow_non_contiguous=True).then_inc(cols_in, 16)
            kv = i["L0_attn_bkv"]
            for col, v in ((c_bk0, kv[0:HD]), (c_bv0, kv[HD:2 * HD]), (c_lnc, i["L1_attn_lnc_w"]), (c_lnd, i["L1_attn_lnd_w"])):
                sp.dma_start(col, v.unsqueeze(0).to_broadcast([NH, HD]).unsqueeze(2)).then_inc(cols_in, 16)
            for col, name in ((c_temp, "L1_attn_temp"), (c_thr, "L1_attn_threshold"), (c_fac, "L1_attn_factor")):
                sp.dma_start(col, i[name].partition_broadcast(P)).then_inc(cols_in, 16)
            for col, name in ((r_lin, "L0_tok_lin_b"), (r_ln2w, "L0_tok_ln2_w"), (r_ln2b, "L0_tok_ln2_b"),
                              (r_bo[0], "L0_attn_bo"), (r_bo[1], "L1_attn_bo"), (r_gb, "L0_ffn_gate_bias")):
                sp.dma_start(col[:, :], i[name].partition_broadcast(P)).then_inc(rows_in, 16)
            pe = i["L0_tok_pos_embedding"]
            band = pe[0, 1:T, :].rearrange("(g w) n -> g (w n)", g=NG)
            sp.dma_start(pos.rearrange("p w n -> p (w n)"),
                         band.unsqueeze(0).to_broadcast([B, NG, NG * D])).then_inc(pos_in, 16)
            sp.dma_start(cls[:, 0, :], i["L0_tok_cls_token"][0, 0, :].partition_broadcast(B)).then_inc(pos_in, 16)
            sp.dma_start(cls[:, 1, :], pe[0, 0, :].partition_broadcast(B)).then_inc(pos_in, 16)
            hv = h_dram.rearrange("(b t) n -> b t n", b=B)
            sp.wait_ge(y_ready, 1)
            sp.dma_start(hv[:, 0, :], cls[:, 0, :]).then_inc(h_stored, 16)
            sp.wait_ge(y_ready, 2)
            sp.dma_start(hv[:, 1:T, :].rearrange("b (g w) n -> b g (w n)", g=NG),
                         y.rearrange("p w n -> p (w n)")).then_inc(h_stored, 16)
            sp.wait_ge(h_stored, 32)
            sp.wait_ge(consts_ready, N_CONSTS)
            sp.dma_start(h[:, 0:TT - 1, :], h_dram[0:(TT - 1) * P, :].rearrange("(t p) n -> p t n", p=P)).then_inc(h_in, 16)
            sp.dma_start(h[0:LAST, TT - 1, :], h_dram[(TT - 1) * P:NT, :]).then_inc(h_in, 16)
            filled(sp, ("bl",))
            for n, name in enumerate(("w_gate", "w_up")):
                sp.dma_start(fraw[n].rearrange("p (o i) -> p o i", o=FC),
                             i["L1_ffn_" + name].rearrange("(o p) i -> p o i", p=P)).then_inc(ffn_in, 16)
            sp.dma_start(fraw[2].rearrange("p (o i) -> p o i", o=KD),
                         i["L1_ffn_w_down"].rearrange("(o p) i -> p o i", p=P)).then_inc(ffn_in, 16)
            filled(sp, ("y", 2))
            for k in range(KD):
                rows = slice(k * P, (k + 1) * P)
                sp.dma_start(w_eg[:, k, :, :], i["L0_ffn_w_gate"][:, rows, :].rearrange("e p i -> p e i")).then_inc(moe_in, 16)
                sp.dma_start(w_eu[:, k, :, :], i["L0_ffn_w_up"][:, rows, :].rearrange("e p i -> p e i")).then_inc(moe_in, 16)
            sp.dma_start(w_ed, i["L0_ffn_w_down"].rearrange("e p n -> p e n")).then_inc(moe_in, 16)
            for dst, name in ((w_sg, "sw_gate"), (w_su, "sw_up"), (w_sd, "sw_down")):
                sp.dma_start(dst, i["L0_ffn_" + name].rearrange("(k p) n -> p k n", p=P)).then_inc(moe_in, 16)
            ov = o_dram.rearrange("b (h t d) -> b t h d", t=T, d=HD)

            def regroup(p):
                sp.wait_ge(o_stored[p], 32)
                for j in range(2):
                    sp.dma_start(regrouped[64 * j:64 * j + T, p, :].rearrange("p (h d) -> p h d", d=HD),
                                 ov[2 * p + j]).then_inc(regrouped_in[p], 16)

            for p in range(B // 2):
                emptied(sp, ("PV", p))
                for j in range(2):
                    sp.dma_start(o_dram[2 * p + j].rearrange("(t n) -> t n", t=T),
                                 heads[64 * j:64 * j + T, p % 2, :, :, :].rearrange("p k h d -> p (k h d)")
                                 ).then_inc(o_stored[p], 16)
                if p:
                    regroup(p - 1)
            regroup(B // 2 - 1)
            ot = out.rearrange("b t n -> (b t) n")
            for t in range(TT):
                n = P if t < TT - 1 else LAST
                emptied(sp, ("dn", t))
                sp.dma_start(ot[t * P:t * P + n, :], h[0:n, t, :]).then_inc(out_stored, 16)
            sp.wait_ge(out_stored, 16 * TT)

        @block.gpsimd
        def _(pool):
            links = [0]

            def link(ins):
                links[0] += 1
                ins.then_inc(pool_chain, 1)
                pool.wait_ge(pool_chain, links[0])

            pool.memset(ident[:, :], 0.0)
            pool.memset(head_of[:, :], 1.0)
            pool.memset(key_of[:, :], 1.0)
            pool.memset(low[:, :, :], 1.0)
            pool.memset(ones[:, :], 1.0)
            pool.memset(eps_c[:, :], EPS)
            pool.memset(nhalf[:, :], -0.5)
            link(pool.memset(two_16[:, :], 2.0 ** -16))
            pool.affine_select(out=ident[:, :], in_=ident[:, :], compare_op=ALU.not_equal, fill=1.0, base=0,
                               pattern=[[-1, P]], channel_multiplier=1)
            pool.affine_select(out=low[:, :, :], in_=low[:, :, :], compare_op=ALU.is_ge, fill=0.0, base=-1,
                               pattern=[[1, NE], [-1, NE]], channel_multiplier=0)
            pool.affine_select(out=head_of[:, :], in_=head_of[:, :], compare_op=ALU.is_ge, fill=0.0, base=0,
                               pattern=[[-HD, NH]], channel_multiplier=1)
            k6 = key_of[:, 0:6].rearrange("p (g j) -> p g j", g=2)
            link(pool.affine_select(out=k6, in_=k6, compare_op=ALU.is_ge, fill=0.0, base=0,
                                    pattern=[[0, 2], [-T, 3]], channel_multiplier=1))
            link(pool.affine_select(out=head_of[:, :], in_=head_of[:, :], compare_op=ALU.is_ge, fill=0.0, base=HD - 1,
                                    pattern=[[HD, NH]], channel_multiplier=-1))
            link(pool.affine_select(out=k6, in_=k6, compare_op=ALU.is_ge, fill=0.0, base=T - 1,
                                    pattern=[[0, 2], [T, 3]], channel_multiplier=-1))
            link(pool.affine_select(out=key_of[:, 6:8], in_=key_of[:, 6:8], compare_op=ALU.is_ge, fill=0.0, base=-T,
                                    pattern=[[-T, 2]], channel_multiplier=1))
            link(pool.affine_select(out=key_of[:, 6:8], in_=key_of[:, 6:8], compare_op=ALU.is_ge, fill=0.0, base=2 * T - 1,
                                    pattern=[[T, 2]], channel_multiplier=-1))
            link(pool.memset(h[64:P, TT - 1, :], 0.0))
            pool.memset(qsT[:, :, :, CH:QW], 0.0)
            pool.memset(queries_n[:, :, :], 0.0)
            pool.memset(regrouped[:, :, :], 0.0).then_inc(consts_ready, 1)

            def inverse_root(n, rows, cols):
                pool.wait_ge(var_ready, n + 1)
                pool.tensor_tensor(rstd[0:rows, 0:cols], var[0:rows, 0:cols], nhalf[0:rows, 0:cols],
                                   ALU.pow).then_inc(rstd_ready, 1)

            inverse_root(0, 96, NG)
            inverse_root(1, 96, NG)
            pool.wait_ge(temps_ready, 1)
            pool.tensor_tensor(temps[:, 0, :], temps[:, 3, :], nhalf[:, 0:3], ALU.pow).then_inc(temps_rooted, 1)
            inverse_root(2, P, TT)

            def spread(dst, src, scale, by):
                for n in range(NH):
                    ins = pool.tensor_scalar(dst[:, :, n, :], src, scale[:, n:n + 1], by, ALU.mult, ALU.mult)
                return ins

            for c in range(2):
                emptied(pool, ("k0", c))
                spread(kexp[c], keys_n[:, c, :].rearrange("p (b k) -> p b k", b=CB), head_of, SM).then_inc(keys_spread, 1)
            inverse_root(3, P, TT)
            filled(pool, ("wo", 0, 2))
            pool.memset(att[:, 0:KD * NP], 0.0).then_inc(attT_cleared, 1)
            pool.wait_ge(var_ready, 5)
            link(pool.tensor_tensor(root[:, :], var[:, 0:TT], nhalf[:, 0:TT], ALU.pow))
            link(pool.tensor_tensor(root2[:, :], root[:, :], root[:, :], ALU.mult))
            link(pool.tensor_scalar(root2[:, :], root2[:, :], -EPS, 1.0 + EPS, ALU.mult, ALU.add))
            link(pool.tensor_tensor(root2[:, :], root2[:, :], nhalf[:, 0:TT], ALU.pow))
            pool.tensor_tensor(rstd[:, 0:TT], root[:, :], root2[:, :], ALU.mult).then_inc(rstd_ready, 1)
            pool.wait_ge(scales_in_use, 1)
            filled(pool, ("d", NE, 2))
            for a in (1, 2, 3):
                for u in range(2):
                    if a > 1:
                        filled(pool, ("fS", a - 1, u))
                    pool.wait_ge(normed, NORMS["k", a, u] + 1)
                    spread(fkeys[:, u], keys_n[:, u, 0:CF].rearrange("p (m k) -> p m k", m=B), k_w,
                           SM).then_inc(fkeys_spread, 1)
                for u in range(2):
                    if a > 1:
                        filled(pool, ("fvb", a - 1, u, 3))
                    emptied(pool, ("vr", a, u))
                    spread(fvals[:, u], v_cur[:, u, :].rearrange("p (m k) -> p m k", m=B), head_of,
                           1.0).then_inc(fvals_spread, 1)
            inverse_root(5, P, TT)

        @block.scalar
        def _(act):
            links = [0]

            def link(ins):
                links[0] += 1
                ins.then_inc(act_chain, 1)
                act.wait_ge(act_chain, links[0])

            def empty(ins):
                ins.then_inc(emptied_by["act"], 1)

            for name, arg in (("q0", "L0_attn_Wq"), ("o0", "L0_attn_Wo"), ("q1", "L1_attn_Wq"),
                              ("k1", "L1_attn_Wk"), ("v1", "L1_attn_Wv"), ("o1", "L1_attn_Wo")):
                act.dma_start(raw[name], i[arg].rearrange("(o p) i -> p o i", p=P)).then_inc(attn_w_in, 16)
            act.dma_start(raw_kv[0:2 * HD, :], i["L0_attn_Wkv"]).then_inc(attn_w_in, 16)
            for n, name in enumerate(("lq", "lk", "lv")):
                act.dma_start(wl[:, n, :], i["L1_attn_W" + name]).then_inc(attn_w_in, 16)
                act.dma_start(blr[:, n:n + 1], i["L1_attn_b" + name].unsqueeze(1), allow_slow_non_contiguous=True).then_inc(attn_w_in, 16)
            act.dma_start(gate_w[:, :, :], i["L0_ffn_gate_w"].rearrange("(k p) e -> p k e", p=P)).then_inc(attn_w_in, 16)
            act.wait_ge(cols_in, 16 * N_COLS)
            for g in range(2):
                for k in range(1, 6, 2):
                    b = take(act, ("xp", k, g))
                    empty(act.activation(patT[:, k, 3 * g:3 * g + 3, :].rearrange("p w t -> p (w t)"), b[:, 0:288],
                                         ACT.Identity, scale=c_ln1w[:, k:k + 1], bias=c_ln1b[:, k:k + 1]))

            for n in ("q0", "o0", "q1", "k1", "v1", "o1"):
                b = take(act, ("wT", n))
                empty(act.copy(wT[n].rearrange("p k o -> p (k o)"), b[:, :]))
            b = take(act, ("wkvT",))[:, 0:4 * HD].rearrange("p (k n) -> p k n", k=KD)
            for n, dst in enumerate((wkT, wvT)):
                for k in range(KD):
                    ins = act.copy(dst[:, k, :].rearrange("p (r d) -> p r d", d=HD),
                                   b[:, k, n * HD:(n + 1) * HD].unsqueeze(1).to_broadcast([P, NH, HD]))
            empty(ins)
            def turned(n, scales=None):
                for j in range(3):
                    b = take(act, ("xT", n, j))
                    tiles = 2 if j < 2 else 1
                    for k in range(KD):
                        dst = xT[:, k, 2 * j * P:(2 * j + tiles) * P].rearrange("p (t c) -> p t c", c=P)
                        src = b[:, 0:tiles * D].rearrange("p (t k c) -> p t k c", k=KD, c=P)[:, :, k, :]
                        if scales is None:
                            ins = act.copy(dst, src)
                        else:
                            ins = act.mul(dst, src, scales[:, k:k + 1])
                    empty(ins)

            def three_times(b, bias, m):
                for r in range(3):
                    ins = act.activation(values3[:, m % 2, :, r * T:(r + 1) * T],
                                         b[:, 0:CH].rearrange("p (b k) -> p b k", b=CB), ACT.Identity, bias=bias)
                empty(ins)

            turned(0)
            for c in range(2):
                b = take(act, ("k0", c))
                empty(act.activation(keys_n[:, c, :], b[:, 0:CH], ACT.Identity, bias=c_bk0))
                b = take(act, ("v0", c))
                three_times(b, c_bv0, c)
                for hf in range(KD):
                    b = take(act, ("q0", hf, c))
                    if (hf, c) == (0, 0):
                        act.wait_ge(consts_ready, N_CONSTS)
                    empty(act.activation(qsT[:, hf, c, 0:CH], b[:, 0:CH], ACT.Identity, bias=c_bq0[:, hf:hf + 1]))

            def exps(s):
                for hf in range(KD):
                    emptied(act, ("S", s, hf))
                    v = probs[:, s % 3, hf, :]
                    act.activation(v, v, ACT.Exp).then_inc(exp_done, 1)

            def probs_turned(s):
                if s >= 2:
                    filled(act, ("PV", s - 2))
                for hf in range(KD):
                    b = take(act, ("PT", s, hf))
                    empty(act.copy(probsT[:, s % 2, hf, :], b[0:G3, 0:3 * P]))

            def centred(key):
                r = NORMS[key]
                which = key[0]
                if r >= NR:
                    act.wait_ge(normed, r - NR + 1)
                b = take(act, ("nc", *key))
                bias = bl[:, 0:1] if which == "q" else bl[:, 1:2]
                act.activation(cen[:, r % NR, :], b[:, 0:CF], ACT.Identity, bias=bias)
                empty(act.activation(sqr[:, r % NR, :], b[:, 0:CF], ACT.Square, bias=bias))

            def inverse_root(key):
                r = NORMS[key]
                b = take(act, ("nv", *key))
                v = rsd[:, r % NR, :]
                ins = act.activation(v, b[:, 0:CF], ACT.Ln, bias=eps_c[:, 0:1])
                empty(ins)
                emptied(act, ("nv", *key))
                act.activation(v, v, ACT.Exp, scale=-0.5).then_inc(root_done, 1)

            for s in range(B // 2 + 1):
                if s < B // 2:
                    exps(s)
                if s:
                    probs_turned(s - 1)
            for p in range(B // 2):
                b = take(act, ("AT", p))
                empty(act.copy(attT[:, :, 2 * T * p:2 * T * (p + 1)].rearrange("p k (j t) -> p k j t", j=2),
                               b[:, 0:2 * P].rearrange("p (k j t) -> p k j t", k=KD, j=2)[:, :, :, 0:T]))
            turned(1)
            b = take(act, ("lg",))
            empty(act.activation(sc.rearrange("p t e -> p (t e)"), b[:, 0:TT * NE], ACT.Sigmoid))
            for e in range(NX + 1):
                if e < NX:
                    for c in range(2):
                        b = take(act, ("g", e, c))
                        if e:
                            emptied(act, ("u", e - 1, c))
                        empty(act.activation(silu[:, c, :], b[:, 0:HP], ACT.Silu))
                if 1 <= e <= 9:
                    w, j = (e - 1) // 3, (e - 1) % 3
                    b = take(act, ("fw", e - 1))
                    if w < 2:
                        empty(act.copy(fT[w][:, :, j * D:(j + 1) * D], b[:, :].rearrange("p (k o) -> p k o", k=KD)))
                    else:
                        empty(act.copy(fT[2][:, 2 * j:2 * j + 2, :], b[:, :].rearrange("p (c o) -> p c o", c=2)))
            turned(2, c_lna)
            act.wait_ge(scales_in_use, 1)
            us = range(2)
            for w, dst in (("k", k_cur), ("q", q_cur), ("v", v_cur)):
                for u in us:
                    b = take(act, (w + "1", u))[:, 0:CF]
                    if w == "k":
                        empty(act.mul(dst[:, u, :], b, KSCALE))
                        continue
                    for f in range(KD):
                        c = slice(f * P, (f + 1) * P)
                        if w == "q":
                            ins = act.activation(dst[:, u, c], b[:, c], ACT.Identity, scale=KSCALE, bias=c_hbq1[:, f:f + 1])
                        else:
                            ins = act.activation(dst[:, u, c], b[:, c], ACT.Identity, bias=c_bv1[:, f:f + 1])
                    empty(ins)

            def refreshed(which, a, u):
                dst, m = (k_cur, 2) if which == "kr" else (v_cur, 3)
                if which == "vr" and a > 1:
                    act.wait_ge(fvals_spread, 2 * (a - 2) + u + 1)
                b = take(act, (which, a, u))
                empty(act.activation(dst[:, u, :], b[:, 0:CF], ACT.Identity, bias=bl[:, m:m + 1]))

            act.preload_act_table_set("natural_log_exp_and_others")
            for w in ("k", "q"):
                for u in us:
                    centred((w, 1, u))
            for w in ("k", "q"):
                for u in us:
                    inverse_root((w, 1, u))
            for w in ("vr", "kr"):
                for u in us:
                    refreshed(w, 1, u)
            for a in (1, 2, 3):
                if a > 1:
                    for u in us:
                        centred(("q", a, u))
                    for u in us:
                        inverse_root(("q", a, u))
                if a < 3:
                    for u in us:
                        centred(("k", a + 1, u))
                for u in us:
                    emptied(act, ("fS", a, u))
                    act.activation(fprobs[:, u, :], fprobs[:, u, :], ACT.Exp).then_inc(fexp_done, 1)
                if a < 2:
                    for u in us:
                        refreshed("kr", a + 1, u)
                if a < 3:
                    for u in us:
                        inverse_root(("k", a + 1, u))
                for u in us:
                    if a > 1:
                        filled(act, ("O", a - 1, u))
                    b = take(act, ("fPT", a, u))
                    empty(act.copy(fprobsT[:, u, :], b[:, 0:CF]))
                if a < 3:
                    for u in us:
                        refreshed("vr", a + 1, u)
            turned(3)
            for w, dst in (("ga", gate), ("up", up)):
                for o in range(FC):
                    for c in range(2):
                        b = take(act, (w, o, c))
                        empty(act.copy(dst[:, o * NP + c * HP:o * NP + (c + 1) * HP], b[:, 0:HP]))
                    if w == "up" and o % 2:
                        n = slice((o // 2) * FC * NP // 3, (o // 2 + 1) * FC * NP // 3)
                        act.wait_ge(gate_ready, o // 2 + 1)
                        act.activation(sig[:, n], gate[:, n], ACT.Sigmoid, scale=qs[:, 1, 0:1]).then_inc(sig_done, 1)

        @block.vector
        def _(dve):
            links = [0]

            def link(ins):
                links[0] += 1
                ins.then_inc(dve_chain, 1)
                dve.wait_ge(dve_chain, links[0])

            def empty(ins):
                ins.then_inc(emptied_by["dve"], 1)

            def rows_of(t):
                return P if t < TT - 1 else LAST

            dve.wait_ge(consts_ready, N_CONSTS)
            dve.tensor_scalar(mean_m[:, :, :], head_of[:, :].unsqueeze(2).to_broadcast([P, NH, HD]), 1.0 / HD, None, ALU.mult)
            id16 = ident[0:HD, 0:HD].unsqueeze(1).to_broadcast([HD, NH, HD])
            dve.tensor_scalar(rep_i[:, :, :], id16, 0.0, None, ALU.add)
            dve.tensor_scalar(rep_c[:, :, :], id16, -1.0 / HD, None, ALU.add).then_inc(derived_ready, 1)

            pv = img[0:96, :].rearrange("p (c r w q) -> p c r w q", c=NC, r=PS, w=NG)
            for c in range(NC):
                dve.wait_ge(images_in[c], 16)
                for w in range(NG):
                    ins = dve.bn_stats(st[0:96, 3 * w + c, :], pv[:, c, :, w, :])
            link(ins)
            for w in range(NG):
                ins = dve.bn_aggr(mv[0:96, w, :], st[0:96, 3 * w:3 * w + 3, :].rearrange("p a b -> p (a b)"))
            link(ins)
            dve.tensor_scalar(var[0:96, 0:NG], mv[0:96, :, 1], EPS, None, ALU.add).then_inc(var_ready, 1)
            dve.wait_ge(rstd_ready, 1)
            po = patches[0:96, :].rearrange("p (w c r q) -> p w c r q", w=NG, c=NC, r=PS)
            for w in range(NG):
                for c in range(NC):
                    ins = dve.tensor_scalar(po[:, w, c, :, :], pv[:, c, :, w, :], mv[0:96, w, 0:1], rstd[0:96, w:w + 1],
                                            ALU.subtract, ALU.mult)
                if w % 3 == 2:
                    ins.then_inc(patches_ready, 1)
            dve.wait_ge(cols_in, 16 * N_COLS)
            for n in range(3):
                ins = dve.tensor_scalar(temps[:, 0, n:n + 1], c_temp, 0.005 * n, None, ALU.add)
            link(ins)
            dve.tensor_scalar(temps[:, 1, :], temps[:, 0, :], 0.0, None, ALU.is_gt)
            link(dve.tensor_scalar(temps[:, 2, :], temps[:, 0, :], 1.0, None, ALU.not_equal))
            dve.tensor_scalar(temps[:, 3, :], temps[:, 0, :], 1e-37, None, ALU.max).then_inc(temps_ready, 1)
            for g in range(2):
                for k in range(0, 6, 2):
                    b = take(dve, ("xp", k, g))
                    empty(dve.tensor_scalar(patT[:, k, 3 * g:3 * g + 3, :].rearrange("p w t -> p (w t)"), b[:, 0:288],
                                            c_ln1w[:, k:k + 1], c_ln1b[:, k:k + 1], ALU.mult, ALU.add))
            dve.wait_ge(pos_in, 48)
            dve.wait_ge(rows_in, 96)
            dve.tensor_tensor(cls[:, 0, :], cls[:, 0, :], cls[:, 1, :], ALU.add).then_inc(y_ready, 1)
            link(dve.tensor_tensor(pos[:, :, :], pos[:, :, :], r_ln2b[0:96, :].unsqueeze(1).to_broadcast([96, NG, D]), ALU.add))
            for j in range(3):
                b = take(dve, ("y", j))
                v = y[:, 2 * j:2 * j + 2, :]
                empty(dve.tensor_tensor(v, b[0:96, :].rearrange("p (w n) -> p w n", w=2),
                                        r_lin[0:96, :].unsqueeze(1).to_broadcast([96, 2, D]), ALU.add))
                emptied(dve, ("y", j))
                for w in (2 * j, 2 * j + 1):
                    ins = dve.bn_stats(st[0:96, w, :], y[:, w, :])
            link(ins)
            for w in range(NG):
                ins = dve.bn_aggr(mv[0:96, w, :], st[0:96, w, :])
            link(ins)
            dve.tensor_scalar(var[0:96, 0:NG], mv[0:96, :, 1], EPS, None, ALU.add).then_inc(var_ready, 1)
            dve.wait_ge(rstd_ready, 2)
            for w in range(NG):
                ins = dve.tensor_scalar(y[:, w, :], y[:, w, :], mv[0:96, w, 0:1], rstd[0:96, w:w + 1],
                                        ALU.subtract, ALU.mult)
            link(ins)
            link(dve.tensor_tensor(y[:, :, :], y[:, :, :], r_ln2w[0:96, :].unsqueeze(1).to_broadcast([96, NG, D]), ALU.mult))
            dve.tensor_tensor(y[:, :, :], y[:, :, :], pos[:, :, :], ALU.add).then_inc(y_ready, 1)
            dve.wait_ge(attn_w_in, 16 * N_ATTN_W)
            dve.tensor_copy(wl8[:, :, :, :], wl[:, :, :].unsqueeze(2).to_broadcast([HD, 3, NH, HD])).then_inc(wl8_ready, 1)
            b = take(dve, ("wl",))
            empty(dve.tensor_tensor(wlT.rearrange("p m (h d) -> p m h d", h=NH),
                                    b[:, :].rearrange("p (m h d) -> p m h d", m=4, h=NH),
                                    head_of[:, :].unsqueeze(1).unsqueeze(3).to_broadcast([P, 4, NH, HD]), ALU.mult))
            b = take(dve, ("bl",))
            empty(dve.tensor_copy(bl[:, :], b[:, 0:4]))
            dve.wait_ge(temps_rooted, 1)
            link(dve.tensor_scalar(temps[:, 0, :], temps[:, 0, :], -1.0, None, ALU.add))
            link(dve.tensor_tensor(temps[:, 1, :], temps[:, 1, :], temps[:, 2, :], ALU.mult))
            link(dve.tensor_tensor(temps[:, 0, :], temps[:, 0, :], temps[:, 1, :], ALU.mult))
            dve.tensor_scalar(q_w[:, :], temps[:, 0, :], 1.0, c_lnc, ALU.add, ALU.mult)
            dve.tensor_scalar(k_w[:, :], head_of[:, :], c_lnd, None, ALU.mult)
            dve.tensor_scalar(c_hbq1, c_bq1, KSCALE, None, ALU.mult).then_inc(scales_in_use, 1)

            def statistics(ts):
                for t in ts:
                    ins = dve.bn_stats(st[:, t, :], h[:, t, :])
                return ins

            def layer_norm(n, stats):
                link(stats)
                for t in range(TT):
                    ins = dve.bn_aggr(mv[:, t, :], st[:, t, :])
                link(ins)
                if n > 2:
                    dve.wait_ge(xn_ready, (n - 2) * TT)
                dve.tensor_scalar(var[:, 0:TT], mv[:, 0:TT, 1], EPS, None, ALU.add).then_inc(var_ready, 1)
                dve.wait_ge(rstd_ready, n + 1)
                for t in range(TT):
                    dve.tensor_scalar(xn[:, t, :], h[:, t, :], mv[:, t, 0:1], rstd[:, t:t + 1],
                                      ALU.subtract, ALU.mult).then_inc(xn_ready, 1)

            def tiles_of(j):
                return range(2 * j, min(2 * j + 2, TT))

            def add_projection(n):
                dve.wait_ge(xn_ready, TT * (1 if n == 0 else 3))
                dve.tensor_tensor(h[:, 0:TT - 1, :], h[:, 0:TT - 1, :],
                                  r_bo[n][:, :].unsqueeze(1).to_broadcast([P, TT - 1, D]), ALU.add)
                link(dve.tensor_tensor(h[0:LAST, TT - 1, :], h[0:LAST, TT - 1, :], r_bo[n][0:LAST, :], ALU.add))
                for j in range(3):
                    b = take(dve, ("wo", n, j))
                    if j < 2:
                        v = h[:, 2 * j:2 * j + 2, :]
                        empty(dve.tensor_tensor(v, b[:, :].rearrange("p (t n) -> p t n", t=2), v, ALU.add))
                    else:
                        v = h[0:LAST, TT - 1, :]
                        empty(dve.tensor_tensor(v, b[0:LAST, 0:D], v, ALU.add))
                    emptied(dve, ("wo", n, j))
                    ins = statistics(tiles_of(j))
                return ins

            def values_by_key(c):
                dve.tensor_copy(vals[c][0:G3, :, :, HD], key_of[:, :].unsqueeze(1).to_broadcast([G3, CB, NH]))
                for j in range(2):
                    b = take(dve, ("vb", c, j))
                    empty(dve.tensor_tensor(vals[c][0:G3, 4 * j:4 * j + 4, :, 0:HD],
                                            b[0:G3, :].rearrange("p (b h d) -> p b h d", b=4, h=NH),
                                            key_of[:, :].unsqueeze(1).unsqueeze(3).to_broadcast([G3, 4, NH, HD]), ALU.mult))

            def scores(s):
                for hf in range(KD):
                    if s >= 1:
                        emptied(dve, ("S", s - 1, hf))
                    if s >= 3:
                        filled(dve, ("PT", s - 3, hf))
                    b = take(dve, ("S", s, hf))[:, 0:KW].rearrange("p (h k) -> p h k", h=NH)
                    link(dve.tensor_reduce(head_max[:, hf, :], b, AX.X, ALU.max))
                    empty(dve.tensor_tensor(probs[:, s % 3, hf, :].rearrange("p (h k) -> p h k", h=NH), b,
                                            head_max[:, hf, :].unsqueeze(2).to_broadcast([P, NH, T]), ALU.subtract))

            def weighted(s):
                if s >= 2:
                    dve.wait_ge(o_stored[s - 2], 32)
                if s:
                    emptied(dve, ("PV", s - 1))
                b = take(dve, ("PV", s))[:, 0:KD * NH * VW].rearrange("p (k h v) -> p k h v", k=KD, h=NH)
                link(dve.reciprocal(head_rec[:, :, :], b[:, :, :, HD]))
                empty(dve.tensor_tensor(heads[:, s % 2, :, :, :], b[:, :, :, 0:HD],
                                        head_rec[:, :, :].unsqueeze(3).to_broadcast([P, KD, NH, HD]), ALU.mult))

            def normalised(key, dst, scale):
                r = NORMS[key]
                dve.wait_ge(root_done, r + 1)
                dve.scalar_tensor_tensor(out=dst, in0=cen[:, r % NR, :].rearrange("p (m t) -> p m t", t=TF), scalar=scale,
                                         in1=rsd[:, r % NR, :].rearrange("p (m t) -> p m t", t=TF),
                                         op0=ALU.mult, op1=ALU.mult).then_inc(normed, 1)

            def normalised_keys(a, u):
                if a > 1:
                    dve.wait_ge(fkeys_spread, 2 * (a - 2) + u + 1)
                normalised(("k", a, u), keys_n[:, u, 0:CF].rearrange("p (m t) -> p m t", t=TF), 1.0)

            def normalised_queries(a, u):
                if a > 1:
                    filled(dve, ("fS", a - 1, u))
                normalised(("q", a, u), queries_n[:, u, TF:].rearrange("p (m t) -> p m t", t=2 * TF)[:, :, 0:TF],
                           q_w[:, a - 1:a])

            dve.wait_ge(h_in, 32)
            layer_norm(2, statistics(range(TT)))
            for c in range(2):
                values_by_key(c)
            for s in range(B // 2 + 2):
                if s < B // 2:
                    scores(s)
                if s >= 2:
                    weighted(s - 2)

            def dequantise(w):
                v = fraw[w].rearrange("p (n k) -> p n k", k=BLK)
                s_ = bs[:, w, :].unsqueeze(2).to_broadcast([P, FC * NB, BLK])
                i_ = bi[:, w, :].unsqueeze(2).to_broadcast([P, FC * NB, BLK])
                link(dve.tensor_reduce(bs[:, w, :], v, AX.X, ALU.max, apply_absolute_value=True))
                link(dve.tensor_scalar(bs[:, w, :], bs[:, w, :], 1.0 / QWT, TINY, ALU.mult, ALU.max))
                link(dve.reciprocal(bi[:, w, :], bs[:, w, :]))
                link(dve.tensor_tensor(v, v, i_, ALU.mult))
                link(dve.tensor_scalar(fraw[w], fraw[w], MAGIC, MAGIC, ALU.add, ALU.subtract))
                dve.tensor_tensor(v, v, s_, ALU.mult).then_inc(fw_ready, 1)

            dve.wait_ge(ffn_in, 48)
            dequantise(0)
            stats = add_projection(0)

            layer_norm(3, stats)
            filled(dve, ("lg",))
            emptied(dve, ("lg",))
            sfc = rt[:, 0, :].rearrange("p (t e) -> p t e", t=TT)
            grp = rt[:, 1, 0:TT * 4].rearrange("p (t g) -> p t g", t=TT)
            grk = rt[:, 2, 0:TT * 4].rearrange("p (t g) -> p t g", t=TT)
            tmp = rt[:, 3, :].rearrange("p (t e) -> p t e", t=TT)
            erk = rt[:, 4, :].rearrange("p (t e) -> p t e", t=TT)
            den = rt[:, 5, 0:TT]

            def top2(values, rank, n):
                other = values.unsqueeze(2).to_broadcast([P, TT, n, n])
                own = values.unsqueeze(3).to_broadcast([P, TT, n, n])
                ga, gb = cmpa[:, :, 0:n, 0:n], cmpb[:, :, 0:n, 0:n]
                dve.tensor_tensor(ga, other, own, ALU.is_gt)
                link(dve.tensor_tensor(gb, other, own, ALU.is_equal))
                link(dve.tensor_tensor(gb, gb, low[:, 0:n, 0:n].unsqueeze(1).to_broadcast([P, TT, n, n]), ALU.mult))
                link(dve.tensor_tensor(ga, ga, gb, ALU.add))
                link(dve.tensor_reduce(rank, ga, AX.X, ALU.add))
                link(dve.tensor_scalar(rank, rank, 2.0, None, ALU.is_lt))

            link(dve.tensor_tensor(sfc, sc[:, :, :], r_gb[:, :].unsqueeze(1).to_broadcast([P, TT, NE]), ALU.add))
            pair = sfc.rearrange("p t (g j) -> p t g j", j=2)
            link(dve.tensor_tensor(grp, pair[:, :, :, 0], pair[:, :, :, 1], ALU.add))
            top2(grp, grk, 4)
            link(dve.tensor_tensor(tmp.rearrange("p t (g j) -> p t g j", j=2), pair,
                                   grk.unsqueeze(3).to_broadcast([P, TT, 4, 2]), ALU.mult))
            top2(tmp, erk, NE)
            link(dve.tensor_tensor(route[:, :, :], erk, sfc, ALU.mult))
            link(dve.tensor_reduce(den, route[:, :, :], AX.X, ALU.add))
            link(dve.tensor_scalar(den, den, 1e-20, None, ALU.add))
            link(dve.reciprocal(den, den))
            link(dve.tensor_tensor(route[:, :, :], route[:, :, :], den.unsqueeze(2).to_broadcast([P, TT, NE]), ALU.mult))
            link(dve.tensor_scalar(route[:, :, :], route[:, :, :], 2.5, None, ALU.mult))

            def hidden(e):
                for c in range(2):
                    emptied(dve, ("g", e, c))
                    if e >= 3:
                        filled(dve, ("d", e - 3, 2))
                    b = take(dve, ("u", e, c))
                    empty(dve.tensor_tensor(hid[:, e % 3, c * HP:(c + 1) * HP], silu[:, c, :], b[:, 0:HP], ALU.mult))

            def add_expert(e):
                for j in range(3):
                    if e:
                        emptied(dve, ("d", e - 1, j))
                    b = take(dve, ("d", e, j))
                    for t in range(2 * j, min(2 * j + 2, TT)):
                        n = rows_of(t)
                        v = h[0:n, t, :]
                        src = b[0:n, (t % 2) * D:(t % 2 + 1) * D]
                        if e < NE:
                            ins = dve.scalar_tensor_tensor(out=v, in0=src, scalar=route[0:n, t, e:e + 1], in1=v,
                                                           op0=ALU.mult, op1=ALU.add)
                        else:
                            ins = dve.tensor_tensor(v, src, v, ALU.add)
                    empty(ins)
                    if e == NE:
                        emptied(dve, ("d", e, j))
                        ins = statistics(tiles_of(j))
                return ins

            for e in range(NX + 1):
                if e < NX:
                    hidden(e)
                if 1 <= e <= NE or e == NX:
                    stats = add_expert(min(e - 1, NE))
                if e in (1, 4):
                    dequantise(1 if e == 1 else 2)
            layer_norm(4, stats)
            def convergence():
                b = take(dve, ("df",))
                empty(dve.tensor_scalar(dfs[:, 1:2], b[:, 0:1], 1.0 / (NT * D), None, ALU.mult))
                emptied(dve, ("df",))
                link(dve.tensor_scalar(dfs[:, 2:3], dfs[:, 1:2], c_fac, c_thr, ALU.mult, ALU.add))
                link(dve.tensor_tensor(dfs[:, 3:4], dfs[:, 1:2], dfs[:, 2:3], ALU.is_lt))
                dve.tensor_scalar(dfs[:, 4:5], dfs[:, 3:4], -1.0, 1.0, ALU.mult, ALU.add)
                link(dve.tensor_scalar(pass_out[1][:, :, :], pass_out[1][:, :, :], dfs[:, 3:4], None, ALU.mult))

            def turned_values(a, u, js):
                for j in js:
                    if a > 1:
                        filled(dve, ("O", a - 1, u))
                    b = take(dve, ("fvb", a, u, j))
                    empty(dve.tensor_copy(fvalsT[:, u, 4 * j:4 * j + 4, :].rearrange("p m n -> p (m n)"), b[:, :]))

            us = range(2)
            for u in us:
                normalised_keys(1, u)
            for u in us:
                normalised_queries(1, u)
            for a in (1, 2, 3):
                if a > 1:
                    turned_values(a, 0, (0, 1))
                    for u in us:
                        normalised_queries(a, u)
                    turned_values(a, 0, (2, 3))
                for u in us:
                    if a > 1:
                        filled(dve, ("fPT", a - 1, u))
                    b = take(dve, ("fS", a, u))[:, 0:CF].rearrange("p (n k) -> p n k", k=TF)
                    link(dve.tensor_reduce(fmax[:, u, :], b, AX.X, ALU.max))
                    empty(dve.tensor_tensor(fprobs[:, u, :].rearrange("p (n k) -> p n k", k=TF), b,
                                            fmax[:, u, :].unsqueeze(2).to_broadcast([P, B, TF]), ALU.subtract))
                if a == 3:
                    d = pass_out[0]
                    link(dve.tensor_tensor(d[:, :, :], pass_out[1][:, :, :], d[:, :, :], ALU.subtract))
                    dve.tensor_reduce(dfs[:, 0:1], d[:, :, :], AX.XY, ALU.add, apply_absolute_value=True).then_inc(df_ready, 1)
                for u in us:
                    dve.wait_ge(fexp_done, 2 * (a - 1) + u + 1)
                    v = fprobs[:, u, :].rearrange("p (n k) -> p n k", k=TF)
                    link(dve.tensor_reduce(fsum[:, u, :], v, AX.X, ALU.add))
                    link(dve.reciprocal(fsum[:, u, :], fsum[:, u, :]))
                    dve.tensor_tensor(v, v, fsum[:, u, :].unsqueeze(2).to_broadcast([P, B, TF]),
                                      ALU.mult).then_inc(fprobs_ready, 1)
                if a == 3:
                    convergence()
                if a == 1:
                    turned_values(a, 0, range(4))
                turned_values(a, 1, range(4))
                if a < 3:
                    for u in us:
                        normalised_keys(a + 1, u)
                for u in us:
                    b = take(dve, ("O", a, u))[:, 0:CF]
                    if a < 3:
                        dve.tensor_copy(pass_out[a - 1][:, u, :], b)
                        empty(dve.tensor_tensor(q_cur[:, u, :], b, q_cur[:, u, :], ALU.add))
                    else:
                        dve.wait_ge(attT_cleared, 1)
                        for f in range(KD):
                            c = slice(f * P, (f + 1) * P)
                            ins = dve.scalar_tensor_tensor(
                                out=attT[:, f, u * CH:(u + 1) * CH].rearrange("p (b t) -> p b t", t=T)[:, :, 0:TF],
                                in0=b[:, c].rearrange("p (b t) -> p b t", t=TF), scalar=dfs[:, 4:5],
                                in1=pass_out[1][:, u, c].rearrange("p (b t) -> p b t", t=TF), op0=ALU.mult, op1=ALU.add)
                        empty(ins)
            stats = add_projection(1)

            layer_norm(5, stats)
            dve.wait_ge(xn_ready, 4 * TT)

            def scale_from(n, unit):
                b = take(dve, ("mxT", n))
                empty(dve.tensor_reduce(gmx[0:1, n:n + 1], b[0:1, 0:P], AX.X, ALU.max))
                b = take(dve, ("mxB", n))
                if unit is None:
                    empty(dve.tensor_scalar(qs[:, n, 0:1], b[:, 0:1], 1.0 / QA, TINY, ALU.mult, ALU.max))
                    emptied(dve, ("mxB", n))
                    link(dve.reciprocal(qs[:, n, 1:2], qs[:, n, 0:1]))
                else:
                    empty(dve.tensor_scalar(qs[:, n, 0:1], b[:, 0:1], unit, 1.0 / QA, ALU.mult, ALU.mult))
                    emptied(dve, ("mxB", n))
                    link(dve.tensor_scalar(qs[:, n, 0:1], qs[:, n, 0:1], TINY, None, ALU.max))
                    link(dve.reciprocal(qs[:, n, 1:2], qs[:, n, 0:1]))
                    link(dve.tensor_tensor(qs[:, n, 1:2], qs[:, n, 1:2], unit, ALU.mult))

            def scale(n):
                return qs[:, n, 0:1]

            def on_grid(v, n):
                return dve.tensor_scalar(v, v, qs[:, n, 1:2], MAGIC, ALU.mult, ALU.add)

            def integers(v):
                return dve.tensor_scalar(v, v, MAGIC, None, ALU.subtract)

            def part_maximum(n, v):
                return dve.tensor_reduce(part[:, n:n + 1], v, AX.X, ALU.max, apply_absolute_value=True)

            def maximum(n, cols_):
                dve.tensor_reduce(mx[:, n:n + 1], part[:, 0:cols_], AX.X, ALU.max).then_inc(mx_ready, 1)

            xf = xn.rearrange("p t n -> p (t n)")
            dve.tensor_reduce(mx[:, 0:1], xf, AX.X, ALU.max, apply_absolute_value=True).then_inc(mx_ready, 1)
            scale_from(0, None)
            link(on_grid(xf, 0))
            for t in range(TT):
                integers(xn[:, t, :]).then_inc(xn_ready, 1)

            def bank_maxima(w, buf, o):
                for c in range(2):
                    emptied(dve, (w, o, c))
                    ins = part_maximum(2 * o + c, buf[:, o * NP + c * HP:o * NP + (c + 1) * HP])
                return ins

            def thirds(v):
                return [v[:, n * FC * NP // 3:(n + 1) * FC * NP // 3] for n in range(3)]

            for o in range(FC):
                ins = bank_maxima("ga", gate, o)
            link(ins)
            maximum(1, 2 * FC)
            scale_from(1, scale(0))
            link(on_grid(gate, 1))
            for v in thirds(gate):
                integers(v).then_inc(gate_ready, 1)
            dve.tensor_tensor(qs[:, 5, 0:1], scale(1), two_16[:, :], ALU.mult)
            dve.tensor_tensor(qs[:, 5, 1:2], scale(1), two_16[:, :], ALU.mult)
            for o in range(0, FC - 2):
                bank_maxima("up", up, o)
            for n, (s_, g_) in enumerate(zip(thirds(sig), thirds(gate))):
                dve.wait_ge(sig_done, n + 1)
                link(dve.tensor_scalar(s_, s_, 65536.0, MAGIC, ALU.mult, ALU.add))
                link(dve.tensor_scalar(s_, s_, MAGIC, 65535.0, ALU.subtract, ALU.min))
                dve.tensor_tensor(s_, s_, g_, ALU.mult).then_inc(silu_ready, 1)
            for o in range(FC - 2, FC):
                ins = bank_maxima("up", up, o)
            link(ins)
            maximum(2, 2 * FC)
            scale_from(2, scale(0))
            link(on_grid(up, 2))
            integers(up)
            dve.wait_ge(mx_ready, 3)
            dve.wait_ge(silu_ready, 3)
            for n, s_ in enumerate(thirds(sig)):
                ins = part_maximum(n, s_)
            link(ins)
            maximum(3, 3)
            scale_from(3, qs[:, 5, 0:1])
            link(on_grid(sig, 3))
            dve.tensor_tensor(qs[:, 5, 1:2], scale(3), scale(2), ALU.mult)
            dve.wait_ge(mx_ready, 4)
            for s_, u_, g_ in zip(thirds(sig), thirds(up), thirds(gate)):
                ins = dve.scalar_tensor_tensor(out=g_, in0=s_, scalar=MAGIC, in1=u_, op0=ALU.subtract, op1=ALU.mult)
            link(ins)
            for n, g_ in enumerate(thirds(gate)):
                ins = part_maximum(n, g_)
            link(ins)
            maximum(4, 3)
            scale_from(4, qs[:, 5, 1:2])
            link(on_grid(gate, 4))
            for t in range(TT):
                integers(gate.rearrange("p (o t) -> p o t", o=FC)[:, :, t * P:(t + 1) * P]).then_inc(o_ready, 1)
            for t in range(TT):
                n = rows_of(t)
                b = take(dve, ("dn", t))
                empty(dve.scalar_tensor_tensor(out=h[0:n, t, :], in0=b[0:n, 0:D], scalar=qs[0:n, 4, 0:1], in1=h[0:n, t, :],
                                               op0=ALU.mult, op1=ALU.add))

        @block.tensor
        def _(pe):
            at_fill = [0]

            def fill(key):
                n = FILL[key]
                assert n == at_fill[0], key
                at_fill[0] += 1
                if n >= 8:
                    emptied(pe, FILLS[n - 8][0])
                return banks[n % 8]

            def full(ins):
                ins.then_inc(bank_filled, 1)

            def product(out_, pairs):
                for n, (a_, b_) in enumerate(pairs):
                    ins = pe.matmul(out_, a_, b_, start=(n == 0), stop=(n == len(pairs) - 1))
                return ins

            pe.wait_ge(consts_ready, N_CONSTS)
            pe.wait_ge(derived_ready, 1)
            pp = patches[0:96, :].rearrange("p (w k n) -> p w k n", w=NG, k=6)
            for g in range(2):
                pe.wait_ge(patches_ready, g + 1)
                for k in range(6):
                    b = fill(("xp", k, g))
                    for w in range(3):
                        ins = pe.transpose(b[:, 96 * w:96 * w + 96], pp[:, 3 * g + w, k, :], ident[0:96, 0:96])
                    full(ins)
            pe.wait_ge(patch_w_in, 16 * NC)
            for j in range(3):
                b = fill(("y", j))
                for w in (2 * j, 2 * j + 1):
                    for k in range(6):
                        emptied(pe, ("xp", k, w // 3))
                    ins = product(b[0:96, (w % 2) * D:(w % 2 + 1) * D], [(patT[:, k, w, :], lin_w[:, k, :]) for k in range(6)])
                full(ins)
            pe.wait_ge(attn_w_in, 16 * N_ATTN_W)
            for n in ("q0", "o0", "q1", "k1", "v1", "o1"):
                b = fill(("wT", n))
                for k in range(KD):
                    for o in range(KD):
                        ins = pe.transpose(b[:, k * D + o * P:k * D + (o + 1) * P], raw[n][:, o, k * P:(k + 1) * P], ident[:, :])
                full(ins)
            b = fill(("wkvT",))
            for k in range(KD):
                ins = pe.transpose(b[:, 2 * HD * k:2 * HD * (k + 1)], raw_kv[0:2 * HD, k * P:(k + 1) * P], ident[0:2 * HD, 0:2 * HD])
            full(ins)
            ci = rep_i.rearrange("p h d -> p (h d)")
            cc_ = rep_c.rearrange("p h d -> p (h d)")
            mats = ((0, cc_), (1, cc_), (1, ci), (2, ci))
            pe.wait_ge(wl8_ready, 1)
            b = fill(("wl",))
            for m, (n, c_) in enumerate(mats):
                ins = product(b[:, m * P:(m + 1) * P], [(wl8[:, n, :, :].rearrange("p h d -> p (h d)"), c_)])
            full(ins)
            b = fill(("bl",))
            for m, (n, c_) in enumerate(mats):
                ins = product(b[:, m:m + 1], [(c_, blr[:, n:n + 1])])
            full(ins)

            def turn(n, ready):
                for j in range(3):
                    b = fill(("xT", n, j))
                    for t in range(2 * j, min(2 * j + 2, TT)):
                        pe.wait_ge(xn_ready, (ready - 1) * TT + t + 1)
                        for k in range(KD):
                            at_ = (t % 2) * D + k * P
                            ins = pe.transpose(b[:, at_:at_ + P], xn[:, t, k * P:(k + 1) * P], ident[:, :])
                    full(ins)

            def columns(key, w, cols_):
                b = fill(key)
                n = cols_.stop - cols_.start
                full(product(b[:, 0:n], [(w(k), xT[:, k, cols_]) for k in range(KD)]))

            def half_cols(c):
                return slice(c * CH, (c + 1) * CH)

            def values_turned(c):
                emptied(pe, ("v0", c))
                for j in range(2):
                    b = fill(("vb", c, j))
                    for n in range(4):
                        ins = pe.transpose(b[0:G3, n * P:(n + 1) * P],
                                           values3[:, c, 4 * j + n, :], ident[:, :])
                    full(ins)

            turn(0, 1)
            emptied(pe, ("wkvT",))
            emptied(pe, ("xT", 0, 2))
            for c in range(2):
                columns(("k0", c), lambda k: wkT[:, k, :], half_cols(c))
                columns(("v0", c), lambda k: wvT[:, k, :], half_cols(c))
                for hf in range(KD):
                    columns(("q0", hf, c), lambda k: wT["q0"][:, k, hf * P:(hf + 1) * P], half_cols(c))
            for c in range(2):
                values_turned(c)

            def attention():
                for s in range(B // 2 + 2):
                    if s < B // 2:
                        c = s // (CB // 2)
                        for hf in range(KD):
                            pe.wait_ge(keys_spread, c + 1)
                            emptied(pe, ("q0", hf, c))
                            b = fill(("S", s, hf))
                            for j in range(2):
                                im_ = 2 * s + j - c * CB
                                ins = product(b[64 * j:64 * j + 64, 0:KW],
                                              [(qsT[:, hf, c, im_ * T:im_ * T + 64],
                                                kexp[c][:, im_, :, :].rearrange("p h k -> p (h k)"))])
                            full(ins)
                    if 0 <= s - 1 < B // 2:
                        for hf in range(KD):
                            pe.wait_ge(exp_done, KD * (s - 1) + hf + 1)
                            b = fill(("PT", s - 1, hf))
                            for g, at_ in enumerate(GROUP_AT):
                                ins = pe.transpose(b[0:G3, g * P:(g + 1) * P],
                                                   probs[:, (s - 1) % 3, hf, at_ * T:at_ * T + G3], ident[:, :])
                            full(ins)
                    if 0 <= s - 2 < B // 2:
                        q = s - 2
                        c = q // (CB // 2)
                        b = fill(("PV", q))
                        for hf in range(KD):
                            emptied(pe, ("PT", q, hf))
                            emptied(pe, ("vb", c, 1))
                            for j in range(2):
                                im_ = 2 * q + j - c * CB
                                for g, (h0, h1) in enumerate(((0, 3), (3, 6), (6, 8))):
                                    lo = (hf * NH + h0) * VW
                                    ins = product(b[64 * j:64 * j + 64, lo:lo + (h1 - h0) * VW],
                                                  [(probsT[:, q % 2, hf, g * P + 64 * j:g * P + 64 * j + 64],
                                                    vals[c][0:G3, im_, h0:h1, :].rearrange("p h v -> p (h v)"))])
                        full(ins)

            def project(n, w):
                for j in range(3):
                    b = fill(("wo", n, j))
                    for t in range(2 * j, min(2 * j + 2, TT)):
                        rows = P if t < TT - 1 else LAST
                        ins = product(b[0:rows, (t % 2) * D:(t % 2 + 1) * D],
                                      [(attT[:, k, t * P:t * P + rows], w[:, k, :]) for k in range(KD)])
                    full(ins)

            attention()
            for p in range(B // 2):
                pe.wait_ge(regrouped_in[p], 32)
                b = fill(("AT", p))
                for k in range(KD):
                    ins = pe.transpose(b[:, k * P:(k + 1) * P], regrouped[:, p, k * P:(k + 1) * P], ident[:, :])
                full(ins)
            emptied(pe, ("AT", B // 2 - 1))
            project(0, wT["o0"])
            turn(1, 2)
            emptied(pe, ("xT", 1, 2))
            b = fill(("lg",))
            for t in range(TT):
                ins = product(b[:, t * NE:(t + 1) * NE], [(xT[:, k, t * P:(t + 1) * P], gate_w[:, k, :]) for k in range(KD)])
            full(ins)
            pe.wait_ge(moe_in, 16 * 8)

            def down(e):
                parts = [(e % 3, w_ed[:, e, :])] if e < NE else [(e % 3, w_sd[:, 0, :]), ((e + 1) % 3, w_sd[:, 1, :])]
                emptied(pe, ("u", e if e < NE else e + 1, 1))
                for j in range(3):
                    b = fill(("d", e, j))
                    for t in range(2 * j, min(2 * j + 2, TT)):
                        ins = product(b[:, (t % 2) * D:(t % 2 + 1) * D], [(hid[:, s_, t * P:(t + 1) * P], w) for s_, w in parts])
                    full(ins)

            for e in range(NX + 1):
                if e < NX:
                    for c in range(2):
                        cols_ = slice(c * HP, (c + 1) * HP)
                        if e < NE:
                            columns(("g", e, c), lambda k: w_eg[:, k, e, :], cols_)
                            columns(("u", e, c), lambda k: w_eu[:, k, e, :], cols_)
                        else:
                            part_ = slice((e - NE) * P, (e - NE + 1) * P)
                            columns(("g", e, c), lambda k: w_sg[:, k, part_], cols_)
                            columns(("u", e, c), lambda k: w_su[:, k, part_], cols_)
                if 1 <= e <= NE or e == NX:
                    down(min(e - 1, NE))
                if 1 <= e <= 9:
                    w, j = (e - 1) // 3, (e - 1) % 3
                    pe.wait_ge(fw_ready, w + 1)
                    b = fill(("fw", e - 1))
                    for x in range(2):
                        for o in range(2):
                            if w < 2:
                                src = fraw[w][:, (2 * j + o) * D + x * P:(2 * j + o) * D + (x + 1) * P]
                            else:
                                src = fraw[w][:, o * FI + (2 * j + x) * P:o * FI + (2 * j + x + 1) * P]
                            ins = pe.transpose(b[:, x * D + o * P:x * D + (o + 1) * P], src, ident[:, :])
                    full(ins)
            turn(2, 3)
            emptied(pe, ("xT", 2, 2))
            us = range(2)
            xf = xT[:, :, 0:NT].rearrange("p k (b t) -> p k b t", t=T)
            for w in ("k", "q", "v"):
                for u in us:
                    b = fill((w + "1", u))
                    for f in range(KD):
                        ins = product(b[:, f * P:(f + 1) * P].rearrange("p (b t) -> p b t", t=TF),
                                      [(wT[w + "1"][:, k, f * P:(f + 1) * P], xf[:, k, u * CB:(u + 1) * CB, 0:TF])
                                       for k in range(KD)])
                    full(ins)

            def head_product(key, m, src):
                b = fill(key)
                full(product(b[:, 0:CF], [(wlT[:, m, :], src[:, key[-1], :])]))

            def variance(key):
                emptied(pe, ("nc", *key))
                b = fill(("nv", *key))
                full(product(b[:, 0:CF], [(mean_m.rearrange("p h d -> p (h d)"), sqr[:, NORMS[key] % NR, :])]))

            def values_by_key(a, u, js):
                pe.wait_ge(fvals_spread, 2 * (a - 1) + u + 1)
                for j in js:
                    b = fill(("fvb", a, u, j))
                    for n in range(4):
                        ins = pe.transpose(b[:, n * P:(n + 1) * P], fvals[:, u, 4 * j + n, :, :].rearrange("p h k -> p (h k)"),
                                           ident[:, :])
                    full(ins)

            for w, m, src in (("k", 1, k_cur), ("q", 0, q_cur)):
                for u in us:
                    emptied(pe, (w + "1", u))
                    head_product(("nc", w, 1, u), m, src)
            for w in ("k", "q"):
                for u in us:
                    variance((w, 1, u))
            for u in us:
                emptied(pe, ("v1", u))
                head_product(("vr", 1, u), 3, v_cur)
            for u in us:
                head_product(("kr", 1, u), 2, k_cur)
            for a in (1, 2, 3):
                if a > 1:
                    for u in us:
                        emptied(pe, ("O", a - 1, u))
                        head_product(("nc", "q", a, u), 0, q_cur)
                    values_by_key(a, 0, (0, 1))
                    for u in us:
                        variance(("q", a, u))
                    values_by_key(a, 0, (2, 3))
                for u in us:
                    pe.wait_ge(fkeys_spread, 2 * (a - 1) + u + 1)
                    pe.wait_ge(normed, NORMS["q", a, u] + 1)
                    b = fill(("fS", a, u))
                    for im in range(CB):
                        g, n = im % 4, im // 4
                        ins = product(b[32 * g:32 * g + 32, n * P:(n + 1) * P],
                                      [(queries_n[:, u, 32 * m + TF * (1 - f):32 * m + TF * (1 - f) + 32],
                                        fkeys[:, u, m, :, :].rearrange("p h k -> p (h k)"))
                                       for f, m in ((0, im), (1, CB + im))])
                    full(ins)
                if a < 3:
                    for u in us:
                        emptied(pe, ("kr", a, u))
                        head_product(("nc", "k", a + 1, u), 1, k_cur)
                    if a < 2:
                        for u in us:
                            head_product(("kr", a + 1, u), 2, k_cur)
                    for u in us:
                        variance(("k", a + 1, u))
                else:
                    pe.wait_ge(df_ready, 1)
                    b = fill(("df",))
                    full(product(b[:, 0:1], [(ones[:, :], dfs[:, 0:1])]))
                if a == 1:
                    values_by_key(a, 0, range(4))
                values_by_key(a, 1, range(4))
                for u in us:
                    pe.wait_ge(fprobs_ready, 2 * (a - 1) + u + 1)
                    b = fill(("fPT", a, u))
                    for n in range(2):
                        ins = pe.transpose(b[:, n * P:(n + 1) * P], fprobs[:, u, n * P:(n + 1) * P], ident[:, :])
                    full(ins)
                if a < 3:
                    for u in us:
                        emptied(pe, ("vr", a, u))
                        head_product(("vr", a + 1, u), 3, v_cur)
                for u in us:
                    emptied(pe, ("fPT", a, u))
                    emptied(pe, ("fvb", a, u, 3))
                    b = fill(("O", a, u))
                    for f in range(KD):
                        for im in range(CB):
                            m = f * CB + im
                            at_ = (im // 4) * P + (im % 4) * 32 + f * TF
                            ins = product(b[:, m * TF:(m + 1) * TF], [(fvalsT[:, u, m, :], fprobsT[:, u, at_:at_ + TF])])
                    full(ins)
            emptied(pe, ("O", 3, 1))
            project(1, wT["o1"])

            def maximum(n):
                pe.wait_ge(mx_ready, n + 1)
                b = fill(("mxT", n))
                full(pe.transpose(b[0:1, 0:P], mx[:, n:n + 1], ident[:, :]))
                b = fill(("mxB", n))
                emptied(pe, ("mxT", n))
                full(product(b[:, 0:1], [(ones[0:1, :], gmx[0:1, n:n + 1])]))

            maximum(0)
            turn(3, 5)
            emptied(pe, ("xT", 3, 2))
            for n, w in enumerate(("ga", "up")):
                for o in range(FC):
                    for c in range(2):
                        columns((w, o, c), lambda k: fT[n][:, k, o * P:(o + 1) * P], slice(c * HP, (c + 1) * HP))
                    if (w, o) == ("up", 1):
                        maximum(1)
            for n in (2, 3, 4):
                maximum(n)
            for t in range(TT):
                pe.wait_ge(o_ready, t + 1)
                rows = P if t < TT - 1 else LAST
                b = fill(("dn", t))
                full(product(b[0:rows, 0:D], [(gate[:, o * NP + t * P:o * NP + t * P + rows], fT[2][:, o, :]) for o in range(FC)]))


_INS = ["x", "L0_tok_ln1_w", "L0_tok_ln1_b", "L0_tok_lin_w", "L0_tok_lin_b", "L0_tok_ln2_w", "L0_tok_ln2_b",
        "L0_tok_pos_embedding", "L0_tok_cls_token", "L0_attn_Wq", "L0_attn_bq", "L0_attn_Wkv", "L0_attn_bkv",
        "L0_attn_Wo", "L0_attn_bo", "L0_ffn_gate_w", "L0_ffn_gate_bias", "L0_ffn_w_gate", "L0_ffn_w_up",
        "L0_ffn_w_down", "L0_ffn_sw_gate", "L0_ffn_sw_up", "L0_ffn_sw_down", "L1_attn_Wq", "L1_attn_bq",
        "L1_attn_Wk", "L1_attn_Wv", "L1_attn_bv", "L1_attn_Wo", "L1_attn_bo", "L1_attn_lna_w", "L1_attn_lnc_w",
        "L1_attn_lnd_w", "L1_attn_Wlq", "L1_attn_blq", "L1_attn_Wlk", "L1_attn_blk", "L1_attn_Wlv", "L1_attn_blv",
        "L1_attn_temp", "L1_attn_threshold", "L1_attn_factor", "L1_ffn_w_gate", "L1_ffn_w_up", "L1_ffn_w_down"]


def kernel(**inputs):
    import numpy as _np
    import concourse.bacc as _bacc
    from concourse import mybir as _mybir
    from concourse.bass_utils import run_bass_kernel_spmd as _run

    nc = _bacc.Bacc("TRN2", target_bir_lowering=False, num_devices=1)
    arrays, args = {}, {}
    for name in _INS:
        a = _np.ascontiguousarray(inputs[name])
        if a.ndim == 0:
            a = a.reshape(1)
        arrays[f"in_{name}"] = a
        args[name] = nc.dram_tensor(f"in_{name}", a.shape, _mybir.dt.from_np(a.dtype), kind="ExternalInput").ap()
    out = nc.dram_tensor("out_tokens", (B, T, D), F32, kind="ExternalOutput").ap()
    build(nc, args, out)
    r = _run(nc, [arrays], core_ids=[0])
    return r.results[0]["out_tokens"]
```

```python
from contextlib import ExitStack

import concourse.bass as bass
from concourse import mybir

F32 = mybir.dt.float32
ALU = mybir.AluOpType
ACT = mybir.ActivationFunctionType
AX = mybir.AxisListType

P = 128
B = 16
NG = 6
T = NG * NG + 1
PS = 16
NC = 3
D = 256
KD = D // P
HD = 16
NH = 8
NT = B * T
TT = 5
LAST = NT - (TT - 1) * P
NP = TT * P
CB = B // 2
CH = CB * T
QW = CH + 28
KW = NH * T
VW = HD + 1
G3 = 3 * T
NE = 8
EI = 128
NX = NE + 2
FI = 768
FC = FI // P
BLK = 32
NB = D // BLK
EPS = 1e-5
SM = HD ** -0.5
MAGIC = 1.5 * 2.0 ** 23
QA = 32767.0
QWT = 7.0
TINY = 1e-12
HP = NT // 2
TF = 2 * NH
CF = B * TF
KSCALE = HD ** -0.25
GROUP_AT = (0, 3, 5)
N_CONSTS = 1
N_COLS = 2 * NC + 4 + 4 + 3
N_ATTN_W = 6 + 1 + 6 + 1


HEADS_FOR_TILES = (range(0, 4), range(4, 7), range(7, 8))
assert all(2 * T * (ps.stop) >= min(2 * P * (j + 1), NT) for j, ps in enumerate(HEADS_FOR_TILES))


def fills():
    f = []
    for t in range(TT):
        f.append((("ad", t), "act"))
    for g in range(2):
        for k in range(6):
            f.append((("xp", k, g), "act" if k % 2 else "dve"))
    for i in range(3):
        f.append((("y", i), "dve"))
    for n in ("q0", "o0", "q1", "k1", "v1", "o1"):
        f.append((("wT", n), "act"))
    f.append((("wkvT",), "act"))
    f.append((("wl",), "dve"))
    f.append((("bl",), "dve"))
    for i in range(3):
        f.append((("xT", 0, i), "act"))
    for c in range(2):
        f.append((("k0", c), "act"))
        f.append((("v0", c), "act"))
        for hf in range(KD):
            f.append((("q0", hf, c), "act"))
    for c in range(2):
        for j in range(2):
            f.append((("vb", c, j), "dve"))

    for s in range(B // 2 + 2):
        if s < B // 2:
            f.extend(((("S", s, hf), "dve") for hf in range(KD)))
        if 0 <= s - 1 < B // 2:
            f.extend(((("PT", s - 1, hf), "act") for hf in range(KD)))
        if 0 <= s - 2 < B // 2:
            f.append((("PV", s - 2), "dve"))
    for j, ps in enumerate(HEADS_FOR_TILES):
        f.extend((("AT", p), "act") for p in ps)
        f.append((("wo", 0, j), "dve"))
    f.extend((("fw", n), "act") for n in range(3))
    for i in range(3):
        f.append((("xT", 1, i), "act"))
    f.extend((("lg", c), "act") for c in range(2))
    f.append((("lgT",), "act"))
    for e in range(NX + 1):
        if e < NX:
            for c in range(2):
                f.append((("g", e, c), "act"))
                f.append((("u", e, c), "dve"))
        if 1 <= e <= NE or e == NX:
            for i in range(3):
                f.append((("d", min(e - 1, NE), i), "dve"))
    f.extend((("fw", n), "act") for n in range(6, 9))
    for i in range(3):
        f.append((("xT", 2, i), "act"))
    us = range(2)
    for w in ("k", "q"):
        f.extend(((w + "1", u), "act") for u in us)
    f.extend((("nc", "k", 1, u), "act") for u in us)
    f.extend((("nc", "q", 1, u), "act") for u in us)
    f.extend((("nv", "k", 1, u), "act") for u in us)
    f.extend((("nv", "q", 1, u), "act") for u in us)
    f.extend((("v1", u), "act") for u in us)
    f.extend((("vr", 1, u), "act") for u in us)
    f.extend((("kr", 1, u), "act") for u in us)
    for a in (1, 2, 3):
        if a > 1:
            f.extend((("nc", "q", a, u), "act") for u in us)
            f.extend((("fvb", a, 0, j), "dve") for j in range(2))
            f.extend((("nv", "q", a, u), "act") for u in us)
            f.extend((("fvb", a, 0, j), "dve") for j in range(2, 4))
        f.extend((("fS", a, u), "dve") for u in us)
        if a < 3:
            f.extend((("nc", "k", a + 1, u), "act") for u in us)
            if a < 2:
                f.extend((("kr", a + 1, u), "act") for u in us)
            f.extend((("nv", "k", a + 1, u), "act") for u in us)
        else:
            f.append((("df",), "dve"))
        if a == 1:
            f.extend((("fvb", a, 0, j), "dve") for j in range(4))
        f.extend((("fvb", a, 1, j), "act") for j in range(4))
        f.extend((("fPT", a, u), "act") for u in us)
        if a < 3:
            f.extend((("vr", a + 1, u), "act") for u in us)
        f.extend((("O", a, u), "act") for u in us)
        f.extend((("OT", a, u), "dve") for u in us)
    for i in range(3):
        f.append((("wo", 1, i), "dve"))
    f.extend((("fw", n), "act") for n in range(3, 6))
    f.extend(max_fills(0))
    for i in range(3):
        f.append((("xT", 3, i), "act"))
    for w in ("ga", "up"):
        for o in range(FC):
            for c in range(2):
                f.append(((w, o, c), "act"))
                if (w, o) == ("up", 0):
                    f.append((("mxT" if c == 0 else "mxB", 1), "dve"))
    f.extend(max_fills(2))
    f.extend(max_fills(3))
    f.extend(max_fills(4))
    for t in range(TT):
        f.append((("dn", t), "dve"))
    return f


def max_fills(n):
    return [(("mxT", n), "dve"), (("mxB", n), "dve")]


FILLS = fills()
FILL = {key: n for n, (key, _) in enumerate(FILLS)}
assert len(FILL) == len(FILLS)
NTH = {}
for _who in ("act", "dve"):
    for _n, _key in enumerate(k for k, w in FILLS if w == _who):
        NTH[_key] = (_who, _n + 1)
NORMS = {key[1:]: n for n, key in enumerate(k for k, _ in FILLS if k[0] == "nc")}


def build(nc, i, out):
    with ExitStack() as ctx:
        def sb(name, *shape):
            return ctx.enter_context(nc.sbuf_tensor(name, list(shape), F32))

        def sem(name):
            return ctx.enter_context(nc.semaphore(name))

        o_dram = nc.dram_tensor("o_scratch", (2, B // 2, T * D), F32).ap()

        QK = CB * KW
        QV = CB * NH * VW
        XI = NC * PS * NG * PS
        BIG = 2 * XI + 6 * NT + 6 * D
        big = sb("big", P, BIG)
        small = sb("small", P, 2 * QV + 3 * FC * D)
        kexp = [big[:, n * QK:(n + 1) * QK].rearrange("p (b h k) -> p b h k", b=CB, h=NH) for n in range(2)]
        vals = [small[:, n * QV:(n + 1) * QV].rearrange("p (b h v) -> p b h v", b=CB, h=NH) for n in range(2)]
        at = [0]

        def cut(region, n):
            at[0] += n
            return region[:, at[0] - n:at[0]]

        img = cut(big, XI)
        patches = cut(big, XI)
        patT = cut(big, 6 * NT).rearrange("p (k t) -> p k t", k=6)
        patT_bt = patT.rearrange("p k (b t) -> p k b t", t=T)
        lin_w = cut(big, 6 * D).rearrange("p (k n) -> p k n", k=6)
        at[0] = 2 * QK
        w_eg = cut(big, KD * NE * EI).rearrange("p (k e i) -> p k e i", k=KD, e=NE)
        w_eu = cut(big, KD * NE * EI).rearrange("p (k e i) -> p k e i", k=KD, e=NE)
        w_ed = cut(big, NE * D).rearrange("p (e n) -> p e n", e=NE)
        w_sg = cut(big, KD * D).rearrange("p (k i) -> p k i", k=KD)
        w_su = cut(big, KD * D).rearrange("p (k i) -> p k i", k=KD)
        w_sd = cut(big, KD * D).rearrange("p (k n) -> p k n", k=KD)
        assert at[0] <= BIG
        at[0] = 0
        fkeys = cut(big, KD * B * P).rearrange("p (u m h k) -> p u m h k", u=2, m=B, h=NH)
        fvals = cut(big, KD * B * P).rearrange("p (u m h k) -> p u m h k", u=2, m=B, h=NH)
        fvalsT = cut(big, KD * B * P).rearrange("p (u m n) -> p u m n", u=2, m=B)
        assert at[0] <= BIG
        at[0] = 0
        gate = cut(big, FC * NT)
        up = cut(big, FC * NT)
        sig = cut(big, FC * NT)
        at[0] = 0
        raw = {n: cut(small, KD * D).rearrange("p (o i) -> p o i", o=KD) for n in ("q0", "o0", "q1", "k1", "v1", "o1")}
        raw_kv = cut(small, D)
        at[0] = 2 * QV
        fraw = [cut(small, FC * D) for _ in range(3)]

        h = sb("h", P, TT, D)
        xn = sb("xn", P, TT, D)
        xT = sb("xT", P, KD, NP)
        att = sb("att", P, 2 * 3 * CH)
        attT = att[:, 0:KD * NP].rearrange("p (k t) -> p k t", k=KD)
        values3 = att[:, :].rearrange("p (n b m) -> p n b m", n=2, b=CB)
        wT = {n: sb("wT_" + n, P, KD, D) for n in raw}
        wkT = sb("wkT", P, KD, P)
        wvT = sb("wvT", P, KD, P)
        fT = [sb("fT0", P, KD, FI), sb("fT1", P, KD, FI), sb("fT2", P, FC, D)]
        qsT = sb("qsT", P, KD, 2, QW)
        cur = sb("cur", P, B // 2 * D)
        q_cur, k_cur, v_cur = (cur[:, n * KD * CF:(n + 1) * KD * CF].rearrange("p (k t) -> p k t", k=KD) for n in range(3))
        regrouped = cur[:, 0:B // 2 * D].rearrange("p (s n) -> p s n", n=D)
        hid = cur[:, 0:3 * NT].rearrange("p (n t) -> p n t", n=3)
        passes = sb("passes", P, NG * D)
        pass_out = [passes[:, n * KD * CF:(n + 1) * KD * CF].rearrange("p (k t) -> p k t", k=KD) for n in range(2)]
        addend = passes[:, 0:TT * (D + 1)].rearrange("p (t n) -> p t n", t=TT)
        keys_n = sb("keys_n", P, 2, CH)
        NR = 4
        cen_all = sb("cen", P, NR * CF)
        cen = cen_all[:, :].rearrange("p (n t) -> p n t", n=NR)
        silu = cen_all[:, 0:2 * HP].rearrange("p (c t) -> p c t", c=2)
        sqr_all = sb("sqr", P, NR * CF)
        sqr = sqr_all[:, :].rearrange("p (n t) -> p n t", n=NR)
        r_lin, r_ln2w, r_ln2b = (sqr_all[:, n * D:(n + 1) * D] for n in range(3))
        rsd_all = sb("rsd", P, NR * CF)
        rsd = rsd_all[:, :].rearrange("p (n t) -> p n t", n=NR)
        token_of = rsd_all[0:T, 0:NT].rearrange("p (b t) -> p b t", t=T)
        larger, equal = (rsd_all[:, n * TT * NE * NE:(n + 1) * TT * NE * NE].rearrange(
            "p (t i j) -> p t i j", t=TT, i=NE) for n in range(2))
        probs_all = sb("probs", P, 3 * KD * KW)
        probs = probs_all[:, :].rearrange("p (n k w) -> p n k w", n=3, k=KD)
        table = probs_all[0:T, 0:D + 1]
        r_cls = probs_all[0:T, 2 * D:3 * D]
        fprobs, fheads = (probs_all[:, n * 2 * CF:(n + 1) * 2 * CF].rearrange(
            "p (u t) -> p u t", u=2) for n in range(2))
        probsT = sb("probsT", G3, 2, KD, 3 * P)
        queries_n = sb("queries_n", P, 2, 2 * CF + TF)
        fprobsT = sb("fprobsT", P, 2, 2 * CF + TF)
        fmax = sb("fmax", P, 2, B)
        fsum = sb("fsum", P, 2, B)
        heads = sb("heads", P, 2, KD, NH, HD)
        head_max = sb("head_max", P, KD, NH)
        head_rec = sb("head_rec", P, KD, NH)
        ident = sb("ident", P, P)
        ones = sb("ones", P, P)
        head_of = sb("head_of", P, NH)
        key_of = sb("key_of", G3, NH)
        mean_m = sb("mean_m", P, NH, HD)
        rep_i = sb("rep_i", HD, NH, HD)
        rep_c = sb("rep_c", HD, NH, HD)
        low = sb("low", P, NE, NE)
        eps_c = sb("eps_c", P, 1)
        nhalf = sb("nhalf", P, 8)
        two_16 = sb("two_16", P, 1)
        magic_c = sb("magic_c", P, 2)
        wl = sb("wl", HD, 3, HD)
        wl8 = sb("wl8", HD, 3, NH, HD)
        blr = sb("blr", HD, 3)
        wlT = sb("wlT", P, 4, P)
        bl = sb("bl", P, 4)
        cols = sb("cols", P, 40)
        c_ln1w, c_ln1b = cols[:, 0:6], cols[:, 6:12]
        c_bq0, c_bq1, c_bv1, c_lna = cols[:, 12:14], cols[:, 14:16], cols[:, 16:18], cols[:, 18:20]
        c_bk0, c_bv0 = cols[:, 20:21], cols[:, 21:22]
        c_lnc, c_lnd, c_temp, c_thr, c_fac = (cols[:, n:n + 1] for n in range(22, 27))
        c_hbq1 = cols[:, 28:30]
        q_w = sb("q_w", P, 3)
        k_w = sb("k_w", P, NH)
        temps = sb("temps", P, 4, 3)
        r_bo = [sb("r_bo0", P, D), sb("r_bo1", P, D)]
        r_gb = sb("r_gb", P, NE)
        gate_w = sb("gate_w", P, KD, NE)
        st = sb("st", P, 18, 6)
        mv = sb("mv", P, NG, 2)
        var = sb("var", P, 8)
        rstd = sb("rstd", P, 8)
        masked = sb("masked", P, 8)
        first = sb("first", T, 2)
        root = sb("root", P, TT)
        root2 = sb("root2", P, TT)
        logits = probs_all[0:NE, 0:NP]
        sc = sb("sc", P, TT, NE)
        rt = sb("rt", P, 6, TT * NE)
        route = sb("route", P, TT, NE)
        bs = sb("bs", P, 3, FC * NB)
        bi = sb("bi", P, 3, FC * NB)
        mx = sb("mx", P, 8)
        gmx = sb("gmx", 1, 8)
        part = sb("part", P, 2 * FC)
        qs = sb("qs", P, 6, 2)
        dfs = sb("dfs", P, 8)

        banks = [ctx.enter_context(nc.psum_tensor(f"bank{n}", [P, 512], F32)) for n in range(8)]

        bank_filled = sem("bank_filled")
        emptied_by = {"act": sem("act_emptied"), "dve": sem("dve_emptied")}
        dve_chain, act_chain, pool_chain = sem("dve_chain"), sem("act_chain"), sem("pool_chain")
        images_in = [sem(f"images_in{n}") for n in range(NC)]
        (patch_w_in, cols_in, attn_w_in, rows_in, pos_in, moe_in, ffn_in, out_stored) = (
            sem(n) for n in ("patch_w_in", "cols_in", "attn_w_in", "rows_in", "pos_in", "moe_in", "ffn_in",
                             "out_stored"))
        o_stored = [sem(f"o_stored{n}") for n in range(B // 2)]
        regrouped_in = [sem(f"regrouped_in{n}") for n in range(3)]
        consts_ready = sem("consts_ready")
        var_ready = sem("var_ready")
        rstd_ready = sem("rstd_ready")
        patches_ready_pool = sem("patches_ready_pool")
        regrouped_cleared = sem("regrouped_cleared")
        patches_ready = sem("patches_ready")
        table_ready = sem("table_ready")
        xn_ready = sem("xn_ready")
        exp_done = sem("exp_done")
        root_done = sem("root_done")
        normed = sem("normed")
        keys_spread = sem("keys_spread")
        fkeys_spread = sem("fkeys_spread")
        fkeys_spread_dve = sem("fkeys_spread_dve")
        fvals_spread = sem("fvals_spread")
        attT_cleared = sem("attT_cleared")
        fexp_done = sem("fexp_done")
        fprobs_ready = sem("fprobs_ready")
        fw_ready = sem("fw_ready")
        mx_ready = sem("mx_ready")
        wl8_ready = sem("wl8_ready")
        gate_ready = sem("gate_ready")
        temps_ready = sem("temps_ready")
        temps_rooted = sem("temps_rooted")
        sig_done = sem("sig_done")
        product_ready = sem("product_ready")
        silu_start = sem("silu_start")
        up_on_grid = sem("up_on_grid")
        up_scaled = sem("up_scaled")
        silu_scaled = sem("silu_scaled")
        silu_on_grid = sem("silu_on_grid")
        silu_ready = sem("silu_ready")
        o_ready = sem("o_ready")
        df_ready = sem("df_ready")
        scales_in_use = sem("scales_in_use")

        def filled(eng, key):
            eng.wait_ge(bank_filled, FILL[key] + 1)

        def emptied(eng, key):
            who, nth = NTH[key]
            eng.wait_ge(emptied_by[who], nth)

        def bank_of(key):
            return banks[FILL[key] % 8]

        def take(eng, key):
            filled(eng, key)
            return bank_of(key)

        def patch_columns(k, g):
            return patT_bt[:, k, :, 1:T].rearrange("p b (g n) -> p n b g", n=NG)[:, 3 * g:3 * g + 3]

        def patches_turned(b):
            return b[:, 0:3 * 96].rearrange("p (n b g) -> p n b g", n=3, b=B)

        block = ctx.enter_context(nc.Block())

        @block.sync
        def _(sp):
            im = i["x"].rearrange("b c (g line) col -> c b g (line col)", g=NG)
            imv = img.rearrange("p (c n) -> p c n", c=NC)
            for c in range(NC):
                sp.dma_start(imv[0:96, c, :], im[c]).then_inc(images_in[c], 16)
            lw = i["L0_tok_lin_w"].rearrange("(k p c) n -> c p k n", k=2, p=P)
            for c in range(NC):
                sp.dma_start(lin_w[:, 2 * c:2 * c + 2, :], lw[c]).then_inc(patch_w_in, 16)
            for col, name in ((c_ln1w, "L0_tok_ln1_w"), (c_ln1b, "L0_tok_ln1_b")):
                v = i[name].rearrange("(k p c) -> c p k", k=2, p=P)
                for c in range(NC):
                    sp.dma_start(col[:, 2 * c:2 * c + 2], v[c], allow_slow_non_contiguous=True).then_inc(cols_in, 16)
            for col, name in ((c_bq0, "L0_attn_bq"), (c_bq1, "L1_attn_bq"), (c_bv1, "L1_attn_bv"), (c_lna, "L1_attn_lna_w")):
                sp.dma_start(col, i[name].rearrange("(k p) -> p k", k=KD), allow_slow_non_contiguous=True).then_inc(cols_in, 16)
            kv = i["L0_attn_bkv"]
            for col, v in ((c_bk0, kv[0:HD]), (c_bv0, kv[HD:2 * HD]), (c_lnc, i["L1_attn_lnc_w"]), (c_lnd, i["L1_attn_lnd_w"])):
                sp.dma_start(col, v.unsqueeze(0).to_broadcast([NH, HD]).unsqueeze(2)).then_inc(cols_in, 16)
            for col, name in ((c_temp, "L1_attn_temp"), (c_thr, "L1_attn_threshold"), (c_fac, "L1_attn_factor")):
                sp.dma_start(col, i[name].partition_broadcast(P)).then_inc(cols_in, 16)
            for col, name in ((r_lin, "L0_tok_lin_b"), (r_ln2w, "L0_tok_ln2_w"),
                              (r_bo[0], "L0_attn_bo"), (r_bo[1], "L1_attn_bo"), (r_gb, "L0_ffn_gate_bias")):
                sp.dma_start(col[:, :], i[name].partition_broadcast(P)).then_inc(rows_in, 16)
            filled(sp, ("bl",))
            for n, name in enumerate(("w_gate", "w_up")):
                sp.dma_start(fraw[n].rearrange("p (o i) -> p o i", o=FC),
                             i["L1_ffn_" + name].rearrange("(o p) i -> p o i", p=P)).then_inc(ffn_in, 16)
            sp.dma_start(fraw[2].rearrange("p (o i) -> p o i", o=KD),
                         i["L1_ffn_w_down"].rearrange("(o p) i -> p o i", p=P)).then_inc(ffn_in, 16)
            filled(sp, ("y", 2))
            for k in range(KD):
                rows = slice(k * P, (k + 1) * P)
                sp.dma_start(w_eg[:, k, :, :], i["L0_ffn_w_gate"][:, rows, :].rearrange("e p i -> p e i")).then_inc(moe_in, 16)
                sp.dma_start(w_eu[:, k, :, :], i["L0_ffn_w_up"][:, rows, :].rearrange("e p i -> p e i")).then_inc(moe_in, 16)
            sp.dma_start(w_ed, i["L0_ffn_w_down"].rearrange("e p n -> p e n")).then_inc(moe_in, 16)
            for dst, name in ((w_sg, "sw_gate"), (w_su, "sw_up"), (w_sd, "sw_down")):
                sp.dma_start(dst, i["L0_ffn_" + name].rearrange("(k p) n -> p k n", p=P)).then_inc(moe_in, 16)

            def regroup(j):
                ps = HEADS_FOR_TILES[j]
                for p in ps:
                    sp.wait_ge(o_stored[p], 32)
                sp.wait_ge(regrouped_cleared, 1)
                for n in range(2):
                    sp.dma_start(regrouped[64 * n:64 * n + T, ps.start:ps.stop, :].rearrange("p s (h d) -> p (s h) d", d=HD),
                                 o_dram[n, ps.start:ps.stop].rearrange("p (h t d) -> t (p h) d", t=T, d=HD)
                                 ).then_inc(regrouped_in[j], 16)

            for p in range(B // 2):
                emptied(sp, ("PV", p))
                for j in range(2):
                    sp.dma_start(o_dram[j, p].rearrange("(t n) -> t n", t=T),
                                 heads[64 * j:64 * j + T, p % 2, :, :, :].rearrange("p k h d -> p (k h d)")
                                 ).then_inc(o_stored[p], 16)
                for j in range(2):
                    if p == HEADS_FOR_TILES[j].stop:
                        regroup(j)
            regroup(2)
            ot = out.rearrange("b t n -> (b t) n")
            for t in range(TT):
                n = P if t < TT - 1 else LAST
                emptied(sp, ("dn", t))
                sp.dma_start(ot[t * P:t * P + n, :], h[0:n, t, :]).then_inc(out_stored, 16)
            sp.wait_ge(out_stored, 16 * TT)

        @block.gpsimd
        def _(pool):
            links = [0]

            def link(ins):
                links[0] += 1
                ins.then_inc(pool_chain, 1)
                pool.wait_ge(pool_chain, links[0])

            pool.memset(ident[:, :], 0.0)
            pool.memset(head_of[:, :], 1.0)
            pool.memset(key_of[:, :], 1.0)
            pool.memset(low[:, :, :], 1.0)
            pool.memset(ones[:, :], 1.0)
            pool.memset(eps_c[:, :], EPS)
            pool.memset(nhalf[:, :], -0.5)
            pool.memset(magic_c[:, 0:1], MAGIC)
            pool.memset(magic_c[:, 1:2], -MAGIC)
            link(pool.memset(two_16[:, :], 2.0 ** -16))
            pool.affine_select(out=ident[:, :], in_=ident[:, :], compare_op=ALU.not_equal, fill=1.0, base=0,
                               pattern=[[-1, P]], channel_multiplier=1)
            pool.affine_select(out=low[:, :, :], in_=low[:, :, :], compare_op=ALU.is_ge, fill=0.0, base=-1,
                               pattern=[[1, NE], [-1, NE]], channel_multiplier=0)
            pool.affine_select(out=head_of[:, :], in_=head_of[:, :], compare_op=ALU.is_ge, fill=0.0, base=0,
                               pattern=[[-HD, NH]], channel_multiplier=1)
            k6 = key_of[:, 0:6].rearrange("p (g j) -> p g j", g=2)
            link(pool.affine_select(out=k6, in_=k6, compare_op=ALU.is_ge, fill=0.0, base=0,
                                    pattern=[[0, 2], [-T, 3]], channel_multiplier=1))
            link(pool.affine_select(out=head_of[:, :], in_=head_of[:, :], compare_op=ALU.is_ge, fill=0.0, base=HD - 1,
                                    pattern=[[HD, NH]], channel_multiplier=-1))
            link(pool.affine_select(out=k6, in_=k6, compare_op=ALU.is_ge, fill=0.0, base=T - 1,
                                    pattern=[[0, 2], [T, 3]], channel_multiplier=-1))
            link(pool.affine_select(out=key_of[:, 6:8], in_=key_of[:, 6:8], compare_op=ALU.is_ge, fill=0.0, base=-T,
                                    pattern=[[-T, 2]], channel_multiplier=1))
            link(pool.affine_select(out=key_of[:, 6:8], in_=key_of[:, 6:8], compare_op=ALU.is_ge, fill=0.0, base=2 * T - 1,
                                    pattern=[[T, 2]], channel_multiplier=-1))
            pool.tensor_copy(token_of, ident[0:T, 0:T].unsqueeze(1).to_broadcast([T, B, T]))
            link(pool.memset(h[64:P, TT - 1, :], 0.0))
            pool.memset(patT_bt[:, :, :, 0], 0.0)
            pool.memset(qsT[:, :, :, CH:QW], 0.0)
            pool.memset(fprobsT[:, :, :], 0.0)
            pool.memset(queries_n[:, :, :], 0.0).then_inc(consts_ready, 1)
            roots = [0]

            def inverse_root(rows, cols):
                roots[0] += 1
                pool.wait_ge(var_ready, roots[0])
                pool.tensor_tensor(rstd[0:rows, cols], var[0:rows, cols], nhalf[0:rows, cols], ALU.pow).then_inc(rstd_ready, 1)

            inverse_root(96, slice(0, NG))
            pv = img[0:96, :].rearrange("p (c line n q) -> p c line n q", c=NC, line=PS, n=NG)
            po = patches[0:96, :].rearrange("p (n c line q) -> p n c line q", n=NG, c=NC, line=PS)
            pool.wait_ge(rstd_ready, 1)
            w = NG - 1
            for c in range(NC):
                ins = pool.tensor_scalar(po[:, w, c, :, :], pv[:, c, :, w, :], mv[0:96, w, 0:1], rstd[0:96, w:w + 1],
                                         ALU.subtract, ALU.mult)
            ins.then_inc(patches_ready_pool, 1)
            pool.memset(regrouped[:, :, :], 0.0).then_inc(regrouped_cleared, 1)
            for j in range(3):
                inverse_root(P if j < 2 else LAST, slice(2 * j, min(2 * j + 2, TT)))
            pool.wait_ge(temps_ready, 1)
            pool.tensor_tensor(temps[:, 0, :], temps[:, 3, :], nhalf[:, 0:3], ALU.pow).then_inc(temps_rooted, 1)
            inverse_root(P, slice(0, TT))

            def spread(dst, src, scale, by, heads_=range(NH)):
                for n in heads_:
                    ins = pool.tensor_scalar(dst[:, :, n, :], src, scale[:, n:n + 1], by, ALU.mult, ALU.mult)
                return ins

            for c in range(2):
                emptied(pool, ("k0", c))
                spread(kexp[c], keys_n[:, c, :].rearrange("p (b k) -> p b k", b=CB), head_of, SM).then_inc(keys_spread, 1)
            inverse_root(P, slice(0, TT))
            filled(pool, ("wo", 0, 2))
            pool.memset(att[:, 0:KD * NP], 0.0).then_inc(attT_cleared, 1)
            pool.wait_ge(var_ready, roots[0] + 1)
            link(pool.tensor_tensor(root[:, :], var[:, 0:TT], nhalf[:, 0:TT], ALU.pow))
            link(pool.tensor_tensor(root2[:, :], root[:, :], root[:, :], ALU.mult))
            link(pool.tensor_scalar(root2[:, :], root2[:, :], -EPS, 1.0 + EPS, ALU.mult, ALU.add))
            link(pool.tensor_tensor(root2[:, :], root2[:, :], nhalf[:, 0:TT], ALU.pow))
            pool.tensor_tensor(rstd[:, 0:TT], root[:, :], root2[:, :], ALU.mult).then_inc(rstd_ready, 1)
            pool.wait_ge(scales_in_use, 1)
            filled(pool, ("d", NE, 2))
            for a in (1, 2, 3):
                for u in range(2):
                    if a > 1:
                        filled(pool, ("fS", a - 1, u))
                    pool.wait_ge(normed, NORMS["k", a, u] + 1)
                    spread(fkeys[:, u], keys_n[:, u, 0:CF].rearrange("p (m k) -> p m k", m=B), k_w, 1.0,
                           range(NH // 2 if a == 1 else NH)).then_inc(fkeys_spread, 1)
                for u in range(2) if a == 1 else ():
                    emptied(pool, ("vr", a, u))
                    spread(fvals[:, u], v_cur[:, u, :].rearrange("p (m k) -> p m k", m=B), head_of,
                           1.0).then_inc(fvals_spread, 1)
            roots[0] += 1
            inverse_root(P, slice(0, TT))
            n = FC * NT // 3
            for m in range(2):
                pool.wait_ge(silu_start, m + 1)
                v = slice(m * n, (m + 1) * n)
                pool.tensor_tensor(sig[:, v], sig[:, v], gate[:, v], ALU.mult).then_inc(silu_ready, 1)
            pool.wait_ge(silu_on_grid, 1)
            pool.wait_ge(up_on_grid, 1)
            pool.tensor_tensor(gate[:, 0:n], sig[:, 0:n], up[:, 0:n], ALU.mult).then_inc(product_ready, 1)

        @block.scalar
        def _(act):
            links = [0]

            def link(ins):
                links[0] += 1
                ins.then_inc(act_chain, 1)
                act.wait_ge(act_chain, links[0])

            def empty(ins):
                ins.then_inc(emptied_by["act"], 1)

            act.dma_start(table[:, 0:D], i["L0_tok_pos_embedding"][0, :, :]).then_inc(pos_in, 16)
            act.dma_start(r_cls, i["L0_tok_cls_token"][0, 0, :].partition_broadcast(T)).then_inc(pos_in, 16)
            act.dma_start(r_ln2b[0:T, :], i["L0_tok_ln2_b"].partition_broadcast(T)).then_inc(pos_in, 16)
            for name, arg in (("q0", "L0_attn_Wq"), ("o0", "L0_attn_Wo"), ("q1", "L1_attn_Wq"),
                              ("k1", "L1_attn_Wk"), ("v1", "L1_attn_Wv"), ("o1", "L1_attn_Wo")):
                act.dma_start(raw[name], i[arg].rearrange("(o p) i -> p o i", p=P)).then_inc(attn_w_in, 16)
            act.dma_start(raw_kv[0:2 * HD, :], i["L0_attn_Wkv"]).then_inc(attn_w_in, 16)
            for n, name in enumerate(("lq", "lk", "lv")):
                act.dma_start(wl[:, n, :], i["L1_attn_W" + name]).then_inc(attn_w_in, 16)
                act.dma_start(blr[:, n:n + 1], i["L1_attn_b" + name].unsqueeze(1), allow_slow_non_contiguous=True).then_inc(attn_w_in, 16)
            act.dma_start(gate_w[:, :, :], i["L0_ffn_gate_w"].rearrange("(k p) e -> p k e", p=P)).then_inc(attn_w_in, 16)
            for t in range(TT):
                n = P if t < TT - 1 else LAST
                b = take(act, ("ad", t))
                empty(act.copy(addend[0:n, t, :], b[0:n, 0:D + 1]))
            act.wait_ge(cols_in, 16 * N_COLS)
            for g in range(2):
                for k in range(1, 6, 2):
                    b = take(act, ("xp", k, g))
                    empty(act.activation(patch_columns(k, g), patches_turned(b),
                                         ACT.Identity, scale=c_ln1w[:, k:k + 1], bias=c_ln1b[:, k:k + 1]))

            for n in ("q0", "o0", "q1", "k1", "v1", "o1"):
                b = take(act, ("wT", n))
                empty(act.copy(wT[n].rearrange("p k o -> p (k o)"), b[:, :]))
            b = take(act, ("wkvT",))[:, 0:4 * HD].rearrange("p (k n) -> p k n", k=KD)
            for n, dst in enumerate((wkT, wvT)):
                for k in range(KD):
                    ins = act.copy(dst[:, k, :].rearrange("p (r d) -> p r d", d=HD),
                                   b[:, k, n * HD:(n + 1) * HD].unsqueeze(1).to_broadcast([P, NH, HD]))
            empty(ins)

            def turned(n, scales=None):
                for j in range(3):
                    b = take(act, ("xT", n, j))
                    tiles = 2 if j < 2 else 1
                    for k in range(KD):
                        dst = xT[:, k, 2 * j * P:(2 * j + tiles) * P].rearrange("p (t c) -> p t c", c=P)
                        src = b[:, 0:tiles * D].rearrange("p (t k c) -> p t k c", k=KD, c=P)[:, :, k, :]
                        if scales is None:
                            ins = act.copy(dst, src)
                        else:
                            ins = act.mul(dst, src, scales[:, k:k + 1])
                    empty(ins)

            def three_times(b, bias, c):
                for r in range(3):
                    ins = act.activation(values3[:, c, :, r * T:(r + 1) * T],
                                         b[:, 0:CH].rearrange("p (b k) -> p b k", b=CB), ACT.Identity, bias=bias)
                empty(ins)

            turned(0)
            for c in range(2):
                b = take(act, ("k0", c))
                empty(act.activation(keys_n[:, c, :], b[:, 0:CH], ACT.Identity, bias=c_bk0))
                b = take(act, ("v0", c))
                three_times(b, c_bv0, c)
                for hf in range(KD):
                    b = take(act, ("q0", hf, c))
                    if (hf, c) == (0, 0):
                        act.wait_ge(consts_ready, N_CONSTS)
                    empty(act.activation(qsT[:, hf, c, 0:CH], b[:, 0:CH], ACT.Identity, bias=c_bq0[:, hf:hf + 1]))

            def exps(s):
                for hf in range(KD):
                    emptied(act, ("S", s, hf))
                    v = probs[:, s % 3, hf, :]
                    act.activation(v, v, ACT.Exp).then_inc(exp_done, 1)

            def probs_turned(s):
                if s >= 2:
                    filled(act, ("PV", s - 2))
                for hf in range(KD):
                    b = take(act, ("PT", s, hf))
                    empty(act.copy(probsT[:, s % 2, hf, :], b[0:G3, 0:3 * P]))

            def centred(key):
                r = NORMS[key]
                which = key[0]
                if r >= NR:
                    act.wait_ge(normed, r - NR + 1)
                b = take(act, ("nc", *key))
                bias = bl[:, 0:1] if which == "q" else bl[:, 1:2]
                act.activation(cen[:, r % NR, :], b[:, 0:CF], ACT.Identity, bias=bias)
                empty(act.activation(sqr[:, r % NR, :], b[:, 0:CF], ACT.Square, bias=bias))

            def inverse_root(key):
                r = NORMS[key]
                b = take(act, ("nv", *key))
                v = rsd[:, r % NR, :]
                ins = act.activation(v, b[:, 0:CF], ACT.Ln, bias=eps_c[:, 0:1])
                empty(ins)
                emptied(act, ("nv", *key))
                act.activation(v, v, ACT.Exp, scale=-0.5).then_inc(root_done, 1)

            for s in range(B // 2 + 1):
                if s < B // 2:
                    exps(s)
                if s:
                    probs_turned(s - 1)

            def weight_turned(n):
                w, j = n // 3, n % 3
                b = take(act, ("fw", n))
                if w < 2:
                    empty(act.copy(fT[w][:, :, j * D:(j + 1) * D], b[:, :].rearrange("p (k o) -> p k o", k=KD)))
                else:
                    empty(act.copy(fT[2][:, 2 * j:2 * j + 2, :], b[:, :].rearrange("p (c o) -> p c o", c=2)))

            for p in range(B // 2):
                b = take(act, ("AT", p))
                empty(act.copy(attT[:, :, 2 * T * p:2 * T * (p + 1)].rearrange("p k (j t) -> p k j t", j=2),
                               b[:, 0:2 * P].rearrange("p (k j t) -> p k j t", k=KD, j=2)[:, :, :, 0:T]))
            for n in range(3):
                weight_turned(n)
            turned(1)
            for c in range(2):
                b = take(act, ("lg", c))
                empty(act.copy(logits[:, c * NP // 2:(c + 1) * NP // 2], b[0:NE, 0:NP // 2]))
            b = take(act, ("lgT",))
            empty(act.activation(sc.rearrange("p t e -> p (t e)"), b[:, 0:TT * NE], ACT.Sigmoid))
            for e in range(NX + 1):
                if e < NX:
                    for c in range(2):
                        b = take(act, ("g", e, c))
                        if e:
                            emptied(act, ("u", e - 1, c))
                        empty(act.activation(silu[:, c, :], b[:, 0:HP], ACT.Silu))
            for n in range(6, 9):
                weight_turned(n)
            turned(2, c_lna)
            act.wait_ge(scales_in_use, 1)
            us = range(2)

            def projected(w, dst):
                for u in us:
                    b = take(act, (w + "1", u))[:, 0:CF]
                    if w == "k":
                        empty(act.mul(dst[:, u, :], b, KSCALE))
                        continue
                    for f in range(KD):
                        c = slice(f * P, (f + 1) * P)
                        if w == "q":
                            ins = act.activation(dst[:, u, c], b[:, c], ACT.Identity, scale=KSCALE, bias=c_hbq1[:, f:f + 1])
                        else:
                            ins = act.activation(dst[:, u, c], b[:, c], ACT.Identity, bias=c_bv1[:, f:f + 1])
                    empty(ins)

            def refreshed(which, a, u):
                dst, m = (k_cur, 2) if which == "kr" else (v_cur, 3)
                if which == "vr" and a > 1:
                    act.wait_ge(fvals_spread, 2 * (a - 2) + u + 1)
                b = take(act, (which, a, u))
                empty(act.activation(dst[:, u, :], b[:, 0:CF], ACT.Identity, bias=bl[:, m:m + 1]))

            projected("k", k_cur)
            projected("q", q_cur)

            def turned_values(a, u, js):
                for j in js:
                    if a > 1:
                        filled(act, ("O", a - 1, u))
                    b = take(act, ("fvb", a, u, j))
                    empty(act.copy(fvalsT[:, u, 4 * j:4 * j + 4, :].rearrange("p m n -> p (m n)"), b[:, :]))

            act.preload_act_table_set("natural_log_exp_and_others")
            for w in ("k", "q"):
                for u in us:
                    centred((w, 1, u))
            for w in ("k", "q"):
                for u in us:
                    inverse_root((w, 1, u))
            projected("v", v_cur)
            for w in ("vr", "kr"):
                for u in us:
                    refreshed(w, 1, u)
            for a in (1, 2, 3):
                if a > 1:
                    for u in us:
                        centred(("q", a, u))
                    for u in us:
                        inverse_root(("q", a, u))
                if a < 3:
                    for u in us:
                        centred(("k", a + 1, u))
                for u in us:
                    emptied(act, ("fS", a, u))
                    act.activation(fprobs[:, u, :], fprobs[:, u, :], ACT.Exp).then_inc(fexp_done, 1)
                if a < 2:
                    for u in us:
                        refreshed("kr", a + 1, u)
                if a < 3:
                    for u in us:
                        inverse_root(("k", a + 1, u))
                turned_values(a, 1, range(4))
                for u in us:
                    if a > 1:
                        filled(act, ("O", a - 1, u))
                    b = take(act, ("fPT", a, u))
                    for f in range(KD):
                        ins = act.copy(fprobsT[:, u, TF + f * CF:TF + (f + 1) * CF].rearrange("p (b c) -> p b c", b=CB)[:, :, 0:TF],
                                       b[:, 0:CF].rearrange("p (b f t) -> p b f t", b=CB, f=KD)[:, :, f, :])
                    empty(ins)
                if a < 3:
                    for u in us:
                        refreshed("vr", a + 1, u)
                for u in us:
                    if a > 1:
                        filled(act, ("OT", a - 1, u))
                    b = take(act, ("O", a, u))
                    empty(act.copy(fheads[:, u, :], b[:, 0:CF]))
            for n in range(3, 6):
                weight_turned(n)
            turned(3)
            for w, dst in (("ga", gate), ("up", up)):
                for o in range(FC):
                    for c in range(2):
                        b = take(act, (w, o, c))
                        empty(act.copy(dst[:, o * NT + c * HP:o * NT + (c + 1) * HP], b[:, 0:HP]))
                    if w == "up" and o % 2:
                        n = slice((o // 2) * FC * NT // 3, (o // 2 + 1) * FC * NT // 3)
                        act.wait_ge(gate_ready, o // 2 + 1)
                        link(act.activation(sig[:, n], gate[:, n], ACT.Sigmoid, scale=qs[:, 1, 0:1]))
                        act.activation(sig[:, n], sig[:, n], ACT.Identity, scale=65536.0,
                                       bias=magic_c[:, 0:1]).then_inc(sig_done, 1)

            act.wait_ge(up_scaled, 1)
            for n in range(3):
                v = up[:, n * FC * NT // 3:(n + 1) * FC * NT // 3]
                link(act.activation(v, v, ACT.Identity, scale=qs[:, 2, 1:2], bias=magic_c[:, 0:1]))
                act.activation(v, v, ACT.Identity, bias=magic_c[:, 1:2]).then_inc(up_on_grid, 1)
            act.wait_ge(silu_scaled, 1)
            v = sig[:, 0:FC * NT // 3]
            link(act.activation(v, v, ACT.Identity, scale=qs[:, 3, 1:2], bias=magic_c[:, 0:1]))
            act.activation(v, v, ACT.Identity, bias=magic_c[:, 1:2]).then_inc(silu_on_grid, 1)

        @block.vector
        def _(dve):
            links = [0]

            def link(ins):
                links[0] += 1
                ins.then_inc(dve_chain, 1)
                dve.wait_ge(dve_chain, links[0])

            def empty(ins):
                ins.then_inc(emptied_by["dve"], 1)

            def rows_of(t):
                return P if t < TT - 1 else LAST

            roots = [0]

            def variance_given(ins, between=None):
                roots[0] += 1
                ins.then_inc(var_ready, 1)
                if between:
                    between()
                dve.wait_ge(rstd_ready, roots[0])

            def make_table():
                dve.wait_ge(consts_ready, N_CONSTS)
                dve.wait_ge(pos_in, 48)
                dve.tensor_scalar(first[:, 1:2], ident[0:T, 0:1], -1.0, 1.0, ALU.mult, ALU.add)
                link(dve.tensor_copy(first[:, 0:1], ident[0:T, 0:1]))
                link(dve.scalar_tensor_tensor(out=table[:, 0:D], in0=r_cls, scalar=first[:, 0:1], in1=table[:, 0:D],
                                              op0=ALU.mult, op1=ALU.add))
                dve.tensor_copy(table[:, D:D + 1], first[:, 1:2])
                link(dve.scalar_tensor_tensor(out=table[:, 0:D], in0=r_ln2b[0:T, :], scalar=first[:, 1:2],
                                              in1=table[:, 0:D], op0=ALU.mult, op1=ALU.add))
                dve.tensor_copy(first[:, 0:1], ident[0:T, 0:1]).then_inc(table_ready, 1)

            def statistics(ts):
                for t in ts:
                    ins = dve.bn_stats(st[:, t, :], h[:, t, :])
                return ins

            def layer_norm(n, stats):
                link(stats)
                for t in range(TT):
                    ins = dve.bn_aggr(mv[:, t, :], st[:, t, :])
                link(ins)
                if n > 2:
                    dve.wait_ge(xn_ready, (n - 2) * TT)
                variance_given(dve.tensor_scalar(var[:, 0:TT], mv[:, 0:TT, 1], EPS, None, ALU.add))
                for t in range(TT):
                    dve.tensor_scalar(xn[:, t, :], h[:, t, :], mv[:, t, 0:1], rstd[:, t:t + 1],
                                      ALU.subtract, ALU.mult).then_inc(xn_ready, 1)

            def tiles_of(j):
                return range(2 * j, min(2 * j + 2, TT))

            pv = img[0:96, :].rearrange("p (c line n q) -> p c line n q", c=NC, line=PS, n=NG)
            for c in range(NC):
                dve.wait_ge(images_in[c], 16)
                for w in range(NG):
                    ins = dve.bn_stats(st[0:96, 3 * w + c, :], pv[:, c, :, w, :])
            link(ins)
            for w in range(NG):
                ins = dve.bn_aggr(mv[0:96, w, :], st[0:96, 3 * w:3 * w + 3, :].rearrange("p a b -> p (a b)"))
            link(ins)
            variance_given(dve.tensor_scalar(var[0:96, 0:NG], mv[0:96, :, 1], EPS, None, ALU.add), make_table)
            po = patches[0:96, :].rearrange("p (n c line q) -> p n c line q", n=NG, c=NC, line=PS)
            for w in range(NG - 1):
                for c in range(NC):
                    ins = dve.tensor_scalar(po[:, w, c, :, :], pv[:, c, :, w, :], mv[0:96, w, 0:1], rstd[0:96, w:w + 1],
                                            ALU.subtract, ALU.mult)
                if w in (NG // 2 - 1, NG - 2):
                    ins.then_inc(patches_ready, 1)
            dve.wait_ge(consts_ready, N_CONSTS)
            dve.tensor_scalar(mean_m[:, :, :], head_of[:, :].unsqueeze(2).to_broadcast([P, NH, HD]), 1.0 / HD, None, ALU.mult)
            id16 = ident[0:HD, 0:HD].unsqueeze(1).to_broadcast([HD, NH, HD])
            dve.tensor_scalar(rep_i[:, :, :], id16, 0.0, None, ALU.add)
            dve.tensor_scalar(rep_c[:, :, :], id16, -1.0 / HD, None, ALU.add)
            dve.wait_ge(cols_in, 16 * N_COLS)
            for n in range(3):
                ins = dve.tensor_scalar(temps[:, 0, n:n + 1], c_temp, 0.005 * n, None, ALU.add)
            link(ins)
            dve.tensor_scalar(temps[:, 1, :], temps[:, 0, :], 0.0, None, ALU.is_gt)
            link(dve.tensor_scalar(temps[:, 2, :], temps[:, 0, :], 1.0, None, ALU.not_equal))
            dve.tensor_scalar(temps[:, 3, :], temps[:, 0, :], 1e-37, None, ALU.max).then_inc(temps_ready, 1)
            for g in range(2):
                for k in range(0, 6, 2):
                    b = take(dve, ("xp", k, g))
                    empty(dve.tensor_scalar(patch_columns(k, g), patches_turned(b),
                                            c_ln1w[:, k:k + 1], c_ln1b[:, k:k + 1], ALU.mult, ALU.add))
            dve.wait_ge(rows_in, 16 * 5)
            dve.wait_ge(attn_w_in, 16 * N_ATTN_W)
            dve.tensor_copy(wl8[:, :, :, :], wl[:, :, :].unsqueeze(2).to_broadcast([HD, 3, NH, HD])).then_inc(wl8_ready, 1)
            for j in range(3):
                b = take(dve, ("y", j))
                n, ts = (P if j < 2 else LAST), tiles_of(j)
                cs = slice(ts.start, ts.stop)
                v = h[0:n, cs, :]
                empty(dve.tensor_tensor(v, b[0:n, 0:len(ts) * D].rearrange("p (t n) -> p t n", t=len(ts)),
                                        r_lin[0:n, :].unsqueeze(1).to_broadcast([n, len(ts), D]), ALU.add))
                emptied(dve, ("y", j))
                for t in ts:
                    ins = dve.bn_stats(st[0:n, t, :], h[0:n, t, :])
                link(ins)
                for t in ts:
                    ins = dve.bn_aggr(mv[0:n, t, :], st[0:n, t, :])
                link(ins)
                variance_given(dve.tensor_scalar(var[0:n, cs], mv[0:n, cs, 1], EPS, None, ALU.add))
                emptied(dve, ("ad", ts[-1]))
                link(dve.tensor_tensor(masked[0:n, cs], rstd[0:n, cs], addend[0:n, cs, D], ALU.mult))
                for t in ts:
                    ins = dve.tensor_scalar(h[0:n, t, :], h[0:n, t, :], mv[0:n, t, 0:1], masked[0:n, t:t + 1],
                                            ALU.subtract, ALU.mult)
                link(ins)
                link(dve.tensor_tensor(v, v, r_ln2w[0:n, :].unsqueeze(1).to_broadcast([n, len(ts), D]), ALU.mult))
                link(dve.tensor_tensor(v, v, addend[0:n, cs, 0:D], ALU.add))
                stats = statistics(ts)
            layer_norm(2, stats)
            b = take(dve, ("wl",))
            empty(dve.tensor_tensor(wlT.rearrange("p m (h d) -> p m h d", h=NH),
                                    b[:, :].rearrange("p (m h d) -> p m h d", m=4, h=NH),
                                    head_of[:, :].unsqueeze(1).unsqueeze(3).to_broadcast([P, 4, NH, HD]), ALU.mult))
            b = take(dve, ("bl",))
            empty(dve.tensor_copy(bl[:, :], b[:, 0:4]))
            dve.wait_ge(temps_rooted, 1)
            link(dve.tensor_scalar(temps[:, 0, :], temps[:, 0, :], -1.0, None, ALU.add))
            link(dve.tensor_tensor(temps[:, 1, :], temps[:, 1, :], temps[:, 2, :], ALU.mult))
            link(dve.tensor_tensor(temps[:, 0, :], temps[:, 0, :], temps[:, 1, :], ALU.mult))
            dve.tensor_scalar(q_w[:, :], temps[:, 0, :], 1.0, c_lnc, ALU.add, ALU.mult)
            dve.tensor_scalar(k_w[:, :], head_of[:, :], c_lnd, SM, ALU.mult, ALU.mult)
            dve.tensor_scalar(c_hbq1, c_bq1, KSCALE, None, ALU.mult).then_inc(scales_in_use, 1)

            def add_projection(n):
                dve.wait_ge(xn_ready, TT * (1 if n == 0 else 3))
                dve.tensor_tensor(h[:, 0:TT - 1, :], h[:, 0:TT - 1, :],
                                  r_bo[n][:, :].unsqueeze(1).to_broadcast([P, TT - 1, D]), ALU.add)
                link(dve.tensor_tensor(h[0:LAST, TT - 1, :], h[0:LAST, TT - 1, :], r_bo[n][0:LAST, :], ALU.add))
                for j in range(3):
                    b = take(dve, ("wo", n, j))
                    if j < 2:
                        v = h[:, 2 * j:2 * j + 2, :]
                        empty(dve.tensor_tensor(v, b[:, :].rearrange("p (t n) -> p t n", t=2), v, ALU.add))
                    else:
                        v = h[0:LAST, TT - 1, :]
                        empty(dve.tensor_tensor(v, b[0:LAST, 0:D], v, ALU.add))
                    emptied(dve, ("wo", n, j))
                    ins = statistics(tiles_of(j))
                return ins

            def values_by_key(c):
                dve.tensor_copy(vals[c][0:G3, :, :, HD], key_of[:, :].unsqueeze(1).to_broadcast([G3, CB, NH]))
                for j in range(2):
                    b = take(dve, ("vb", c, j))
                    empty(dve.tensor_tensor(vals[c][0:G3, 4 * j:4 * j + 4, :, 0:HD],
                                            b[0:G3, :].rearrange("p (b h d) -> p b h d", b=4, h=NH),
                                            key_of[:, :].unsqueeze(1).unsqueeze(3).to_broadcast([G3, 4, NH, HD]), ALU.mult))

            def scores(s):
                for hf in range(KD):
                    if s >= 1:
                        emptied(dve, ("S", s - 1, hf))
                    if s >= 3:
                        filled(dve, ("PT", s - 3, hf))
                    b = take(dve, ("S", s, hf))[:, 0:KW].rearrange("p (h k) -> p h k", h=NH)
                    link(dve.tensor_reduce(head_max[:, hf, :], b, AX.X, ALU.max))
                    empty(dve.tensor_tensor(probs[:, s % 3, hf, :].rearrange("p (h k) -> p h k", h=NH), b,
                                            head_max[:, hf, :].unsqueeze(2).to_broadcast([P, NH, T]), ALU.subtract))

            def weighted(s):
                if s >= 2:
                    dve.wait_ge(o_stored[s - 2], 32)
                if s:
                    emptied(dve, ("PV", s - 1))
                b = take(dve, ("PV", s))[:, 0:KD * NH * VW].rearrange("p (k h v) -> p k h v", k=KD, h=NH)
                link(dve.reciprocal(head_rec[:, :, :], b[:, :, :, HD]))
                empty(dve.tensor_tensor(heads[:, s % 2, :, :, :], b[:, :, :, 0:HD],
                                        head_rec[:, :, :].unsqueeze(3).to_broadcast([P, KD, NH, HD]), ALU.mult))

            def normalised(key, dst, scale):
                r = NORMS[key]
                dve.wait_ge(root_done, r + 1)
                dve.scalar_tensor_tensor(out=dst, in0=cen[:, r % NR, :].rearrange("p (m t) -> p m t", t=TF), scalar=scale,
                                         in1=rsd[:, r % NR, :].rearrange("p (m t) -> p m t", t=TF),
                                         op0=ALU.mult, op1=ALU.mult).then_inc(normed, 1)

            def normalised_keys(a, u):
                if a > 1:
                    dve.wait_ge(fkeys_spread, 2 * (a - 2) + u + 1)
                normalised(("k", a, u), keys_n[:, u, 0:CF].rearrange("p (m t) -> p m t", t=TF), 1.0)

            def normalised_queries(a, u):
                if a > 1:
                    filled(dve, ("fS", a - 1, u))
                normalised(("q", a, u), queries_n[:, u, TF:].rearrange("p (m t) -> p m t", t=2 * TF)[:, :, 0:TF],
                           q_w[:, a - 1:a])

            for c in range(2):
                values_by_key(c)
            for s in range(B // 2 + 2):
                if s < B // 2:
                    scores(s)
                if s >= 2:
                    weighted(s - 2)

            def dequantise(w):
                v = fraw[w].rearrange("p (n k) -> p n k", k=BLK)
                s_ = bs[:, w, :].unsqueeze(2).to_broadcast([P, FC * NB, BLK])
                i_ = bi[:, w, :].unsqueeze(2).to_broadcast([P, FC * NB, BLK])
                link(dve.tensor_reduce(bs[:, w, :], v, AX.X, ALU.max, apply_absolute_value=True))
                link(dve.tensor_scalar(bs[:, w, :], bs[:, w, :], 1.0 / QWT, TINY, ALU.mult, ALU.max))
                link(dve.reciprocal(bi[:, w, :], bs[:, w, :]))
                link(dve.tensor_tensor(v, v, i_, ALU.mult))
                link(dve.tensor_scalar(fraw[w], fraw[w], MAGIC, MAGIC, ALU.add, ALU.subtract))
                dve.tensor_tensor(v, v, s_, ALU.mult).then_inc(fw_ready, 1)

            dve.wait_ge(ffn_in, 48)
            dequantise(0)
            stats = add_projection(0)

            layer_norm(3, stats)
            emptied(dve, ("lgT",))
            sfc = rt[:, 0, :].rearrange("p (t e) -> p t e", t=TT)
            grp = rt[:, 1, 0:TT * 4].rearrange("p (t g) -> p t g", t=TT)
            grk = rt[:, 2, 0:TT * 4].rearrange("p (t g) -> p t g", t=TT)
            tmp = rt[:, 3, :].rearrange("p (t e) -> p t e", t=TT)
            erk = rt[:, 4, :].rearrange("p (t e) -> p t e", t=TT)
            den = rt[:, 5, 0:TT]

            def top2(values, rank, n):
                other = values.unsqueeze(2).to_broadcast([P, TT, n, n])
                own = values.unsqueeze(3).to_broadcast([P, TT, n, n])
                ga, gb = larger[:, :, 0:n, 0:n], equal[:, :, 0:n, 0:n]
                dve.tensor_tensor(ga, other, own, ALU.is_gt)
                link(dve.tensor_tensor(gb, other, own, ALU.is_equal))
                link(dve.tensor_tensor(gb, gb, low[:, 0:n, 0:n].unsqueeze(1).to_broadcast([P, TT, n, n]), ALU.mult))
                link(dve.tensor_tensor(ga, ga, gb, ALU.add))
                link(dve.tensor_reduce(rank, ga, AX.X, ALU.add))
                link(dve.tensor_scalar(rank, rank, 2.0, None, ALU.is_lt))

            link(dve.tensor_tensor(sfc, sc[:, :, :], r_gb[:, :].unsqueeze(1).to_broadcast([P, TT, NE]), ALU.add))
            pair = sfc.rearrange("p t (g j) -> p t g j", j=2)
            link(dve.tensor_tensor(grp, pair[:, :, :, 0], pair[:, :, :, 1], ALU.add))
            top2(grp, grk, 4)
            link(dve.tensor_tensor(tmp.rearrange("p t (g j) -> p t g j", j=2), pair,
                                   grk.unsqueeze(3).to_broadcast([P, TT, 4, 2]), ALU.mult))
            top2(tmp, erk, NE)
            link(dve.tensor_tensor(route[:, :, :], erk, sfc, ALU.mult))
            link(dve.tensor_reduce(den, route[:, :, :], AX.X, ALU.add))
            link(dve.tensor_scalar(den, den, 1e-20, None, ALU.add))
            link(dve.reciprocal(den, den))
            link(dve.tensor_tensor(route[:, :, :], route[:, :, :], den.unsqueeze(2).to_broadcast([P, TT, NE]), ALU.mult))
            link(dve.tensor_scalar(route[:, :, :], route[:, :, :], 2.5, None, ALU.mult))

            def hidden(e):
                for c in range(2):
                    emptied(dve, ("g", e, c))
                    if e >= 3:
                        filled(dve, ("d", e - 3, 2))
                    b = take(dve, ("u", e, c))
                    empty(dve.tensor_tensor(hid[:, e % 3, c * HP:(c + 1) * HP], silu[:, c, :], b[:, 0:HP], ALU.mult))

            def add_expert(e):
                for j in range(3):
                    if e:
                        emptied(dve, ("d", e - 1, j))
                    b = take(dve, ("d", e, j))
                    for t in range(2 * j, min(2 * j + 2, TT)):
                        n = rows_of(t)
                        v = h[0:n, t, :]
                        src = b[0:n, (t % 2) * D:(t % 2 + 1) * D]
                        if e < NE:
                            ins = dve.scalar_tensor_tensor(out=v, in0=src, scalar=route[0:n, t, e:e + 1], in1=v,
                                                           op0=ALU.mult, op1=ALU.add)
                        else:
                            ins = dve.tensor_tensor(v, src, v, ALU.add)
                    empty(ins)
                    if e == NE:
                        emptied(dve, ("d", e, j))
                        ins = statistics(tiles_of(j))
                return ins

            for e in range(NX + 1):
                if e < NX:
                    hidden(e)
                if 1 <= e <= NE or e == NX:
                    stats = add_expert(min(e - 1, NE))
                if e in (1, 4):
                    dequantise(1 if e == 1 else 2)
            layer_norm(4, stats)

            def convergence():
                b = take(dve, ("df",))
                empty(dve.tensor_scalar(dfs[:, 1:2], b[:, 0:1], 1.0 / (NT * D), None, ALU.mult))
                emptied(dve, ("df",))
                link(dve.tensor_scalar(dfs[:, 2:3], dfs[:, 1:2], c_fac, c_thr, ALU.mult, ALU.add))
                link(dve.tensor_tensor(dfs[:, 3:4], dfs[:, 1:2], dfs[:, 2:3], ALU.is_lt))
                dve.tensor_scalar(dfs[:, 4:5], dfs[:, 3:4], -1.0, 1.0, ALU.mult, ALU.add)
                link(dve.tensor_scalar(pass_out[1][:, :, :], pass_out[1][:, :, :], dfs[:, 3:4], None, ALU.mult))

            def turned_values(a, u, js):
                for j in js:
                    if a > 1:
                        filled(dve, ("O", a - 1, u))
                    b = take(dve, ("fvb", a, u, j))
                    empty(dve.tensor_copy(fvalsT[:, u, 4 * j:4 * j + 4, :].rearrange("p m n -> p (m n)"), b[:, :]))

            def spread_values(a, u):
                filled(dve, ("fvb", a - 1, u, 3))
                emptied(dve, ("vr", a, u))
                dve.tensor_tensor(fvals[:, u],
                                  v_cur[:, u, :].rearrange("p (m k) -> p m k", m=B).unsqueeze(2).to_broadcast([P, B, NH, TF]),
                                  head_of[:, :].unsqueeze(1).unsqueeze(3).to_broadcast([P, B, NH, TF]),
                                  ALU.mult).then_inc(fvals_spread, 1)

            us = range(2)
            filled(dve, ("d", NE, 2))
            for u in us:
                normalised_keys(1, u)
                dve.wait_ge(normed, NORMS["k", 1, u] + 1)
                upper = slice(NH // 2, NH)
                dve.tensor_tensor(fkeys[:, u, :, upper, :],
                                  keys_n[:, u, 0:CF].rearrange("p (m k) -> p m k", m=B).unsqueeze(2).to_broadcast([P, B, NH // 2, TF]),
                                  k_w[:, upper].unsqueeze(1).unsqueeze(3).to_broadcast([P, B, NH // 2, TF]),
                                  ALU.mult).then_inc(fkeys_spread_dve, 1)
            for u in us:
                normalised_queries(1, u)
            for a in (1, 2, 3):
                if a > 1:
                    turned_values(a, 0, (0, 1))
                    for u in us:
                        normalised_queries(a, u)
                    turned_values(a, 0, (2, 3))
                for u in us:
                    if a > 1:
                        filled(dve, ("fPT", a - 1, u))
                    b = take(dve, ("fS", a, u))[:, 0:CF].rearrange("p (n k) -> p n k", k=TF)
                    link(dve.tensor_reduce(fmax[:, u, :], b, AX.X, ALU.max))
                    empty(dve.tensor_tensor(fprobs[:, u, :].rearrange("p (n k) -> p n k", k=TF), b,
                                            fmax[:, u, :].unsqueeze(2).to_broadcast([P, B, TF]), ALU.subtract))
                if a == 3:
                    d = pass_out[0]
                    link(dve.tensor_tensor(d[:, :, :], pass_out[1][:, :, :], d[:, :, :], ALU.subtract))
                    dve.tensor_reduce(dfs[:, 0:1], d[:, :, :], AX.XY, ALU.add, apply_absolute_value=True).then_inc(df_ready, 1)
                for u in us:
                    dve.wait_ge(fexp_done, 2 * (a - 1) + u + 1)
                    v = fprobs[:, u, :].rearrange("p (n k) -> p n k", k=TF)
                    link(dve.tensor_reduce(fsum[:, u, :], v, AX.X, ALU.add))
                    link(dve.reciprocal(fsum[:, u, :], fsum[:, u, :]))
                    dve.tensor_tensor(v, v, fsum[:, u, :].unsqueeze(2).to_broadcast([P, B, TF]),
                                      ALU.mult).then_inc(fprobs_ready, 1)
                if a == 3:
                    convergence()
                if a == 1:
                    turned_values(a, 0, range(4))
                if a < 3:
                    for u in us:
                        normalised_keys(a + 1, u)
                    spread_values(a + 1, 0)
                for u in us:
                    b = take(dve, ("OT", a, u))[:, 0:CF].rearrange("p (b f t) -> p f b t", b=CB, f=KD)
                    if a < 3:
                        dve.tensor_copy(pass_out[a - 1][:, u, :].rearrange("p (f b t) -> p f b t", f=KD, b=CB), b)
                        q = q_cur[:, u, :].rearrange("p (f b t) -> p f b t", f=KD, b=CB)
                        empty(dve.tensor_tensor(q, b, q, ALU.add))
                    else:
                        dve.wait_ge(attT_cleared, 1)
                        for f in range(KD):
                            ins = dve.scalar_tensor_tensor(
                                out=attT[:, f, u * CH:(u + 1) * CH].rearrange("p (b t) -> p b t", t=T)[:, :, 0:TF],
                                in0=b[:, f], scalar=dfs[:, 4:5],
                                in1=pass_out[1][:, u, f * P:(f + 1) * P].rearrange("p (b t) -> p b t", t=TF),
                                op0=ALU.mult, op1=ALU.add)
                        empty(ins)
                if a < 3:
                    spread_values(a + 1, 1)
            stats = add_projection(1)

            layer_norm(5, stats)
            dve.wait_ge(xn_ready, 4 * TT)

            def scale_from(n, unit):
                b = take(dve, ("mxT", n))
                empty(dve.tensor_reduce(gmx[0:1, n:n + 1], b[0:1, 0:P], AX.X, ALU.max))
                b = take(dve, ("mxB", n))
                if unit is None:
                    empty(dve.tensor_scalar(qs[:, n, 0:1], b[:, 0:1], 1.0 / QA, TINY, ALU.mult, ALU.max))
                    emptied(dve, ("mxB", n))
                    return link(dve.reciprocal(qs[:, n, 1:2], qs[:, n, 0:1]))
                else:
                    empty(dve.tensor_scalar(qs[:, n, 0:1], b[:, 0:1], unit, 1.0 / QA, ALU.mult, ALU.mult))
                    emptied(dve, ("mxB", n))
                    link(dve.tensor_scalar(qs[:, n, 0:1], qs[:, n, 0:1], TINY, None, ALU.max))
                    link(dve.reciprocal(qs[:, n, 1:2], qs[:, n, 0:1]))
                    return dve.tensor_tensor(qs[:, n, 1:2], qs[:, n, 1:2], unit, ALU.mult)

            def scale(n):
                return qs[:, n, 0:1]

            def on_grid(v, n):
                return dve.tensor_scalar(v, v, qs[:, n, 1:2], MAGIC, ALU.mult, ALU.add)

            def integers(v):
                return dve.tensor_scalar(v, v, MAGIC, None, ALU.subtract)

            def part_maximum(n, v):
                return dve.tensor_reduce(part[:, n:n + 1], v, AX.X, ALU.max, apply_absolute_value=True)

            def maximum(n, cols_):
                dve.tensor_reduce(mx[:, n:n + 1], part[:, 0:cols_], AX.X, ALU.max).then_inc(mx_ready, 1)

            xf = xn.rearrange("p t n -> p (t n)")
            dve.tensor_reduce(mx[:, 0:1], xf, AX.X, ALU.max, apply_absolute_value=True).then_inc(mx_ready, 1)
            scale_from(0, None)
            link(on_grid(xf, 0))
            for t in range(TT):
                integers(xn[:, t, :]).then_inc(xn_ready, 1)

            def bank_maxima(w, buf, o):
                for c in range(2):
                    emptied(dve, (w, o, c))
                    ins = part_maximum(2 * o + c, buf[:, o * NT + c * HP:o * NT + (c + 1) * HP])
                return ins

            def thirds(v):
                return [v[:, n * FC * NT // 3:(n + 1) * FC * NT // 3] for n in range(3)]

            for o in range(FC):
                ins = bank_maxima("ga", gate, o)
            link(ins)
            maximum(1, 2 * FC)
            link(scale_from(1, scale(0)))
            link(on_grid(gate, 1))
            for v in thirds(gate):
                integers(v).then_inc(gate_ready, 1)
            dve.tensor_tensor(qs[:, 5, 0:1], scale(1), two_16[:, :], ALU.mult)
            dve.tensor_tensor(qs[:, 5, 1:2], scale(1), two_16[:, :], ALU.mult)
            for o in range(0, FC - 2):
                bank_maxima("up", up, o)
            for n, (s_, g_) in enumerate(zip(thirds(sig), thirds(gate))):
                dve.wait_ge(sig_done, n + 1)
                ins = dve.tensor_scalar(s_, s_, MAGIC, 65535.0, ALU.subtract, ALU.min)
                if n < 2:
                    ins.then_inc(silu_start, 1)
                if n == 0:
                    for o in range(FC - 2, FC):
                        ins = bank_maxima("up", up, o)
                    link(ins)
                    maximum(2, 2 * FC)
                if n == 2:
                    link(ins)
                    link(dve.tensor_tensor(s_, s_, g_, ALU.mult))
                if n == 1:
                    scale_from(2, scale(0)).then_inc(up_scaled, 1)
            for n in (2, 0, 1):
                if n < 2:
                    dve.wait_ge(silu_ready, n + 1)
                ins = part_maximum(n, thirds(sig)[n])
            link(ins)
            maximum(3, 3)
            scale_from(3, qs[:, 5, 0:1]).then_inc(silu_scaled, 1)
            dve.wait_ge(silu_scaled, 1)
            link(on_grid(sig[:, FC * NT // 3:], 3))
            dve.wait_ge(up_scaled, 1)
            dve.tensor_tensor(qs[:, 5, 1:2], scale(3), scale(2), ALU.mult)
            dve.wait_ge(mx_ready, 4)
            for n in (2, 1):
                dve.wait_ge(up_on_grid, 3)
                link(dve.scalar_tensor_tensor(out=thirds(gate)[n], in0=thirds(sig)[n], scalar=MAGIC, in1=thirds(up)[n],
                                              op0=ALU.subtract, op1=ALU.mult))
            for n in (2, 1, 0):
                if n == 0:
                    dve.wait_ge(product_ready, 1)
                ins = part_maximum(n, thirds(gate)[n])
            link(ins)
            maximum(4, 3)
            link(scale_from(4, qs[:, 5, 1:2]))
            for t in range(TT):
                v = gate.rearrange("p (o t) -> p o t", o=FC)[:, :, t * P:min((t + 1) * P, NT)]
                link(on_grid(v, 4))
                integers(v).then_inc(o_ready, 1)
            for t in range(TT):
                n = rows_of(t)
                b = take(dve, ("dn", t))
                empty(dve.scalar_tensor_tensor(out=h[0:n, t, :], in0=b[0:n, 0:D], scalar=qs[0:n, 4, 0:1], in1=h[0:n, t, :],
                                               op0=ALU.mult, op1=ALU.add))

        @block.tensor
        def _(pe):
            at_fill = [0]

            def fill(key):
                n = FILL[key]
                assert n == at_fill[0], key
                at_fill[0] += 1
                if n >= 8:
                    emptied(pe, FILLS[n - 8][0])
                return banks[n % 8]

            def full(ins):
                ins.then_inc(bank_filled, 1)

            def keep_awake(b, n):
                for _ in range(n):
                    pe.matmul(b[:, 0:P], ones[:, :], ident[:, :], start=True, stop=True)

            def product(out_, pairs):
                for n, (a_, b_) in enumerate(pairs):
                    ins = pe.matmul(out_, a_, b_, start=(n == 0), stop=(n == len(pairs) - 1))
                return ins

            pe.wait_ge(consts_ready, N_CONSTS)
            one_hot = token_of.rearrange("p b t -> p (b t)")
            for t in range(TT):
                rows = P if t < TT - 1 else LAST
                b = fill(("ad", t))
                if t == 0:
                    keep_awake(b, 4)
                    pe.wait_ge(table_ready, 1)
                full(product(b[0:rows, 0:D + 1], [(one_hot[:, t * P:t * P + rows], table)]))
            pp = patches[0:96, :].rearrange("p (w k n) -> p w k n", w=NG, k=6)
            for g in range(2):
                for k in range(6):
                    b = fill(("xp", k, g))
                    if (k, g) == (0, 0):
                        keep_awake(b, 6)
                    if k == 0:
                        pe.wait_ge(patches_ready, g + 1)
                        if g:
                            pe.wait_ge(patches_ready_pool, 1)
                    for w in range(3):
                        ins = pe.transpose(b[:, 96 * w:96 * w + 96], pp[:, 3 * g + w, k, :], ident[0:96, 0:96])
                    full(ins)
            pe.wait_ge(patch_w_in, 16 * NC)
            for j in range(3):
                b = fill(("y", j))
                for k in range(6):
                    emptied(pe, ("xp", k, 1))
                for t in range(2 * j, min(2 * j + 2, TT)):
                    rows = P if t < TT - 1 else LAST
                    ins = product(b[0:rows, (t % 2) * D:(t % 2 + 1) * D], [(patT[:, k, t * P:t * P + rows], lin_w[:, k, :]) for k in range(6)])
                full(ins)
            pe.wait_ge(attn_w_in, 16 * N_ATTN_W)
            for n in ("q0", "o0", "q1", "k1", "v1", "o1"):
                b = fill(("wT", n))
                for k in range(KD):
                    for o in range(KD):
                        ins = pe.transpose(b[:, k * D + o * P:k * D + (o + 1) * P], raw[n][:, o, k * P:(k + 1) * P], ident[:, :])
                full(ins)
            b = fill(("wkvT",))
            for k in range(KD):
                ins = pe.transpose(b[:, 2 * HD * k:2 * HD * (k + 1)], raw_kv[0:2 * HD, k * P:(k + 1) * P], ident[0:2 * HD, 0:2 * HD])
            full(ins)
            ci = rep_i.rearrange("p h d -> p (h d)")
            cc_ = rep_c.rearrange("p h d -> p (h d)")
            mats = ((0, cc_), (1, cc_), (1, ci), (2, ci))
            pe.wait_ge(wl8_ready, 1)
            b = fill(("wl",))
            for m, (n, c_) in enumerate(mats):
                ins = product(b[:, m * P:(m + 1) * P], [(wl8[:, n, :, :].rearrange("p h d -> p (h d)"), c_)])
            full(ins)
            b = fill(("bl",))
            for m, (n, c_) in enumerate(mats):
                ins = product(b[:, m:m + 1], [(c_, blr[:, n:n + 1])])
            full(ins)

            def turn(n, ready, awake=0):
                for j in range(3):
                    b = fill(("xT", n, j))
                    if j == 0:
                        keep_awake(b, awake)
                    for t in range(2 * j, min(2 * j + 2, TT)):
                        pe.wait_ge(xn_ready, (ready - 1) * TT + t + 1)
                        for k in range(KD):
                            at_ = (t % 2) * D + k * P
                            ins = pe.transpose(b[:, at_:at_ + P], xn[:, t, k * P:(k + 1) * P], ident[:, :])
                    full(ins)

            def columns(key, w, cols_):
                b = fill(key)
                n = cols_.stop - cols_.start
                full(product(b[:, 0:n], [(w(k), xT[:, k, cols_]) for k in range(KD)]))

            def half_cols(c):
                return slice(c * CH, (c + 1) * CH)

            def values_turned(c):
                emptied(pe, ("v0", c))
                for j in range(2):
                    b = fill(("vb", c, j))
                    for n in range(4):
                        ins = pe.transpose(b[0:G3, n * P:(n + 1) * P],
                                           values3[:, c, 4 * j + n, :], ident[:, :])
                    full(ins)

            turn(0, 1, awake=6)
            emptied(pe, ("wkvT",))
            emptied(pe, ("xT", 0, 2))
            for c in range(2):
                columns(("k0", c), lambda k: wkT[:, k, :], half_cols(c))
                columns(("v0", c), lambda k: wvT[:, k, :], half_cols(c))
                for hf in range(KD):
                    columns(("q0", hf, c), lambda k: wT["q0"][:, k, hf * P:(hf + 1) * P], half_cols(c))
            for c in range(2):
                values_turned(c)

            def attention():
                for s in range(B // 2 + 2):
                    if s < B // 2:
                        c = s // (CB // 2)
                        for hf in range(KD):
                            pe.wait_ge(keys_spread, c + 1)
                            emptied(pe, ("q0", hf, c))
                            b = fill(("S", s, hf))
                            for j in range(2):
                                im_ = 2 * s + j - c * CB
                                ins = product(b[64 * j:64 * j + 64, 0:KW],
                                              [(qsT[:, hf, c, im_ * T:im_ * T + 64],
                                                kexp[c][:, im_, :, :].rearrange("p h k -> p (h k)"))])
                            full(ins)
                    if 0 <= s - 1 < B // 2:
                        for hf in range(KD):
                            pe.wait_ge(exp_done, KD * (s - 1) + hf + 1)
                            b = fill(("PT", s - 1, hf))
                            for g, at_ in enumerate(GROUP_AT):
                                ins = pe.transpose(b[0:G3, g * P:(g + 1) * P],
                                                   probs[:, (s - 1) % 3, hf, at_ * T:at_ * T + G3], ident[:, :])
                            full(ins)
                    if 0 <= s - 2 < B // 2:
                        q = s - 2
                        c = q // (CB // 2)
                        b = fill(("PV", q))
                        for hf in range(KD):
                            emptied(pe, ("PT", q, hf))
                            emptied(pe, ("vb", c, 1))
                            for j in range(2):
                                im_ = 2 * q + j - c * CB
                                for g, (h0, h1) in enumerate(((0, 3), (3, 6), (6, 8))):
                                    lo = (hf * NH + h0) * VW
                                    ins = product(b[64 * j:64 * j + 64, lo:lo + (h1 - h0) * VW],
                                                  [(probsT[:, q % 2, hf, g * P + 64 * j:g * P + 64 * j + 64],
                                                    vals[c][0:G3, im_, h0:h1, :].rearrange("p h v -> p (h v)"))])
                        full(ins)

            def project(n, w, js=range(3)):
                for j in js:
                    b = fill(("wo", n, j))
                    for t in range(2 * j, min(2 * j + 2, TT)):
                        rows = P if t < TT - 1 else LAST
                        ins = product(b[0:rows, (t % 2) * D:(t % 2 + 1) * D],
                                      [(attT[:, k, t * P:t * P + rows], w[:, k, :]) for k in range(KD)])
                    full(ins)

            attention()

            def weight_turned(n):
                w, j = n // 3, n % 3
                pe.wait_ge(fw_ready, w + 1)
                b = fill(("fw", n))
                for x in range(2):
                    for o in range(2):
                        if w < 2:
                            src = fraw[w][:, (2 * j + o) * D + x * P:(2 * j + o) * D + (x + 1) * P]
                        else:
                            src = fraw[w][:, o * FI + (2 * j + x) * P:o * FI + (2 * j + x + 1) * P]
                        ins = pe.transpose(b[:, x * D + o * P:x * D + (o + 1) * P], src, ident[:, :])
                full(ins)

            for j, ps in enumerate(HEADS_FOR_TILES):
                for p in ps:
                    pe.wait_ge(regrouped_in[j], 32)
                    b = fill(("AT", p))
                    for k in range(KD):
                        ins = pe.transpose(b[:, k * P:(k + 1) * P], regrouped[:, p, k * P:(k + 1) * P], ident[:, :])
                    full(ins)
                emptied(pe, ("AT", ps[-1]))
                project(0, wT["o0"], [j])
            for n in range(3):
                weight_turned(n)
            turn(1, 2, awake=6)
            for c in range(2):
                emptied(pe, ("xT", 1, 1 + c))
                b = fill(("lg", c))
                full(product(b[0:NE, 0:NP // 2], [(gate_w[:, k, :], xT[:, k, c * NP // 2:(c + 1) * NP // 2]) for k in range(KD)]))
            b = fill(("lgT",))
            for c in range(2):
                emptied(pe, ("lg", c))
            for t in range(TT):
                ins = pe.transpose(b[:, t * NE:(t + 1) * NE], logits[:, t * P:(t + 1) * P], ident[0:NE, 0:NE])
            full(ins)
            pe.wait_ge(moe_in, 16 * 8)

            def down(e):
                parts = [(e % 3, w_ed[:, e, :])] if e < NE else [(e % 3, w_sd[:, 0, :]), ((e + 1) % 3, w_sd[:, 1, :])]
                emptied(pe, ("u", e if e < NE else e + 1, 1))
                for j in range(3):
                    b = fill(("d", e, j))
                    for t in range(2 * j, min(2 * j + 2, TT)):
                        rows = P if t < TT - 1 else LAST
                        ins = product(b[0:rows, (t % 2) * D:(t % 2 + 1) * D],
                                      [(hid[:, s_, t * P:t * P + rows], w) for s_, w in parts])
                    full(ins)

            for e in range(NX + 1):
                if e < NX:
                    for c in range(2):
                        cols_ = slice(c * HP, (c + 1) * HP)
                        if e < NE:
                            columns(("g", e, c), lambda k: w_eg[:, k, e, :], cols_)
                            columns(("u", e, c), lambda k: w_eu[:, k, e, :], cols_)
                        else:
                            part_ = slice((e - NE) * P, (e - NE + 1) * P)
                            columns(("g", e, c), lambda k: w_sg[:, k, part_], cols_)
                            columns(("u", e, c), lambda k: w_su[:, k, part_], cols_)
                if 1 <= e <= NE or e == NX:
                    down(min(e - 1, NE))
            for n in range(6, 9):
                weight_turned(n)
            turn(2, 3, awake=8)
            emptied(pe, ("xT", 2, 2))
            us = range(2)
            xf = xT[:, :, 0:NT].rearrange("p k (b t) -> p k b t", t=T)

            def projection(w):
                for u in us:
                    b = fill((w + "1", u))
                    for f in range(KD):
                        ins = product(b[:, f * P:(f + 1) * P].rearrange("p (b t) -> p b t", t=TF),
                                      [(wT[w + "1"][:, k, f * P:(f + 1) * P], xf[:, k, u * CB:(u + 1) * CB, 0:TF])
                                       for k in range(KD)])
                    full(ins)

            def head_product(key, m, src):
                b = fill(key)
                full(product(b[:, 0:CF], [(wlT[:, m, :], src[:, key[-1], :])]))

            def variance(key):
                emptied(pe, ("nc", *key))
                b = fill(("nv", *key))
                full(product(b[:, 0:CF], [(mean_m.rearrange("p h d -> p (h d)"), sqr[:, NORMS[key] % NR, :])]))

            def values_by_key(a, u, js):
                pe.wait_ge(fvals_spread, 2 * (a - 1) + u + 1)
                for j in js:
                    b = fill(("fvb", a, u, j))
                    for n in range(4):
                        ins = pe.transpose(b[:, n * P:(n + 1) * P], fvals[:, u, 4 * j + n, :, :].rearrange("p h k -> p (h k)"),
                                           ident[:, :])
                    full(ins)

            projection("k")
            projection("q")
            for w, m, src in (("k", 1, k_cur), ("q", 0, q_cur)):
                for u in us:
                    emptied(pe, (w + "1", u))
                    head_product(("nc", w, 1, u), m, src)
            for w in ("k", "q"):
                for u in us:
                    variance((w, 1, u))
            projection("v")
            for u in us:
                emptied(pe, ("v1", u))
                head_product(("vr", 1, u), 3, v_cur)
            for u in us:
                head_product(("kr", 1, u), 2, k_cur)
            for a in (1, 2, 3):
                if a > 1:
                    for u in us:
                        emptied(pe, ("OT", a - 1, u))
                        head_product(("nc", "q", a, u), 0, q_cur)
                    values_by_key(a, 0, (0, 1))
                    for u in us:
                        variance(("q", a, u))
                    values_by_key(a, 0, (2, 3))
                for u in us:
                    pe.wait_ge(fkeys_spread, 2 * (a - 1) + u + 1)
                    if a == 1:
                        pe.wait_ge(fkeys_spread_dve, u + 1)
                    pe.wait_ge(normed, NORMS["q", a, u] + 1)
                    b = fill(("fS", a, u))
                    for im in range(CB):
                        g, n = im % 4, im // 4
                        ins = product(b[32 * g:32 * g + 32, n * P:(n + 1) * P],
                                      [(queries_n[:, u, 32 * m + TF * (1 - f):32 * m + TF * (1 - f) + 32],
                                        fkeys[:, u, m, :, :].rearrange("p h k -> p (h k)"))
                                       for f, m in ((0, im), (1, CB + im))])
                    full(ins)
                if a < 3:
                    for u in us:
                        emptied(pe, ("kr", a, u))
                        head_product(("nc", "k", a + 1, u), 1, k_cur)
                    if a < 2:
                        for u in us:
                            head_product(("kr", a + 1, u), 2, k_cur)
                    for u in us:
                        variance(("k", a + 1, u))
                else:
                    pe.wait_ge(df_ready, 1)
                    b = fill(("df",))
                    full(product(b[:, 0:1], [(ones[:, :], dfs[:, 0:1])]))
                if a == 1:
                    values_by_key(a, 0, range(4))
                values_by_key(a, 1, range(4))
                for u in us:
                    pe.wait_ge(fprobs_ready, 2 * (a - 1) + u + 1)
                    b = fill(("fPT", a, u))
                    for n in range(2):
                        ins = pe.transpose(b[:, n * P:(n + 1) * P], fprobs[:, u, n * P:(n + 1) * P], ident[:, :])
                    full(ins)
                if a < 3:
                    for u in us:
                        emptied(pe, ("vr", a, u))
                        head_product(("vr", a + 1, u), 3, v_cur)
                for u in us:
                    emptied(pe, ("fPT", a, u))
                    emptied(pe, ("fvb", a, u, 3))
                    b = fill(("O", a, u))
                    for im in range(CB):
                        g, n = im % 4, im // 4
                        ins = product(b[32 * g:32 * g + 32, n * P:(n + 1) * P],
                                      [(fprobsT[:, u, 32 * m + TF * (1 - f):32 * m + TF * (1 - f) + 32], fvalsT[:, u, m, :])
                                       for f, m in ((0, im), (1, CB + im))])
                    full(ins)
                for u in us:
                    emptied(pe, ("O", a, u))
                    b = fill(("OT", a, u))
                    for n in range(2):
                        ins = pe.transpose(b[:, n * P:(n + 1) * P], fheads[:, u, n * P:(n + 1) * P], ident[:, :])
                    full(ins)
            emptied(pe, ("OT", 3, 1))
            project(1, wT["o1"])
            for n in range(3, 6):
                weight_turned(n)

            def maximum_turned(n, awake=0):
                b = fill(("mxT", n))
                keep_awake(b, awake)
                pe.wait_ge(mx_ready, n + 1)
                full(pe.transpose(b[0:1, 0:P], mx[:, n:n + 1], ident[:, :]))

            def maximum_spread(n):
                b = fill(("mxB", n))
                emptied(pe, ("mxT", n))
                full(product(b[:, 0:1], [(ones[0:1, :], gmx[0:1, n:n + 1])]))

            def maximum(n, awake=0):
                maximum_turned(n, awake)
                maximum_spread(n)

            maximum(0, awake=8)
            turn(3, 5)
            for n, w in enumerate(("ga", "up")):
                for o in range(FC):
                    for c in range(2):
                        if (w, o) == ("ga", 0):
                            emptied(pe, ("xT", 3, 1 + c))
                        columns((w, o, c), lambda k: fT[n][:, k, o * P:(o + 1) * P], slice(c * HP, (c + 1) * HP))
                        if (w, o) == ("up", 0):
                            maximum_turned(1) if c == 0 else maximum_spread(1)
            for n in (2, 3, 4):
                maximum(n, awake=18 if n == 4 else 0)
            for t in range(TT):
                rows = P if t < TT - 1 else LAST
                b = fill(("dn", t))
                if t == 0:
                    keep_awake(b, 8)
                pe.wait_ge(o_ready, t + 1)
                full(product(b[0:rows, 0:D], [(gate[:, o * NT + t * P:o * NT + t * P + rows], fT[2][:, o, :]) for o in range(FC)]))


_INS = ["x", "L0_tok_ln1_w", "L0_tok_ln1_b", "L0_tok_lin_w", "L0_tok_lin_b", "L0_tok_ln2_w", "L0_tok_ln2_b",
        "L0_tok_pos_embedding", "L0_tok_cls_token", "L0_attn_Wq", "L0_attn_bq", "L0_attn_Wkv", "L0_attn_bkv",
        "L0_attn_Wo", "L0_attn_bo", "L0_ffn_gate_w", "L0_ffn_gate_bias", "L0_ffn_w_gate", "L0_ffn_w_up",
        "L0_ffn_w_down", "L0_ffn_sw_gate", "L0_ffn_sw_up", "L0_ffn_sw_down", "L1_attn_Wq", "L1_attn_bq",
        "L1_attn_Wk", "L1_attn_Wv", "L1_attn_bv", "L1_attn_Wo", "L1_attn_bo", "L1_attn_lna_w", "L1_attn_lnc_w",
        "L1_attn_lnd_w", "L1_attn_Wlq", "L1_attn_blq", "L1_attn_Wlk", "L1_attn_blk", "L1_attn_Wlv", "L1_attn_blv",
        "L1_attn_temp", "L1_attn_threshold", "L1_attn_factor", "L1_ffn_w_gate", "L1_ffn_w_up", "L1_ffn_w_down"]


def kernel(**inputs):
    import numpy as _np
    import concourse.bacc as _bacc
    from concourse import mybir as _mybir
    from concourse.bass_utils import run_bass_kernel_spmd as _run

    nc = _bacc.Bacc("TRN2", target_bir_lowering=False, num_devices=1)
    arrays, args = {}, {}
    for name in _INS:
        a = _np.ascontiguousarray(inputs[name])
        if a.ndim == 0:
            a = a.reshape(1)
        arrays[f"in_{name}"] = a
        args[name] = nc.dram_tensor(f"in_{name}", a.shape, _mybir.dt.from_np(a.dtype), kind="ExternalInput").ap()
    out = nc.dram_tensor("out_tokens", (B, T, D), F32, kind="ExternalOutput").ap()
    build(nc, args, out)
    r = _run(nc, [arrays], core_ids=[0])
    return r.results[0]["out_tokens"]
```
